# Optimizing a Trainium2 kernel written in Bass

```python
import numpy as np
import jax
import jax.numpy as jnp

def _softmax(x, axis=-1):
    return jax.nn.softmax(x, axis=axis)

def _gelu(x):
    return jax.nn.gelu(x, approximate=True)

def _silu(x):
    return jax.nn.silu(x)

def _sigmoid(x):
    return jax.nn.sigmoid(x)

def _layernorm(x, axis=-1, eps=1e-05):
    m = jnp.mean(x, axis=axis, keepdims=True)
    v = jnp.var(x, axis=axis, keepdims=True)
    return (x - m) / jnp.sqrt(v + eps)

def _scatter_add(tgt, idx, src, axis=0):
    return tgt.at[idx].add(src)

def _segment_sum(src, seg, n):
    return jax.ops.segment_sum(src, seg, n)
kernel_name = 'mk_gnn_preln_d4_gnn_r16_21765d'

def setup_inputs(seed: int=0):
    np.random.seed(seed)
    _w = jnp.asarray

    def _rec_inputs():
        import jax
        import jax.numpy as jnp
        _gk = jax.random.key(seed)
        x = -0.0003713 + 1 * jax.random.normal(jax.random.fold_in(_gk, 1), (3125, 128), jnp.float32)
        src = jax.random.randint(jax.random.fold_in(_gk, 2), (100000,), 0, 3125, jnp.int32)
        dst = jnp.minimum((3125 * jax.random.uniform(jax.random.fold_in(_gk, 3), (100000,)) ** 2.0).astype(jnp.int32), 49999)
        _o = jnp.argsort(dst, stable=True)
        src = src[_o]
        dst = dst[_o]
        edge_weight = jax.random.uniform(jax.random.fold_in(_gk, 13), (100000,), jnp.float32, 0.0, 1)
        edge_weight1 = -0.000152433 + 0.999798 * jax.random.normal(jax.random.fold_in(_gk, 14), (100000, 1), jnp.float32)
        return (x, src, dst, edge_weight, edge_weight1)
    x, src, dst, edge_weight, edge_weight1 = _rec_inputs()

    def _L0_gnn_setup():
        import jax, jax.numpy as jnp
        import numpy as np
        N = 6250
        E = 40000
        D = 128

        def _weighted_mean_agg(ft, w, src, dst, n_nodes):
            m = ft[src] * w[:, None]
            msum = jax.ops.segment_sum(m, dst, num_segments=n_nodes)
            wsum = jax.ops.segment_sum(w, dst, num_segments=n_nodes)
            safe = jnp.where(wsum > 0, wsum, 1.0)
            return jnp.where((wsum > 0)[:, None], msum / safe[:, None], 0.0)
        key = jax.random.key(seed)
        ks = jax.random.split(key, 10)
        s = 1.0 / np.sqrt(D)
        feat = jax.random.normal(ks[0], (N, D), jnp.float32)
        w = jax.random.uniform(ks[1], (E,), jnp.float32)
        src = jax.random.randint(ks[2], (E,), 0, N, dtype=jnp.int32)
        dst = jax.random.randint(ks[3], (E,), 0, N, dtype=jnp.int32)
        W1 = jax.random.uniform(ks[4], (D, D), jnp.float32, -s, s)
        W2 = jax.random.uniform(ks[5], (D, D), jnp.float32, -s, s)
        sg = 1.0 / np.sqrt(D)
        w_ih = jax.random.uniform(ks[6], (3 * D, 2 * D), jnp.float32, -sg, sg)
        w_hh = jax.random.uniform(ks[7], (3 * D, D), jnp.float32, -sg, sg)
        b_ih = jax.random.uniform(ks[8], (3 * D,), jnp.float32, -sg, sg)
        b_hh = jax.random.uniform(ks[9], (3 * D,), jnp.float32, -sg, sg)
        return {'feat': feat, 'w': w, 'src': src, 'dst': dst, 'W1': W1, 'W2': W2, 'w_ih': w_ih, 'w_hh': w_hh, 'b_ih': b_ih, 'b_hh': b_hh}
    _L0_gnn_all = _L0_gnn_setup()
    _L0_gnn_in = {k: v for k, v in _L0_gnn_all.items() if k in ('W1', 'W2', 'w_ih', 'w_hh', 'b_ih', 'b_hh')}
    del _L0_gnn_all

    def _L1_gnn_setup():
        import jax, jax.numpy as jnp
        import numpy as np
        N = 6250
        E = 200000
        D = 128
        K = 3
        key = jax.random.key(seed)
        k1, k2, k3, k4, k5 = jax.random.split(key, 5)
        x = jax.random.normal(k1, (N, D), dtype=jnp.float32)
        edge_row = jax.random.randint(k2, (E,), 0, N, dtype=jnp.int32)
        edge_col = jax.random.randint(k3, (E,), 0, N, dtype=jnp.int32)
        edge_val = jax.random.uniform(k4, (E,), dtype=jnp.float32)
        alpha_logits = jax.random.normal(k5, (K + 1,), dtype=jnp.float32)
        return {'x': x, 'edge_row': edge_row, 'edge_col': edge_col, 'edge_val': edge_val, 'alpha_logits': alpha_logits}
    _L1_gnn_all = _L1_gnn_setup()
    _L1_gnn_in = {k: v for k, v in _L1_gnn_all.items() if k in ('alpha_logits',)}
    del _L1_gnn_all

    def _L2_gnn_setup():
        import jax, jax.numpy as jnp
        import numpy as np
        H = 2
        C = 128
        K_ORDER = 4
        BETA = 0.5

        def _gcn_conv(x, row, col, deg_inv, n):
            msg = x[row]
            agg = jax.ops.segment_sum(msg, col, num_segments=n)
            return agg * deg_inv[:, None, None]

        def _attn_conv(qs, ks, vs):
            n = qs.shape[0]
            kvs = jnp.einsum('lhm,lhd->hmd', ks, vs)
            qkvs = jnp.einsum('nhm,hmd->nhd', qs, kvs)
            vs_sum = vs.sum(axis=0)
            num = qkvs + vs_sum[None, :, :]
            ks_sum = ks.sum(axis=0)
            qks_sum = jnp.einsum('nhm,hm->nh', qs, ks_sum)[:, :, None]
            den = qks_sum + jnp.asarray(n, qs.dtype)
            return num / den
        key = jax.random.key(seed)
        ks = jax.random.split(key, 8)
        N, E = (6250, 100000)
        x = jax.random.normal(ks[0], (N, C), jnp.float32)
        edge_index = jax.random.randint(ks[1], (2, E), 0, N, jnp.int64)
        s_in = 1.0 / np.sqrt(C)
        s_out = 1.0 / np.sqrt(H * C * (K_ORDER + 1))
        Wq_w = jax.random.normal(ks[2], (C, H * C), jnp.float32) * s_in
        Wq_b = jax.random.normal(ks[3], (H * C,), jnp.float32) * s_in
        Wk_w = jax.random.normal(ks[4], (C, H * C), jnp.float32) * s_in
        Wk_b = jax.random.normal(ks[5], (H * C,), jnp.float32) * s_in
        Wo_w = jax.random.normal(ks[6], (H * C * (K_ORDER + 1), C), jnp.float32) * s_out
        Wo_b = jax.random.normal(ks[7], (C,), jnp.float32) * s_out
        return {'x': x, 'edge_index': edge_index, 'Wq_w': Wq_w, 'Wq_b': Wq_b, 'Wk_w': Wk_w, 'Wk_b': Wk_b, 'Wo_w': Wo_w, 'Wo_b': Wo_b}
    _L2_gnn_all = _L2_gnn_setup()
    _L2_gnn_in = {k: v for k, v in _L2_gnn_all.items() if k in ('Wq_w', 'Wq_b', 'Wk_w', 'Wk_b', 'Wo_w', 'Wo_b')}
    del _L2_gnn_all

    def _L3_gnn_setup():
        import jax, jax.numpy as jnp
        import numpy as np
        N_NODES = 625
        N_EDGES = 40000
        HID = 128
        key = jax.random.key(seed)
        ks = jax.random.split(key, 8)
        h = jax.random.normal(ks[0], (N_NODES, HID), dtype=jnp.float32)
        edge_index = jax.random.randint(ks[1], (2, N_EDGES), 0, N_NODES, dtype=jnp.int64)
        edge_attr = jax.random.normal(ks[2], (N_EDGES, 1), dtype=jnp.float32)
        s1 = 1.0 / np.sqrt(2 * HID + 1)
        s2 = 1.0 / np.sqrt(HID)
        s3 = 1.0 / np.sqrt(2 * HID)
        return {'h': h, 'edge_index': edge_index, 'edge_attr': edge_attr, 'msg_w1': jax.random.normal(ks[3], (2 * HID + 1, HID), dtype=jnp.float32) * s1, 'msg_b1': jnp.zeros((HID,), dtype=jnp.float32), 'msg_w2': jax.random.normal(ks[4], (HID, HID), dtype=jnp.float32) * s2, 'msg_b2': jnp.zeros((HID,), dtype=jnp.float32), 'upd_w1': jax.random.normal(ks[5], (2 * HID, HID), dtype=jnp.float32) * s3, 'upd_b1': jnp.zeros((HID,), dtype=jnp.float32), 'upd_w2': jax.random.normal(ks[6], (HID, HID), dtype=jnp.float32) * s2, 'upd_b2': jnp.zeros((HID,), dtype=jnp.float32)}
    _L3_gnn_all = _L3_gnn_setup()
    _L3_gnn_in = {k: v for k, v in _L3_gnn_all.items() if k in ('msg_w1', 'msg_b1', 'msg_w2', 'msg_b2', 'upd_w1', 'upd_b1', 'upd_w2', 'upd_b2')}
    del _L3_gnn_all
    return {'x': x, 'src': src, 'dst': dst, 'edge_weight': edge_weight, 'edge_weight1': edge_weight1, 'L0_gnn_W1': _L0_gnn_in['W1'], 'L0_gnn_W2': _L0_gnn_in['W2'], 'L0_gnn_w_ih': _L0_gnn_in['w_ih'], 'L0_gnn_w_hh': _L0_gnn_in['w_hh'], 'L0_gnn_b_ih': _L0_gnn_in['b_ih'], 'L0_gnn_b_hh': _L0_gnn_in['b_hh'], 'L1_gnn_alpha_logits': _L1_gnn_in['alpha_logits'], 'L2_gnn_Wq_w': _L2_gnn_in['Wq_w'], 'L2_gnn_Wq_b': _L2_gnn_in['Wq_b'], 'L2_gnn_Wk_w': _L2_gnn_in['Wk_w'], 'L2_gnn_Wk_b': _L2_gnn_in['Wk_b'], 'L2_gnn_Wo_w': _L2_gnn_in['Wo_w'], 'L2_gnn_Wo_b': _L2_gnn_in['Wo_b'], 'L3_gnn_msg_w1': _L3_gnn_in['msg_w1'], 'L3_gnn_msg_b1': _L3_gnn_in['msg_b1'], 'L3_gnn_msg_w2': _L3_gnn_in['msg_w2'], 'L3_gnn_msg_b2': _L3_gnn_in['msg_b2'], 'L3_gnn_upd_w1': _L3_gnn_in['upd_w1'], 'L3_gnn_upd_b1': _L3_gnn_in['upd_b1'], 'L3_gnn_upd_w2': _L3_gnn_in['upd_w2'], 'L3_gnn_upd_b2': _L3_gnn_in['upd_b2']}

def reference(x, src, dst, edge_weight, edge_weight1, L0_gnn_W1, L0_gnn_W2, L0_gnn_w_ih, L0_gnn_w_hh, L0_gnn_b_ih, L0_gnn_b_hh, L1_gnn_alpha_logits, L2_gnn_Wq_w, L2_gnn_Wq_b, L2_gnn_Wk_w, L2_gnn_Wk_b, L2_gnn_Wo_w, L2_gnn_Wo_b, L3_gnn_msg_w1, L3_gnn_msg_b1, L3_gnn_msg_w2, L3_gnn_msg_b2, L3_gnn_upd_w1, L3_gnn_upd_b1, L3_gnn_upd_w2, L3_gnn_upd_b2):
    import jax
    import jax.numpy as jnp

    def _L0_gnn_ref(feat, w, src, dst, W1, W2, w_ih, w_hh, b_ih, b_hh):
        import jax, jax.numpy as jnp
        import numpy as np
        N = 6250
        E = 40000
        D = 128

        def _weighted_mean_agg(ft, w, src, dst, n_nodes):
            m = ft[src] * w[:, None]
            msum = jax.ops.segment_sum(m, dst, num_segments=n_nodes)
            wsum = jax.ops.segment_sum(w, dst, num_segments=n_nodes)
            safe = jnp.where(wsum > 0, wsum, 1.0)
            return jnp.where((wsum > 0)[:, None], msum / safe[:, None], 0.0)
        n = feat.shape[0]
        neigh1 = _weighted_mean_agg(feat, w, src, dst, n)
        neigh2 = _weighted_mean_agg(feat, w, dst, src, n)
        hn = jnp.concatenate([neigh1 @ W1.T, neigh2 @ W2.T], axis=1)
        gi = hn @ w_ih.T + b_ih
        gh = feat @ w_hh.T + b_hh
        i_r, i_z, i_n = jnp.split(gi, 3, axis=1)
        h_r, h_z, h_n = jnp.split(gh, 3, axis=1)
        r = jax.nn.sigmoid(i_r + h_r)
        z = jax.nn.sigmoid(i_z + h_z)
        nn_ = jnp.tanh(i_n + r * h_n)
        return nn_ + z * (feat - nn_)

    def _L1_gnn_ref(x, edge_row, edge_col, edge_val, alpha_logits):
        import jax, jax.numpy as jnp
        import numpy as np
        N = 6250
        E = 200000
        D = 128
        K = 3
        n = x.shape[0]
        alpha = jax.nn.softmax(alpha_logits)

        def spmm(X):
            return jax.ops.segment_sum(edge_val[:, None] * X[edge_col], edge_row, num_segments=n)
        Yk = x
        Y = alpha[0] * Yk
        for k in range(1, alpha.shape[0]):
            Yk = spmm(Yk)
            Y = Y + alpha[k] * Yk
        return Y

    def _L2_gnn_ref(x, edge_index, Wq_w, Wq_b, Wk_w, Wk_b, Wo_w, Wo_b):
        import jax, jax.numpy as jnp
        import numpy as np
        H = 2
        C = 128
        K_ORDER = 4
        BETA = 0.5

        def _gcn_conv(x, row, col, deg_inv, n):
            msg = x[row]
            agg = jax.ops.segment_sum(msg, col, num_segments=n)
            return agg * deg_inv[:, None, None]

        def _attn_conv(qs, ks, vs):
            n = qs.shape[0]
            kvs = jnp.einsum('lhm,lhd->hmd', ks, vs)
            qkvs = jnp.einsum('nhm,hmd->nhd', qs, kvs)
            vs_sum = vs.sum(axis=0)
            num = qkvs + vs_sum[None, :, :]
            ks_sum = ks.sum(axis=0)
            qks_sum = jnp.einsum('nhm,hm->nh', qs, ks_sum)[:, :, None]
            den = qks_sum + jnp.asarray(n, qs.dtype)
            return num / den
        n = x.shape[0]
        row, col = (edge_index[0], edge_index[1])
        deg = jax.ops.segment_sum(jnp.ones(row.shape[0], x.dtype), col, num_segments=n)
        deg_inv = jnp.where(deg > 0, 1.0 / deg, 0.0)
        query = (x @ Wq_w + Wq_b).reshape(n, H, C)
        key = (x @ Wk_w + Wk_b).reshape(n, H, C)
        qs = query / jnp.linalg.norm(query, axis=2, keepdims=True)
        ks = key / jnp.linalg.norm(key, axis=2, keepdims=True)
        x0 = jnp.broadcast_to(x[:, None, :], (n, H, C))
        terms = [x0]
        for _ in range(K_ORDER):
            prev = terms[-1]
            gcn_i = _gcn_conv(prev, row, col, deg_inv, n)
            attn_i = _attn_conv(qs, ks, prev)
            terms.append(BETA * gcn_i + attn_i)
        xcat = jnp.concatenate(terms, axis=-1)
        xcat = xcat.reshape(n, H * C * (K_ORDER + 1))
        return (xcat @ Wo_w + Wo_b) / H

    def _L3_gnn_ref(h, edge_index, edge_attr, msg_w1, msg_b1, msg_w2, msg_b2, upd_w1, upd_b1, upd_w2, upd_b2):
        import jax, jax.numpy as jnp
        import numpy as np
        N_NODES = 625
        N_EDGES = 40000
        HID = 128
        src, dst = (edge_index[0], edge_index[1])
        m_in = jnp.concatenate([h[src], h[dst], edge_attr], axis=1)
        msg = jax.nn.relu(m_in @ msg_w1 + msg_b1) @ msg_w2 + msg_b2
        agg = jax.ops.segment_sum(msg, dst, num_segments=h.shape[0])
        upd_in = jnp.concatenate([h, agg], axis=1)
        upd = jax.nn.relu(upd_in @ upd_w1 + upd_b1) @ upd_w2 + upd_b2
        return h + upd
    edge_index = jnp.stack([src, dst])
    h = jnp.maximum(_layernorm(x, axis=-1), 0.0)
    x = x + _L0_gnn_ref(h, edge_weight, src, dst, L0_gnn_W1, L0_gnn_W2, L0_gnn_w_ih, L0_gnn_w_hh, L0_gnn_b_ih, L0_gnn_b_hh)
    h = jnp.maximum(_layernorm(x, axis=-1), 0.0)
    x = x + _L1_gnn_ref(h, src, dst, edge_weight, L1_gnn_alpha_logits)
    h = jnp.maximum(_layernorm(x, axis=-1), 0.0)
    x = x + _L2_gnn_ref(h, edge_index, L2_gnn_Wq_w, L2_gnn_Wq_b, L2_gnn_Wk_w, L2_gnn_Wk_b, L2_gnn_Wo_w, L2_gnn_Wo_b)
    h = jnp.maximum(_layernorm(x, axis=-1), 0.0)
    x = x + _L3_gnn_ref(h, edge_index, edge_weight1, L3_gnn_msg_w1, L3_gnn_msg_b1, L3_gnn_msg_w2, L3_gnn_msg_b2, L3_gnn_upd_w1, L3_gnn_upd_b1, L3_gnn_upd_w2, L3_gnn_upd_b2)
    return x

_drawn_inputs = setup_inputs


def setup_inputs(seed=0):
    import zlib

    import numpy as np

    out = dict(_drawn_inputs(seed))
    spreads = {'L3_gnn_msg_b1': (0.0, 2.0),
     'L3_gnn_msg_b2': (0.0, 0.8),
     'L3_gnn_upd_b1': (0.0, 2.0),
     'L3_gnn_upd_b2': (0.0, 2.0)}
    factors = {'edge_weight1': 64.0,
     'L0_gnn_b_hh': 3.755,
     'L2_gnn_Wq_w': 64.0,
     'L2_gnn_Wq_b': 64.0,
     'L2_gnn_Wk_w': 64.0,
     'L2_gnn_Wk_b': 64.0,
     'L2_gnn_Wo_w': 25.003,
     'L2_gnn_Wo_b': 64.0,
     'L3_gnn_msg_w1': 2.741}
    for name, (base, spread) in spreads.items():
        noise = np.random.default_rng([zlib.crc32(name.encode()), seed]).standard_normal(out[name].shape)
        drawn = base * np.exp(spread * noise) if base else spread * noise
        out[name] = jnp.asarray(drawn.astype(out[name].dtype))
    for name, factor in factors.items():
        out[name] = (out[name] * factor).astype(out[name].dtype)
    return out
```

```python
import concourse.bass as bass
from concourse import mybir
from contextlib import ExitStack

F32 = mybir.dt.float32
F16 = mybir.dt.float16
BF16 = mybir.dt.bfloat16
I32 = mybir.dt.int32
ALU = mybir.AluOpType
ACT = mybir.ActivationFunctionType
AX = mybir.AxisListType

N = 3125
E = 100000
D = 128
B = 125
NB = N // B
WIN = 25
WPB = B // WIN
NW = N // WIN
TE = 128
CT = 7
NT = CT * 128
PAD = 4000
FAR = 100000.0
KW = WIN * NB
KEVEN = KW + 1
HEADS = 2
ORDER = 4
EPS = 1e-5
CHUNKS = [(c, min(512, N - c)) for c in range(0, N, 512)]
GROUPS = [(g, min(4, NB - g)) for g in range(0, NB, 4)]


class Counter:

    def __init__(self, eng):
        self.eng = eng
        self.reg = eng.alloc_register()
        eng.reg_mov(self.reg, 0)

    def next(self):
        self.eng.reg_add(self.reg, self.reg, 1)
        return self.eng.snap(self.reg)


class Chain:

    def __init__(self, eng, sem):
        self.eng, self.sem, self.n = eng, sem, 0

    def __call__(self, ins):
        self.n += 1
        ins.then_inc(self.sem, 1)
        self.eng.wait_ge(self.sem, self.n)


class Phase:

    used = []

    def __init__(self, nc, name):
        self.nc, self.name, self.ctx, self.sems = nc, name, ExitStack(), []

    def __enter__(self):
        self.ctx.__enter__()
        return self

    def __exit__(self, *a):
        done = self.ctx.__exit__(*a)
        self.used.extend(self.sems)
        if len(self.used) > 80:
            self.nc.clear_and_free_semaphores(list(self.used))
            self.nc.all_engine_barrier()
            self.used.clear()
        return done

    def sb(self, name, shape, dt=F32):
        return self.ctx.enter_context(self.nc.sbuf_tensor(f"{self.name}_{name}", shape, dt))

    def ps(self, name="ps"):
        return self.ctx.enter_context(self.nc.psum_tensor(f"{self.name}_{name}", [128, 8, 512], F32))

    def sem(self, name):
        sem = self.nc.alloc_semaphore(f"{self.name}_{name}")
        self.sems.append(sem)
        return sem


def bc(ap, n):
    return ap.unsqueeze(2).to_broadcast([ap.shape[0], ap.shape[1], n])


def tile_range(eng, g, at):
    lo = eng.value_load(g.bounds[0:1, bass.ds(at, 1)], min_val=0, max_val=E // TE)
    hi = eng.value_load(g.bounds[0:1, bass.ds(at + 128, 1)], min_val=0, max_val=E // TE + 1)
    return lo, hi


def setup_phase(nc, g, io):
    with Phase(nc, "setup") as ph:
        raw = [ph.sb(f"raw{i}", [128, CT, 128], dt) for i, dt in enumerate((I32, I32, F32, F32))]
        dst_q = ph.sb("dst_q", [128, CT, 128])
        src_q = ph.sb("src_q", [128, CT, 128])
        src_t = ph.sb("src_t", [128, NT])
        w_t = ph.sb("w_t", [128, NT])
        t1 = ph.sb("t1", [128, NT])
        ti = ph.sb("ti", [128, NT], I32)
        tb = ph.sb("tb", [128, NT], BF16)
        mx = ph.sb("mx", [128, 2, CT])
        diag = ph.sb("diag", [128, 2, CT, 128])
        ones = ph.sb("ones", [128, 128])
        mxb = ph.sb("mxb", [128, 2, NT])
        pid = ph.sb("pid", [128, NT])
        thr = ph.sb("thr", [128, 4])
        pt = ph.sb("pt", [128, NT])
        lim = ph.sb("lim", [128, 4])
        ps = ph.ps()
        s_pad = ph.sem("pad")
        s_in = ph.sem("in")
        s_x = ph.sem("x")
        s_const = ph.sem("const")
        s_f = ph.sem("f")
        s_tr = ph.sem("tr")
        s_diag = ph.sem("diag")
        s_copied = ph.sem("copied")
        s_bc = ph.sem("bc")
        s_lim = ph.sem("lim")
        s_row = ph.sem("row")
        s_d = ph.sem("d")
        block = ph.ctx.enter_context(nc.Block())
        full = E // TE
        rows, tail = full - 128 * (CT - 1), E - full * TE

        @block.sync
        def _(sp):
            sp.wait_ge(s_pad, 4)
            for r, a in zip(raw, (io["dst"], io["src"], io["w"], io["ea"])):
                sp.dma_start(r[:, 0:CT - 1, :],
                             a[0:128 * (CT - 1) * TE].rearrange("(c q p) -> q c p", q=128, p=TE)).then_inc(s_in, 16)
                sp.dma_start(r[0:rows, CT - 1, :],
                             a[128 * (CT - 1) * TE:full * TE].rearrange("(q p) -> q p", p=TE)).then_inc(s_in, 16)
                sp.dma_start(r[rows:rows + 1, CT - 1, 0:tail],
                             a[full * TE:E].rearrange("(q p) -> q p", q=1)).then_inc(s_in, 16)
            sp.dma_start(g.x[:], io["x"].rearrange("(b p) d -> p b d", p=B)).then_inc(s_x, 16)
            sp.wait_ge(s_x, 16)

        @block.gpsimd
        def _(pool):
            pool.memset(raw[0][:], PAD).then_inc(s_pad, 1)
            for r in raw[1:]:
                pool.memset(r[:], 0).then_inc(s_pad, 1)
            pool.memset(g.ident[:], 0.0).then_inc(s_const, 1)
            pool.wait_ge(s_const, 1)
            pool.affine_select(out=g.ident[:], in_=g.ident[:], compare_op=ALU.not_equal, fill=1.0, base=0,
                               pattern=[[-1, 128]], channel_multiplier=1).then_inc(s_const, 1)
            pool.iota(g.key_id[:], [[1, KEVEN]], base=0, channel_multiplier=0,
                      allow_small_or_imprecise_dtypes=True).then_inc(s_const, 1)
            pool.iota(pid[:], [[1, NT]], base=0, channel_multiplier=0,
                      allow_small_or_imprecise_dtypes=True).then_inc(s_const, 1)
            for i, (base, step) in enumerate(((0, WIN), (WIN - 1, WIN), (0, B), (B - 1, B))):
                pool.iota(thr[:, i:i + 1], [[0, 1]], base=base, channel_multiplier=step,
                          allow_small_or_imprecise_dtypes=True).then_inc(s_const, 1)
            pool.memset(ones[:], 1.0).then_inc(s_const, 1)
            pool.memset(g.h[:, :, D:D + 1], 1.0).then_inc(s_const, 1)

        @block.tensor
        def _(pe):
            pe.wait_ge(s_const, 10)
            pe.wait_ge(s_in, 192)
            pe.wait_ge(s_f, 2)
            for i, a in enumerate((dst_q, src_q, raw[2], raw[3])):
                for c in range(CT):
                    last = pe.transpose(ps[:, 2 * i + c // 4, (c % 4) * 128:(c % 4) * 128 + 128], a[:, c, :], g.ident[:])
                last.then_inc(s_tr, 1)
            pe.wait_ge(s_diag, 2)
            pe.wait_ge(s_copied, 1)
            for i in range(2):
                for c in range(CT):
                    last = pe.matmul(ps[:, 2 * i + c // 4, (c % 4) * 128:(c % 4) * 128 + 128], ones[:],
                                     diag[:, i, c, :], start=True, stop=True)
            last.then_inc(s_bc, 1)
            pe.wait_ge(s_lim, 1)
            for i in range(4):
                last = pe.transpose(ps[0:1, 4, i * 128:(i + 1) * 128], lim[:, i:i + 1], g.ident[:])
            last.then_inc(s_row, 1)

        @block.vector
        def _(v):
            do = Chain(v, s_d)
            v.wait_ge(s_in, 192)
            v.tensor_copy(dst_q[:], raw[0][:]).then_inc(s_f, 1)
            v.tensor_copy(src_q[:], raw[1][:]).then_inc(s_f, 1)
            v.wait_ge(s_f, 2)
            v.tensor_reduce(mx[:, 0, :], dst_q[:], AX.X, ALU.max)
            do(v.tensor_reduce(mx[:, 1, :], dst_q[:], AX.X, ALU.min))
            v.wait_ge(s_const, 10)
            for i in range(2):
                for c in range(CT):
                    last = v.tensor_scalar(diag[:, i, c, :], g.ident[:], mx[:, i, c:c + 1], None, ALU.mult)
                last.then_inc(s_diag, 1)
            v.wait_ge(s_tr, 4)
            for i, a in enumerate((g.dst, src_t, w_t, g.ea)):
                v.tensor_copy(a[:, 0:512], ps[:, 2 * i, :])
                last = v.tensor_copy(a[:, 512:NT], ps[:, 2 * i + 1, 0:NT - 512])
            last.then_inc(s_copied, 1)
            v.wait_ge(s_copied, 1)
            blk, lane = g.key, g.lane
            do(v.tensor_scalar(ti[:], src_t[:], 1.0 / B, None, ALU.mult))
            do(v.tensor_copy(blk[:], ti[:]))
            do(v.scalar_tensor_tensor(lane[:], blk[:], -float(B), src_t[:], ALU.mult, ALU.add))
            do(v.tensor_scalar(t1[:], lane[:], 0.0, None, ALU.is_lt))
            do(v.tensor_tensor(blk[:], blk[:], t1[:], ALU.subtract))
            do(v.scalar_tensor_tensor(lane[:], t1[:], float(B), lane[:], ALU.mult, ALU.add))
            do(v.tensor_scalar(t1[:], lane[:], float(B), None, ALU.is_ge))
            do(v.tensor_tensor(blk[:], blk[:], t1[:], ALU.add))
            do(v.scalar_tensor_tensor(lane[:], t1[:], -float(B), lane[:], ALU.mult, ALU.add))
            do(v.scalar_tensor_tensor(g.key[:], g.dst[:], float(NB), blk[:], ALU.mult, ALU.add))
            do(v.tensor_copy(g.src_idx[:], src_t[:]))
            for i in range(3):
                do(v.tensor_copy(tb[:], w_t[:]))
                do(v.tensor_copy(g.wpart[i][:], tb[:]))
                if i < 2:
                    do(v.tensor_tensor(w_t[:], w_t[:], g.wpart[i][:], ALU.subtract))
            v.wait_ge(s_bc, 1)
            for i in range(2):
                v.tensor_copy(mxb[:, i, 0:512], ps[:, 2 * i, :])
                last = v.tensor_copy(mxb[:, i, 512:NT], ps[:, 2 * i + 1, 0:NT - 512])
            do(last)
            for k in range(2):
                do(v.tensor_scalar(pt[:], mxb[:, 0, :], thr[:, 2 * k:2 * k + 1], FAR, ALU.is_lt, ALU.mult))
                do(v.tensor_tensor(pt[:], pt[:], pid[:], ALU.add))
                do(v.tensor_reduce(lim[:, 2 * k:2 * k + 1], pt[:], AX.X, ALU.min))
                do(v.tensor_scalar(pt[:], mxb[:, 1, :], thr[:, 2 * k + 1:2 * k + 2], -FAR, ALU.is_gt, ALU.mult))
                do(v.tensor_tensor(pt[:], pt[:], pid[:], ALU.add))
                do(v.tensor_reduce(lim[:, 2 * k + 1:2 * k + 2], pt[:], AX.X, ALU.max))
                do(v.tensor_scalar(lim[:, 2 * k + 1:2 * k + 2], lim[:, 2 * k + 1:2 * k + 2], 1.0, 0.0,
                                   ALU.add, ALU.max))
            v.memset(t1[:, 0:1], 0.0).then_inc(s_lim, 1)
            v.wait_ge(s_row, 1)
            v.tensor_copy(g.bounds[:], ps[0:1, 4, :])


def norm_phase(nc, g, name):
    with Phase(nc, name) as ph:
        xc = ph.sb("xc", [B, NB, D])
        sq = ph.sb("sq", [B, NB, D])
        m = ph.sb("m", [B, NB])
        r = ph.sb("r", [B, NB])
        s_v = ph.sem("v")
        s_sd = ph.sem("sd")
        s_h = ph.sem("h")
        s_d = ph.sem("d")
        block = ph.ctx.enter_context(nc.Block())

        @block.vector
        def _(v):
            do = Chain(v, s_d)
            do(v.tensor_reduce(m[:], g.x[:], AX.X, ALU.add))
            do(v.tensor_scalar(m[:], m[:], 1.0 / D, None, ALU.mult))
            do(v.tensor_tensor(xc[:], g.x[:], bc(m[:], D), ALU.subtract))
            do(v.tensor_tensor(sq[:], xc[:], xc[:], ALU.mult))
            do(v.tensor_reduce(r[:], sq[:], AX.X, ALU.add))
            v.tensor_scalar(r[:], r[:], 1.0 / D, EPS, ALU.mult, ALU.add).then_inc(s_v, 1)
            v.wait_ge(s_sd, 1)
            do(v.reciprocal(m[:], r[:]))
            v.tensor_tensor(sq[:], xc[:], bc(m[:], D), ALU.mult).then_inc(s_h, 1)

        @block.scalar
        def _(a):
            a.wait_ge(s_v, 1)
            a.activation(r[:], r[:], ACT.Sqrt).then_inc(s_sd, 1)
            a.wait_ge(s_h, 1)
            a.activation(g.h[:, :, 0:D], sq[:], ACT.Relu)


def build_phase(nc, g, dr):
    with Phase(nc, "build") as ph:
        left = [ph.sb(f"left{s}", [128, 4, 128], BF16) for s in range(2)]
        right = [ph.sb(f"right{s}", [128, KEVEN], BF16) for s in range(2)]
        stage = [ph.sb(f"stage{j}", [B, 2, WIN, NB]) for j in range(WPB)]
        adj = ph.sb("adj", [B, NB, B])
        cnt = [ph.sb(f"cnt{i}", [B, NB, B], BF16) for i in range(2)]
        adj_t = ph.sb("adj_t", [B, N])
        rowsum = ph.sb("rowsum", [B, NB])
        ps = ph.ps()
        s_lane = [ph.sem(f"lane{s}") for s in range(2)]
        s_ready = [ph.sem(f"ready{s}") for s in range(2)]
        s_scaled = [ph.sem(f"scaled{s}") for s in range(2)]
        s_free = [ph.sem(f"free{s}") for s in range(2)]
        s_key = ph.sem("key")
        s_acc = ph.sem("acc")
        s_staged = ph.sem("staged")
        s_unstaged = ph.sem("unstaged")
        s_pool = ph.sem("pool")
        s_adj = ph.sem("adj")
        s_tr = ph.sem("tr")
        s_trc = ph.sem("trc")
        s_n1 = ph.sem("n1")
        s_n1c = ph.sem("n1c")
        s_sum = ph.sem("sum")
        s_sumadd = ph.sem("sumadd")
        s_adjout = ph.sem("adjout")
        s_cntout = ph.sem("cntout")
        s_tick = ph.sem("tick")
        block = ph.ctx.enter_context(nc.Block())
        NG = len(GROUPS)
        COUNT = 3
        PIECES = [[(0, 0, 500), (1, 0, KW - 500)], [(1, KW - 500, 500), (2, 0, 2 * KW - 1000)]]

        @block.vector
        def _(v):
            rounds = Counter(v)

            def factors(t, n):
                for s in range(2):
                    at = bass.ds(t + s, 1)
                    v.wait_ge(s_free[s], n)
                    v.tensor_scalar(left[s][:, COUNT, :], g.key_id[:, 0:128], g.lane[:, at], None,
                                    ALU.is_equal).then_inc(s_lane[s], 1)
                    v.tensor_scalar(left[s][:, 0, :], g.key_id[:, 0:128], g.lane[:, at], g.wpart[0][:, at],
                                    ALU.is_equal, ALU.mult)
                    v.tensor_scalar(right[s][:], g.key_id[:], g.key[:, at], None, ALU.is_equal).then_inc(s_ready[s], 1)

            def window(w, first):
                lo, hi = tile_range(v, g, w)
                if not first:
                    so_far = v.snap(rounds.reg)
                    for s in range(2):
                        v.wait_ge(s_ready[s], so_far)
                    v.tensor_scalar(g.key[:], g.key[:], -float(KW), None, ALU.add).then_inc(s_key, 1)
                    v.wait_ge(s_key, v.snap(w))
                factors(lo, rounds.next())
                with v.Fori(lo + 2, hi, 2) as t:
                    factors(t, rounds.next())

            def row_sums(d):
                v.wait_ge(s_adj, d + 1)
                v.tensor_reduce(rowsum[:], adj[:], AX.X, ALU.add).then_inc(s_sum, 1)
                v.wait_ge(s_sum, d + 1)
                v.tensor_tensor(g.wsum_src[:], g.wsum_src[:], rowsum[:], ALU.add).then_inc(s_sumadd, 1)

            v.memset(g.wsum_src[:], 0.0).then_inc(s_sumadd, 1)
            v.wait_ge(s_sumadd, 1)
            for j in range(WPB):
                window(j, j == 0)
            with v.Fori(1, NB) as d:
                window(d * WPB, False)
                row_sums(d - 1)
                v.wait_ge(s_sumadd, d + 1)
                for j in range(1, WPB):
                    window(d * WPB + j, False)
            row_sums(NB - 1)

        @block.tensor
        def _(pe):
            rounds = Counter(pe)
            for s in range(2):
                pe.sem_inc(s_free[s], 1)

            def products(bank, n, start):
                for s in range(2):
                    pe.wait_ge(s_ready[s], n)
                    pe.wait_ge(s_scaled[s], n)
                    for k in (0, COUNT, 1, 2):
                        col = 0
                        for off, c0, c1 in PIECES[k == COUNT]:
                            opens = start and s == 0 and ((k == 0) or (off == 2))
                            last = pe.matmul(ps[0:B, bank + off, c0:c1], left[s][:, k, 0:B],
                                             right[s][:, col:col + c1 - c0], start=opens, stop=False,
                                             skip_group_check=True)
                            col += c1 - c0
                    last.then_inc(s_free[s], 1)

            def window(w, j, reuse):
                lo, hi = tile_range(pe, g, w)
                if reuse is not None:
                    pe.wait_ge(s_staged, pe.snap(reuse))
                bank = 3 * (j % 2)
                products(bank, rounds.next(), True)
                with pe.Fori(lo + 2, hi, 2) as t:
                    products(bank, rounds.next(), False)
                pe.drain().then_inc(s_acc, 1)

            def finish(d):
                pe.wait_ge(s_adj, d + 1)
                for i, (b0, n) in enumerate(GROUPS):
                    if i >= 2:
                        pe.wait_ge(s_trc, d * NG + (i - 1))
                    for k in range(n):
                        last = pe.transpose(ps[0:B, 6 + i % 2, k * B:(k + 1) * B], adj[:, b0 + k, :], g.ident[0:B, 0:B])
                    last.then_inc(s_tr, 1)
                pe.wait_ge(s_trc, d * NG + (NG - 1))
                for k in range(NB):
                    last = pe.matmul(ps[0:B, 7, 0:D + 1], adj[:, k, :], g.h[:, k, :], start=k == 0, stop=k == NB - 1)
                last.then_inc(s_n1, 1)

            for j in range(WPB):
                window(j, j, j - 1 if j >= 2 else None)
            with pe.Fori(1, NB) as d:
                window(d * WPB, 0, d * WPB)
                finish(d - 1)
                pe.wait_ge(s_trc, d * NG)
                pe.wait_ge(s_n1c, d)
                for j in range(1, WPB):
                    window(d * WPB + j, j, d * WPB + (j - 1))
            finish(NB - 1)

        @block.scalar
        def _(a):
            rounds = Counter(a)

            def scaled(t, n):
                for s in range(2):
                    at = bass.ds(t + s, 1)
                    a.wait_ge(s_lane[s], n)
                    a.activation(left[s][:, 1, :], left[s][:, COUNT, :], ACT.Copy, scale=g.wpart[1][:, at])
                    a.activation(left[s][:, 2, :], left[s][:, COUNT, :], ACT.Copy,
                                 scale=g.wpart[2][:, at]).then_inc(s_scaled[s], 1)

            def staged(w, j, reuse):
                a.wait_ge(s_acc, w + 1)
                if reuse is not None:
                    a.wait_ge(s_unstaged, reuse)
                flat = stage[j][:].rearrange("p a k h -> p (a k h)")
                bank = 3 * (j % 2)
                for i in range(2):
                    col = i * KW
                    for k, (off, c0, c1) in enumerate(PIECES[i]):
                        sums = {"accum_out": g.winsum[:, bass.ds(w * 2 + k, 1)]} if i else {}
                        last = a.activation(flat[:, col:col + c1 - c0], ps[0:B, bank + off, c0:c1], ACT.Copy, **sums)
                        col += c1 - c0
                last.then_inc(s_staged, 1)

            def finish(d, first):
                if not first:
                    a.wait_ge(s_adjout, d * 16)
                for i, (b0, n) in enumerate(GROUPS):
                    a.wait_ge(s_tr, d * NG + (i + 1))
                    a.activation(adj_t[:, b0 * B:(b0 + n) * B], ps[0:B, 6 + i % 2, 0:n * B], ACT.Copy).then_inc(s_trc, 1)
                a.wait_ge(s_n1, d + 1)
                a.activation(g.n1[:, bass.ds(d, 1), :].rearrange("p a k -> p (a k)"), ps[0:B, 7, 0:D + 1],
                             ACT.Copy).then_inc(s_n1c, 1)

            def window(w, between):
                lo, hi = tile_range(a, g, w)
                scaled(lo, rounds.next())
                between()
                with a.Fori(lo + 2, hi, 2) as t:
                    scaled(t, rounds.next())

            def block_of(d, before, own):
                window(d * WPB, lambda: before and staged(d * WPB - 1, WPB - 1, before(WPB - 1)))

                def first_two():
                    staged(d * WPB, 0, own and own(0))
                    if before:
                        finish(d - 1, before is none)

                window(d * WPB + 1, first_two)
                for j in range(2, WPB):
                    window(d * WPB + j, lambda: staged(d * WPB + (j - 1), j - 1, own and own(j - 1)))

            none = lambda j: None
            block_of(0, None, None)
            back = lambda d: lambda j: d * WPB - (WPB - 1) + j
            block_of(1, none, back(1))
            with a.Fori(2, NB) as d:
                block_of(d, back(d - 1), back(d))
            staged(NW - 1, WPB - 1, back(NB - 1)(WPB - 1))
            finish(NB - 1, False)

        @block.gpsimd
        def _(pool):
            def unstage(w, j):
                pool.wait_ge(s_staged, w + 1)
                pool.sem_inc(s_tick, 1)
                cols = lambda t: t[:, :, j * WIN:(j + 1) * WIN].rearrange("p h k -> p k h")
                pool.tensor_copy(cols(cnt[0]), stage[j][:, 1, :, :]).then_inc(s_pool, 1)
                pool.tensor_copy(cols(adj), stage[j][:, 0, :, :])
                pool.wait_ge(s_pool, w + 1)
                pool.tensor_tensor(cols(cnt[1]), stage[j][:, 1, :, :], cols(cnt[0]), ALU.subtract).then_inc(s_unstaged, 1)

            def block_of(d, first):
                if not first:
                    pool.wait_ge(s_n1, d)
                    pool.wait_ge(s_sum, d)
                    pool.wait_ge(s_cntout, d * 32)
                for j in range(WPB):
                    unstage(d * WPB + j, j)
                pool.wait_ge(s_unstaged, d * WPB + WPB)
                pool.sem_inc(s_adj, 1)

            block_of(0, True)
            with pool.Fori(1, NB) as d:
                block_of(d, False)

        @block.sync
        def _(sp):
            with sp.Fori(0, NB) as d:
                built, moved = sp.snap(d + 1), sp.snap(d * NG + NG)
                sp.wait_ge(s_adj, built)
                sp.sem_inc(s_tick, 1)
                for i in range(2):
                    sp.dma_start(dr.cnt[i, bass.ds(d, 1), :, :].rearrange("a p n -> p (a n)"),
                                 cnt[i][:].rearrange("p h k -> p (h k)")).then_inc(s_cntout, 16)
                sp.wait_ge(s_trc, moved)
                sp.sem_inc(s_tick, 1)
                sp.dma_start(dr.adj_t[bass.ds(d, 1), :, :].rearrange("a p n -> p (a n)"), adj_t[:]).then_inc(s_adjout, 16)
            sp.wait_ge(s_cntout, NB * 32)
            sp.wait_ge(s_adjout, NB * 16)


class Obj:
    pass


def program(nc, io, out):
    ctx = ExitStack()
    Phase.used.clear()
    with ctx:
        def sb(name, shape, dt=F32):
            return ctx.enter_context(nc.sbuf_tensor(name, shape, dt))

        g, dr = Obj(), Obj()
        dr.cnt = nc.dram_tensor("cnt_panels", (2, NB, B, N), BF16, kind="Internal").ap()
        dr.adj_t = nc.dram_tensor("adj_rows", (NB, B, N), F32, kind="Internal").ap()
        dr.table = nc.dram_tensor("src_table", (N, D), F32, kind="Internal").ap()
        g.x = sb("x", [B, NB, D])
        g.h = sb("h", [B, NB, D + 1])
        g.ident = sb("ident", [128, 128])
        g.dst = sb("dst", [128, NT])
        g.src_idx = sb("src_idx", [128, NT], I32)
        g.ea = sb("ea", [128, NT])
        g.bounds = sb("bounds", [1, 512], I32)
        g.n1 = sb("n1", [B, NB, D + 1])
        g.wsum_src = sb("wsum_src", [B, NB])
        g.winsum = sb("winsum", [B, 2 * NW])
        g.deg = sb("deg", [B, NB])
        with ExitStack() as building:
            def sb2(name, shape, dt=F32):
                return building.enter_context(nc.sbuf_tensor(name, shape, dt))

            g.key_id = sb2("key_id", [128, KEVEN], F16)
            g.key = sb2("key", [128, NT])
            g.lane = sb2("lane", [128, NT])
            g.wpart = [sb2(f"wpart{i}", [128, NT]) for i in range(3)]
            setup_phase(nc, g, io)
            norm_phase(nc, g, "norm0")
            build_phase(nc, g, dr)
        layers(nc, g, dr, io, out)


def chunk_copies(eng_a, eng_v, k):
    return eng_a if k % 2 == 0 else eng_v


def spmm_t_phase(nc, g, dr, name, y_in, y_out, scale, alpha, src_scale=None):
    R = 5
    with Phase(nc, name) as ph:
        rows = [ph.sb(f"rows{i}", [B, N]) for i in range(R)]
        y_one = [ph.sb(f"y_one{i}", [B, D]) for i in range(R)]
        y_t = ph.sb("y_t", [D, N])
        ps = ph.ps()
        s_row = [ph.sem(f"row{i}") for i in range(R)]
        s_used = [ph.sem(f"used{i}") for i in range(R)]
        s_one = [ph.sem(f"one{i}") for i in range(R)]
        s_tick = ph.sem("tick")
        s_sum = ph.sem("sum")
        s_tc = [ph.sem(f"tc{i}") for i in range(2)]
        s_tr = ph.sem("tr")
        s_d = ph.sem("d")
        block = ph.ctx.enter_context(nc.Block())

        @block.sync
        def _(sp):
            def load(o, i):
                sp.dma_start(rows[i][:], dr.adj_t[bass.ds(o * R + i, 1), :, :].rearrange("a p n -> p (a n)")).then_inc(s_row[i], 16)

            for i in range(R):
                load(0, i)
            with sp.Fori(1, NB // R) as o:
                for i in range(R):
                    sp.wait_ge(s_used[i], sp.snap(o))
                    sp.sem_inc(s_tick, 1)
                    load(o, i)

        @block.scalar
        def _(a):
            def one(o, i):
                a.activation(y_one[i][:], y_in[:, bass.ds(o * R + i, 1), 0:D].rearrange("p a k -> p (a k)"),
                             ACT.Copy).then_inc(s_one[i], 1)

            for i in range(R):
                one(0, i)
            with a.Fori(1, NB // R) as o:
                for i in range(R):
                    a.wait_ge(s_used[i], a.snap(o))
                    one(o, i)
            a.wait_ge(s_sum, 1)
            for k, (c, n) in enumerate(CHUNKS):
                if k % 2 == 0:
                    a.activation(y_t[:, c:c + n], ps[:, k, 0:n], ACT.Copy).then_inc(s_tc[0], 1)

        @block.tensor
        def _(pe):
            def product(o, i, first):
                pe.wait_ge(s_row[i], o * 16 + 16)
                pe.wait_ge(s_one[i], o + 1)
                for k, (c, n) in enumerate(CHUNKS):
                    last = pe.matmul(ps[:, k, 0:n], y_one[i][:], rows[i][:, c:c + n], start=first, stop=False,
                                     skip_group_check=True)
                return last

            for i in range(R):
                product(0, i, i == 0).then_inc(s_used[i], 1)
            with pe.Fori(1, NB // R) as o:
                for i in range(R):
                    product(o, i, False).then_inc(s_used[i], 1)
            pe.drain().then_inc(s_sum, 1)
            pe.wait_ge(s_tc[0], 4)
            pe.wait_ge(s_tc[1], 3)
            for k, (b0, n) in enumerate(GROUPS):
                for j in range(n):
                    last = pe.transpose(ps[0:B, k, j * D:(j + 1) * D], y_t[:, (b0 + j) * B:(b0 + j + 1) * B], g.ident[:])
                last.then_inc(s_tr, 1)

        @block.vector
        def _(v):
            do = Chain(v, s_d)
            v.wait_ge(s_sum, 1)
            for k, (c, n) in enumerate(CHUNKS):
                if k % 2 == 1:
                    v.tensor_copy(y_t[:, c:c + n], ps[:, k, 0:n]).then_inc(s_tc[1], 1)
            for k, (b0, n) in enumerate(GROUPS):
                v.wait_ge(s_tr, k + 1)
                last = v.tensor_copy(y_out[:, b0:b0 + n, 0:D], ps[0:B, k, 0:n * D].rearrange("p (a k) -> p a k", k=D))
            do(last)
            if scale is not None:
                do(v.tensor_tensor(y_out[:, :, 0:D], y_out[:, :, 0:D], bc(scale, D), ALU.mult))
            if alpha is not None:
                do(v.scalar_tensor_tensor(g.x[:], y_out[:, :, 0:D], alpha, g.x[:], ALU.mult, ALU.add))


def transposed(pe, ps, bank, in_, ident, blocks, sem):
    for j, b in enumerate(blocks):
        last = pe.transpose(ps[:, bank, j * B:(j + 1) * B], in_(b), ident[0:B, 0:B])
    last.then_inc(sem, 1)


def weights_phase(nc, g, io, w):
    with Phase(nc, "gruw") as ph:
        w12 = [ph.sb(f"w{i}", [D, D]) for i in range(2)]
        wih = ph.sb("wih", [128, 3, 2 * D])
        whh = ph.sb("whh", [128, 3, D])
        wih_t = ph.sb("wih_t", [128, 2, 3 * D])
        bih = ph.sb("bih", [1, 3 * D])
        ps = ph.ps()
        s_in = ph.sem("in")
        s_tr = ph.sem("tr")
        s_c = ph.sem("c")
        s_m = ph.sem("m")
        s_d = ph.sem("d")
        block = ph.ctx.enter_context(nc.Block())

        @block.sync
        def _(sp):
            sp.dma_start(w12[0][:], io["W1"]).then_inc(s_in, 16)
            sp.dma_start(w12[1][:], io["W2"]).then_inc(s_in, 16)
            sp.dma_start(wih[:], io["w_ih"].rearrange("(t p) k -> p t k", p=128)).then_inc(s_in, 16)
            sp.dma_start(whh[:], io["w_hh"].rearrange("(t p) k -> p t k", p=128)).then_inc(s_in, 16)
            sp.dma_start(bih[:], io["b_ih"].rearrange("(a k) -> a k", a=1)).then_inc(s_in, 16)
            sp.dma_start(w.bhh[:], io["b_hh"].rearrange("(a k) -> a k", a=1)).then_inc(s_in, 16)
            sp.dma_start(w.alpha[:], io["alpha"].rearrange("(a k) -> a k", a=1).to_broadcast([B, 4])).then_inc(s_in, 16)

        @block.tensor
        def _(pe):
            pe.wait_ge(s_in, 112)
            for i in range(2):
                for t in range(3):
                    last = pe.transpose(ps[:, i, t * D:(t + 1) * D], wih[:, t, i * D:(i + 1) * D], g.ident[:])
                last.then_inc(s_tr, 1)
            for t in range(3):
                last = pe.transpose(ps[:, 2, t * D:(t + 1) * D], whh[:, t, :], g.ident[:])
            last.then_inc(s_tr, 1)
            pe.wait_ge(s_c, 3)
            for i in range(2):
                last = pe.matmul(ps[:, 3 + i, 0:3 * D], w12[i][:], wih_t[:, i, :], start=True, stop=True)
            last.then_inc(s_m, 1)

        @block.vector
        def _(v):
            v.wait_ge(s_tr, 3)
            for i in range(2):
                v.tensor_copy(wih_t[:, i, :], ps[:, i, 0:3 * D]).then_inc(s_c, 1)
            v.tensor_copy(w.whh_t[:], ps[:, 2, 0:3 * D]).then_inc(s_c, 1)
            do = Chain(v, s_d)
            do(v.tensor_tensor(w.brow[:, 0:2 * D], bih[:, 0:2 * D], w.bhh[:, 0:2 * D], ALU.add))
            do(v.tensor_copy(w.brow[:, 2 * D:3 * D], bih[:, 2 * D:3 * D]))
            v.wait_ge(s_m, 1)
            for i in range(2):
                v.tensor_copy(w.m[:, i, :], ps[:, 3 + i, 0:3 * D])
            do(v.tensor_reduce(w.tmp[:, 0:1], w.alpha[:], AX.X, ALU.max))
            v.tensor_scalar(w.alpha[:], w.alpha[:], w.tmp[:, 0:1], None, ALU.subtract).then_inc(s_c, 1)
            v.wait_ge(s_c, 5)
            do(v.tensor_reduce(w.tmp[:, 0:1], w.alpha[:], AX.X, ALU.add))
            do(v.reciprocal(w.tmp[:, 1:2], w.tmp[:, 0:1]))
            do(v.tensor_scalar(w.alpha[:], w.alpha[:], w.tmp[:, 1:2], None, ALU.mult))
            for sums, out in ((g.wsum_src[:], w.r_src[:]), (g.n1[:, :, D], w.r_dst[:])):
                do(v.tensor_scalar(w.pos[:], sums, 0.0, None, ALU.is_gt))
                do(v.tensor_tensor(out, sums, w.pos[:], ALU.mult))
                do(v.tensor_scalar(w.neg[:], w.pos[:], -1.0, 1.0, ALU.mult, ALU.add))
                do(v.tensor_tensor(out, out, w.neg[:], ALU.add))
                do(v.reciprocal(out, out))
                do(v.tensor_tensor(out, out, w.pos[:], ALU.mult))
            do(v.tensor_tensor(g.n1[:, :, 0:D], g.n1[:, :, 0:D], bc(w.r_dst[:], D), ALU.mult))

        @block.scalar
        def _(a):
            a.wait_ge(s_c, 4)
            a.activation(w.alpha[:], w.alpha[:], ACT.Exp).then_inc(s_c, 1)


def gru_phase(nc, g, w, n2):
    with Phase(nc, "gru") as ph:
        tr = [ph.sb(f"tr{i}", [D, N]) for i in range(3)]
        rz = ph.sb("rz", [B, NB, 2 * D])
        t = ph.sb("t", [B, NB, D])
        ones = ph.sb("ones", [1, B])
        ps = ph.ps()
        s_one = ph.sem("one")
        s_tr = ph.sem("tr")
        s_c = [ph.sem(f"c{i}") for i in range(2)]
        s_g = ph.sem("g")
        s_sig = ph.sem("sig")
        s_t = ph.sem("t")
        s_nn = ph.sem("nn")
        s_d = ph.sem("d")
        block = ph.ctx.enter_context(nc.Block())
        jobs = [(i, b0, n) for i in range(3) for b0, n in GROUPS]
        srcs = [g.n1, n2, g.h]
        even, odd = (len(jobs) + 1) // 2, len(jobs) // 2

        @block.tensor
        def _(pe):
            for k, (i, b0, n) in enumerate(jobs):
                if k >= 8:
                    pe.wait_ge(s_c[k % 2], (k - 8) // 2 + 1)
                transposed(pe, ps, k % 8, lambda b: srcs[i][:, b, 0:D], g.ident, range(b0, b0 + n), s_tr)
            pe.wait_ge(s_c[0], even)
            pe.wait_ge(s_c[1], odd)
            pe.wait_ge(s_one, 1)
            for b in range(NB):
                at = slice(b * B, (b + 1) * B)
                p, q = 2 * (b % 3), 2 * (b % 3) + 1
                if b >= 3:
                    pe.wait_ge(s_t, b - 2)
                pe.matmul(ps[0:B, p, 0:3 * D], tr[0][:, at], w.m[:, 0, :], start=True, stop=False)
                pe.matmul(ps[0:B, p, 0:3 * D], tr[1][:, at], w.m[:, 1, :], start=False, stop=False)
                pe.matmul(ps[0:B, p, 0:2 * D], tr[2][:, at], w.whh_t[:, 0:2 * D], start=False, stop=False)
                pe.matmul(ps[0:B, p, 0:3 * D], ones[:], w.brow[:], start=False, stop=True)
                pe.matmul(ps[0:B, q, 0:D], tr[2][:, at], w.whh_t[:, 2 * D:3 * D], start=True, stop=False)
                pe.matmul(ps[0:B, q, 0:D], ones[:], w.bhh[:, 2 * D:3 * D], start=False, stop=True).then_inc(s_g, 1)

        @block.scalar
        def _(a):
            for k, (i, b0, n) in enumerate(jobs):
                if k % 2 == 0:
                    a.wait_ge(s_tr, k + 1)
                    a.activation(tr[i][:, b0 * B:(b0 + n) * B], ps[:, k % 8, 0:n * B], ACT.Copy).then_inc(s_c[0], 1)
            for b in range(NB):
                a.wait_ge(s_g, b + 1)
                a.activation(rz[:, b, :], ps[0:B, 2 * (b % 3), 0:2 * D], ACT.Sigmoid).then_inc(s_sig, 1)
            a.wait_ge(s_t, NB)
            a.activation(t[:], t[:], ACT.Tanh).then_inc(s_nn, 1)

        @block.vector
        def _(v):
            v.memset(ones[:], 1.0).then_inc(s_one, 1)
            for k, (i, b0, n) in enumerate(jobs):
                if k % 2 == 1:
                    v.wait_ge(s_tr, k + 1)
                    v.tensor_copy(tr[i][:, b0 * B:(b0 + n) * B], ps[:, k % 8, 0:n * B]).then_inc(s_c[1], 1)
            do = Chain(v, s_d)
            for b in range(NB):
                v.wait_ge(s_sig, b + 1)
                do(v.tensor_tensor(t[:, b, :], rz[:, b, 0:D], ps[0:B, 2 * (b % 3) + 1, 0:D], ALU.mult))
                v.tensor_tensor(t[:, b, :], t[:, b, :], ps[0:B, 2 * (b % 3), 2 * D:3 * D], ALU.add).then_inc(s_t, 1)
            v.wait_ge(s_nn, 1)
            do(v.tensor_tensor(rz[:, :, 0:D], g.h[:, :, 0:D], t[:], ALU.subtract))
            do(v.tensor_tensor(rz[:, :, 0:D], rz[:, :, 0:D], rz[:, :, D:2 * D], ALU.mult))
            do(v.tensor_tensor(g.x[:], g.x[:], t[:], ALU.add))
            do(v.tensor_tensor(g.x[:], g.x[:], rz[:, :, 0:D], ALU.add))


def query_key_phase(nc, g, io, a2):
    with Phase(nc, "qk") as ph:
        h_t = ph.sb("h_t", [D, N])
        wqk = ph.sb("wqk", [D, 2, HEADS * D])
        bqk = ph.sb("bqk", [1, 2, HEADS * D])
        q = ph.sb("q", [B, NB, HEADS * D])
        sq = ph.sb("sq", [B, 2, HEADS * D])
        nrm = ph.sb("nrm", [B, 2, NB, HEADS])
        inv = ph.sb("inv", [B, 2, NB, HEADS])
        ones = ph.sb("ones", [B, 1])
        onerow = ph.sb("onerow", [1, B])
        ksum = ph.sb("ksum", [D, HEADS])
        ps = ph.ps()
        s_in = ph.sem("in")
        s_one = ph.sem("one")
        s_tr = ph.sem("tr")
        s_c = [ph.sem(f"c{i}") for i in range(2)]
        s_q = ph.sem("q")
        s_qc = ph.sem("qc")
        s_sq = ph.sem("sq")
        s_n = ph.sem("n")
        s_unit = ph.sem("unit")
        s_qt = ph.sem("qt")
        s_qtc = [ph.sem(f"qtc{i}") for i in range(2)]
        s_ks = ph.sem("ks")
        s_ksc = ph.sem("ksc")
        s_den = ph.sem("den")
        s_d = ph.sem("d")
        block = ph.ctx.enter_context(nc.Block())
        jobs = [(h, b0, n) for h in range(HEADS) for b0, n in GROUPS]

        @block.sync
        def _(sp):
            for i, n in enumerate(("Wq", "Wk")):
                sp.dma_start(wqk[:, i, :], io[n + "_w"]).then_inc(s_in, 16)
                sp.dma_start(bqk[:, i, :], io[n + "_b"].rearrange("(a k) -> a k", a=1)).then_inc(s_in, 16)

        @block.tensor
        def _(pe):
            for k, (b0, n) in enumerate(GROUPS):
                transposed(pe, ps, k, lambda b: g.h[:, b, 0:D], g.ident, range(b0, b0 + n), s_tr)
            pe.wait_ge(s_c[0], 4)
            pe.wait_ge(s_c[1], 3)
            pe.wait_ge(s_in, 64)
            pe.wait_ge(s_one, 2)
            for b in range(NB):
                if b >= 4:
                    pe.wait_ge(s_qc, b - 3)
                for i in range(2):
                    at = slice(i * HEADS * D, (i + 1) * HEADS * D)
                    pe.matmul(ps[0:B, b % 4, at], h_t[:, b * B:(b + 1) * B], wqk[:, i, :], start=True, stop=False)
                    last = pe.matmul(ps[0:B, b % 4, at], onerow[:], bqk[:, i, :], start=False, stop=True)
                last.then_inc(s_q, 1)
            pe.wait_ge(s_unit, 2)
            pe.wait_ge(s_qc, NB)
            for h in range(HEADS):
                for b in range(NB):
                    last = pe.matmul(ps[:, 7, h:h + 1], a2.ks[:, b, h * D:(h + 1) * D], ones[:], start=b == 0,
                                     stop=b == NB - 1)
            last.then_inc(s_ks, 1)
            for k, (h, b0, n) in enumerate(jobs):
                if k >= 4:
                    pe.wait_ge(s_qtc[k % 2], (k - 4) // 2 + 1)
                transposed(pe, ps, k % 4, lambda b: q[:, b, h * D:(h + 1) * D], g.ident, range(b0, b0 + n), s_qt)
            pe.wait_ge(s_qtc[0], 7)
            pe.wait_ge(s_qtc[1], 7)
            pe.wait_ge(s_ksc, 1)
            for b in range(NB):
                for h in range(HEADS):
                    last = pe.matmul(ps[0:B, 6, b * HEADS + h:b * HEADS + h + 1], a2.qs_t[:, h, b * B:(b + 1) * B],
                                     ksum[:, h:h + 1], start=True, stop=True)
            last.then_inc(s_den, 1)

        @block.scalar
        def _(a):
            for k, (b0, n) in enumerate(GROUPS):
                if k % 2 == 0:
                    a.wait_ge(s_tr, k + 1)
                    a.activation(h_t[:, b0 * B:(b0 + n) * B], ps[:, k, 0:n * B], ACT.Copy).then_inc(s_c[0], 1)
            for b in range(NB):
                a.wait_ge(s_q, b + 1)
                if b:
                    a.wait_ge(s_sq, b)
                for i in range(2):
                    for h in range(HEADS):
                        at = (i * HEADS + h) * D
                        last = a.activation(sq[:, i, h * D:(h + 1) * D], ps[0:B, b % 4, at:at + D], ACT.Square,
                                            accum_out=nrm[:, i, b, h:h + 1])
                last.then_inc(s_sq, 1)
            a.wait_ge(s_sq, NB)
            a.activation(nrm[:], nrm[:], ACT.Sqrt).then_inc(s_n, 1)
            for k, (h, b0, n) in enumerate(jobs):
                if k % 2 == 0:
                    a.wait_ge(s_qt, k + 1)
                    a.activation(a2.qs_t[:, h, b0 * B:(b0 + n) * B], ps[:, k % 4, 0:n * B], ACT.Copy).then_inc(s_qtc[0], 1)

        @block.vector
        def _(v):
            do = Chain(v, s_d)
            v.memset(ones[:], 1.0).then_inc(s_one, 1)
            v.memset(onerow[:], 1.0).then_inc(s_one, 1)
            for k, (b0, n) in enumerate(GROUPS):
                if k % 2 == 1:
                    v.wait_ge(s_tr, k + 1)
                    v.tensor_copy(h_t[:, b0 * B:(b0 + n) * B], ps[:, k, 0:n * B]).then_inc(s_c[1], 1)
            for b in range(NB):
                v.wait_ge(s_sq, b + 1)
                v.tensor_copy(q[:, b, :], ps[0:B, b % 4, 0:HEADS * D])
                v.tensor_copy(a2.ks[:, b, :], ps[0:B, b % 4, HEADS * D:2 * HEADS * D]).then_inc(s_qc, 1)
            v.wait_ge(s_qc, NB)
            v.wait_ge(s_n, 1)
            do(v.reciprocal(inv[:], nrm[:]))
            for i, t in enumerate((q, a2.ks)):
                heads = t[:].rearrange("p b (h k) -> p (b h) k", h=HEADS)
                v.tensor_tensor(heads, heads, bc(inv[:, i, :, :].rearrange("p b h -> p (b h)"), D),
                                ALU.mult).then_inc(s_unit, 1)
            v.wait_ge(s_ks, 1)
            v.tensor_copy(ksum[:], ps[:, 7, 0:HEADS]).then_inc(s_ksc, 1)
            for k, (h, b0, n) in enumerate(jobs):
                if k % 2 == 1:
                    v.wait_ge(s_qt, k + 1)
                    v.tensor_copy(a2.qs_t[:, h, b0 * B:(b0 + n) * B], ps[:, k % 4, 0:n * B]).then_inc(s_qtc[1], 1)
            v.wait_ge(s_den, 1)
            do(v.tensor_scalar(a2.rden[:], ps[0:B, 6, 0:NB * HEADS], float(N), None, ALU.add))
            do(v.reciprocal(a2.rden[:], a2.rden[:]))
            for h in range(HEADS):
                v.tensor_copy(a2.t[:, :, h * D:(h + 1) * D], g.h[:, :, 0:D])
            do(v.tensor_reduce(a2.most[:], g.winsum[:], AX.X, ALU.max))


def parts_flag_phase(nc, g, a2):
    with Phase(nc, "flag") as ph:
        row = ph.sb("row", [1, B])
        most = ph.sb("most", [1, 1])
        ps = ph.ps()
        s_t = ph.sem("t")
        s_d = ph.sem("d")
        block = ph.ctx.enter_context(nc.Block())

        @block.tensor
        def _(pe):
            pe.transpose(ps[0:1, 0, 0:B], a2.most[:], g.ident[0:B, 0:B]).then_inc(s_t, 1)

        @block.vector
        def _(v):
            do = Chain(v, s_d)
            v.wait_ge(s_t, 1)
            do(v.tensor_copy(row[:], ps[0:1, 0, 0:B]))
            do(v.tensor_reduce(most[:], row[:], AX.X, ALU.max))
            do(v.tensor_scalar(most[:], most[:], 256.0, 1.0, ALU.is_gt, ALU.add))
            do(v.tensor_copy(a2.nparts[:], most[:]))
            do(v.memset(a2.xp[:, :, 0, HEADS * D:HEADS * D + 1], 1.0))


def term_phase(nc, g, a2, k, last_term):
    with Phase(nc, f"term{k}") as ph:
        t_t = ph.sb("t_t", [D, 4, 4 * B])
        rest = ph.sb("rest", [B, 5, HEADS * D])
        ones = ph.sb("ones", [B, 1])
        ps = ph.ps()
        s_one = ph.sem("one")
        s_tr = ph.sem("tr")
        s_tc = ph.sem("tc")
        s_y = ph.sem("y")
        s_yc = ph.sem("yc")
        s_kv = ph.sem("kv")
        s_d = ph.sem("d")
        s_p = ph.sem("p")
        block = ph.ctx.enter_context(nc.Block())
        W = HEADS * D

        @block.tensor
        def _(pe):
            pe.wait_ge(s_one, 1)
            if not last_term:
                for h in range(HEADS):
                    for b in range(NB):
                        pe.matmul(ps[:, 6, h * D:(h + 1) * D], a2.ks[:, b, h * D:(h + 1) * D],
                                  a2.t[:, b, h * D:(h + 1) * D], start=b == 0, stop=b == NB - 1)
                for b in range(NB):
                    last = pe.matmul(ps[0:1, 7, 0:W], ones[:], a2.t[:, b, 0:W], start=b == 0, stop=b == NB - 1)
                last.then_inc(s_kv, 1)

            def project(i, b0, n):
                pe.wait_ge(s_tc, 2 * i + 2)
                if i >= 2:
                    pe.wait_ge(s_yc, i - 1)
                for j in range(n):
                    for h in range(HEADS):
                        last = pe.matmul(ps[0:B, 4 + i % 2, j * D:(j + 1) * D],
                                         t_t[:, 2 * (i % 2) + h, j * B:(j + 1) * B],
                                         a2.wo[:, h * (ORDER + 1) + k, :], start=h == 0, stop=h == HEADS - 1)
                last.then_inc(s_y, 1)

            for i, (b0, n) in enumerate(GROUPS):
                for h in range(HEADS):
                    transposed(pe, ps, 2 * (i % 2) + h, lambda b: a2.t[:, b, h * D:(h + 1) * D], g.ident,
                               range(b0, b0 + n), s_tr)
                if i:
                    project(i - 1, *GROUPS[i - 1])
            project(len(GROUPS) - 1, *GROUPS[-1])

        @block.scalar
        def _(a):
            for i, (b0, n) in enumerate(GROUPS):
                for h in range(HEADS):
                    a.wait_ge(s_tr, 2 * i + h + 1)
                    if i >= 2:
                        a.wait_ge(s_y, i - 1)
                    a.activation(t_t[:, 2 * (i % 2) + h, 0:n * B], ps[:, 2 * (i % 2) + h, 0:n * B],
                                 ACT.Copy).then_inc(s_tc, 1)

        @block.gpsimd
        def _(pool):
            pool.memset(ones[:], 1.0).then_inc(s_one, 1)

        @block.vector
        def _(v):
            do = Chain(v, s_d)
            for i, (b0, n) in enumerate(GROUPS):
                if not last_term and i < 5:
                    at = slice(5 * i, 5 * i + 5)
                    do(v.tensor_copy(a2.xp[:, at, 0, 0:W], a2.t[:, at, 0:W]))
                    do(v.tensor_tensor(rest[:], a2.t[:, at, 0:W], a2.xp[:, at, 0, 0:W], ALU.subtract))
                    do(v.tensor_copy(a2.xp[:, at, 1, 0:W], rest[:]))
                    do(v.tensor_tensor(rest[:], rest[:], a2.xp[:, at, 1, 0:W], ALU.subtract))
                    do(v.tensor_copy(a2.xp[:, at, 2, 0:W], rest[:]))
                v.wait_ge(s_y, i + 1)
                blocks = ps[0:B, 4 + i % 2, 0:n * D].rearrange("p (a k) -> p a k", k=D)
                if k == 0:
                    v.tensor_copy(a2.y[:, b0:b0 + n, :], blocks).then_inc(s_yc, 1)
                else:
                    v.tensor_tensor(a2.y[:, b0:b0 + n, :], a2.y[:, b0:b0 + n, :], blocks, ALU.add).then_inc(s_yc, 1)
            if not last_term:
                v.wait_ge(s_kv, 1)
                v.tensor_copy(a2.kv[:], ps[:, 6, 0:W])
                do(v.tensor_copy(a2.vsum[:], ps[0:1, 7, 0:W]))
            else:
                v.wait_ge(s_yc, len(GROUPS))
                do(v.tensor_tensor(a2.y[:], a2.y[:], a2.wob[:].unsqueeze(1).to_broadcast([B, NB, D]), ALU.add))
                do(v.scalar_tensor_tensor(g.x[:], a2.y[:], 1.0 / HEADS, g.x[:], ALU.mult, ALU.add))


def count_phase(nc, g, dr, a2, k):
    R = 5
    W = HEADS * D
    lo = D if k == 0 else 0
    with Phase(nc, f"count{k}") as ph:
        panel = [ph.sb(f"panel{i}", [B, N], BF16) for i in range(R)]
        ps = ph.ps()
        s_zero = ph.sem("zero")
        s_in = [ph.sem(f"in{i}") for i in range(R)]
        s_used = [ph.sem(f"used{i}") for i in range(R)]
        s_added = [ph.sem(f"added{i}") for i in range(R)]
        s_tick = ph.sem("tick")
        block = ph.ctx.enter_context(nc.Block())

        @block.gpsimd
        def _(pool):
            pool.memset(a2.t[:], 0.0).then_inc(s_zero, 1)

        @block.sync
        def _(sp):
            nparts = sp.value_load(a2.nparts[0:1, 0:1], min_val=1, max_val=2)
            rounds = Counter(sp)
            for i in range(R):
                sp.sem_inc(s_used[i], 1)
            with sp.Fori(0, nparts) as part:
                with sp.Fori(0, NB // R) as o:
                    n = rounds.next()
                    for i in range(R):
                        sp.wait_ge(s_used[i], n)
                        sp.sem_inc(s_tick, 1)
                        sp.dma_start(panel[i][:], dr.cnt[bass.ds(part, 1), bass.ds(o * R + i, 1), :, :]
                                     .rearrange("q a p n -> p (q a n)")).then_inc(s_in[i], 16)

        @block.tensor
        def _(pe):
            nparts = pe.value_load(a2.nparts[0:1, 0:1], min_val=1, max_val=2)
            rounds = Counter(pe)
            for i in range(R):
                pe.sem_inc(s_added[i], 1)
            with pe.Fori(0, nparts):
                with pe.Fori(0, NB // R):
                    n = rounds.next()
                    landed = pe.snap(n * 16)
                    for i in range(R):
                        pe.wait_ge(s_in[i], landed)
                        pe.wait_ge(s_added[i], n)
                        for b in range(NB):
                            for p in range(3):
                                hi = W + 1 if p == 0 else W
                                last = pe.matmul(ps[0:B, i, lo:hi], panel[i][:, b * B:(b + 1) * B],
                                                 a2.xp[:, b, p, lo:hi], start=b == 0 and p == 0,
                                                 stop=b == NB - 1 and p == 2, skip_group_check=True)
                        last.then_inc(s_used[i], 1)

        @block.vector
        def _(v):
            nparts = v.value_load(a2.nparts[0:1, 0:1], min_val=1, max_val=2)
            rounds = Counter(v)
            v.wait_ge(s_zero, 1)
            with v.Fori(0, nparts):
                with v.Fori(0, NB // R) as o:
                    n = rounds.next()
                    used = v.snap(n + 1)
                    for i in range(R):
                        at = a2.t[:, bass.ds(o * R + i, 1), lo:W + 1].rearrange("p a k -> p (a k)")
                        v.wait_ge(s_used[i], used)
                        v.tensor_tensor(at, at, ps[0:B, i, lo:W + 1], ALU.add).then_inc(s_added[i], 1)


def combine_phase(nc, g, a2, k):
    W = HEADS * D
    with Phase(nc, f"comb{k}") as ph:
        pos = ph.sb("pos", [B, NB])
        neg = ph.sb("neg", [B, NB])
        onerow = ph.sb("onerow", [1, B])
        ps = ph.ps()
        s_one = ph.sem("one")
        s_at = ph.sem("at")
        s_free = ph.sem("free")
        s_d = ph.sem("d")
        block = ph.ctx.enter_context(nc.Block())
        K = 8

        @block.tensor
        def _(pe):
            pe.wait_ge(s_one, 1)
            for b in range(NB):
                if b >= K:
                    pe.wait_ge(s_free, b - K + 1)
                for h in range(HEADS):
                    at = slice(h * D, (h + 1) * D)
                    pe.matmul(ps[0:B, b % K, at], a2.qs_t[:, h, b * B:(b + 1) * B], a2.kv[:, at], start=True, stop=False)
                    last = pe.matmul(ps[0:B, b % K, at], onerow[:], a2.vsum[:, at], start=False, stop=True)
                last.then_inc(s_at, 1)

        @block.vector
        def _(v):
            do = Chain(v, s_d)
            v.memset(onerow[:], 1.0).then_inc(s_one, 1)
            if k == 0:
                do(v.tensor_copy(g.deg[:], a2.t[:, :, W]))
                do(v.tensor_scalar(pos[:], g.deg[:], 0.0, None, ALU.is_gt))
                do(v.tensor_scalar(neg[:], pos[:], -1.0, 1.0, ALU.mult, ALU.add))
                do(v.tensor_tensor(neg[:], neg[:], g.deg[:], ALU.add))
                do(v.reciprocal(neg[:], neg[:]))
                do(v.scalar_tensor_tensor(a2.half_inv[:], neg[:], 0.5, pos[:], ALU.mult, ALU.mult))
                do(v.tensor_copy(a2.t[:, :, 0:D], a2.t[:, :, D:W]))
            do(v.tensor_tensor(a2.t[:, :, 0:W], a2.t[:, :, 0:W], bc(a2.half_inv[:], W), ALU.mult))
            for b in range(NB):
                v.wait_ge(s_at, b + 1)
                for h in range(HEADS):
                    at = slice(h * D, (h + 1) * D)
                    last = v.scalar_tensor_tensor(a2.t[:, b, at], ps[0:B, b % K, at],
                                                  a2.rden[:, b * HEADS + h:b * HEADS + h + 1], a2.t[:, b, at],
                                                  ALU.mult, ALU.add)
                last.then_inc(s_free, 1)


def message_table_phase(nc, g, dr, io, a3):
    with Phase(nc, "table") as ph:
        w1 = ph.sb("w1", [D, 2, D])
        b1 = ph.sb("b1", [1, 2 * D])
        onerow = ph.sb("onerow", [1, B])
        src = ph.sb("src", [B, NB, D])
        ps = ph.ps()
        s_in = ph.sem("in")
        s_one = ph.sem("one")
        s_tr = ph.sem("tr")
        s_c = [ph.sem(f"c{i}") for i in range(2)]
        s_p = ph.sem("p")
        s_pc = [ph.sem(f"pc{i}") for i in range(2)]
        s_out = ph.sem("out")
        block = ph.ctx.enter_context(nc.Block())

        @block.sync
        def _(sp):
            sp.dma_start(w1[:], io["mw1"][0:2 * D, :].rearrange("(a p) k -> p a k", p=D)).then_inc(s_in, 16)
            sp.wait_ge(s_one, 1)
            sp.dma_start(b1[:, D:2 * D], io["mb1"].rearrange("(a k) -> a k", a=1)).then_inc(s_in, 16)
            sp.dma_start(a3.q[B:B + 1, :], io["mw1"][2 * D:2 * D + 1, :]).then_inc(s_in, 16)
            sp.wait_ge(s_pc[0], NB)
            sp.dma_start(dr.table.rearrange("(b p) d -> p b d", p=B), src[:]).then_inc(s_out, 16)
            sp.wait_ge(s_out, 16)
            sp.wait_ge(s_in, 48)

        @block.tensor
        def _(pe):
            for k, (b0, n) in enumerate(GROUPS):
                transposed(pe, ps, k, lambda b: g.h[:, b, 0:D], g.ident, range(b0, b0 + n), s_tr)
            pe.wait_ge(s_c[0], 4)
            pe.wait_ge(s_c[1], 3)
            pe.wait_ge(s_in, 48)
            pe.wait_ge(s_one, 2)
            for b in range(NB):
                if b >= 8:
                    pe.wait_ge(s_pc[0], b - 7)
                    pe.wait_ge(s_pc[1], b - 7)
                pe.matmul(ps[0:B, b % 8, 0:2 * D], a3.h_t[:, b * B:(b + 1) * B], w1[:].rearrange("p a k -> p (a k)"),
                          start=True, stop=False)
                pe.matmul(ps[0:B, b % 8, 0:2 * D], onerow[:], b1[:], start=False, stop=True).then_inc(s_p, 1)

        @block.scalar
        def _(a):
            for k, (b0, n) in enumerate(GROUPS):
                if k % 2 == 0:
                    a.wait_ge(s_tr, k + 1)
                    a.activation(a3.h_t[:, b0 * B:(b0 + n) * B], ps[:, k, 0:n * B], ACT.Copy).then_inc(s_c[0], 1)
            for b in range(NB):
                a.wait_ge(s_p, b + 1)
                a.activation(src[:, b, :], ps[0:B, b % 8, 0:D], ACT.Copy).then_inc(s_pc[0], 1)

        @block.vector
        def _(v):
            v.memset(b1[:], 0.0).then_inc(s_one, 1)
            v.memset(onerow[:], 1.0).then_inc(s_one, 1)
            for k, (b0, n) in enumerate(GROUPS):
                if k % 2 == 1:
                    v.wait_ge(s_tr, k + 1)
                    v.tensor_copy(a3.h_t[:, b0 * B:(b0 + n) * B], ps[:, k, 0:n * B]).then_inc(s_c[1], 1)
            for b in range(NB):
                v.wait_ge(s_pc[0], b + 1)
                v.tensor_copy(a3.q_all[:, b, :], ps[0:B, b % 8, D:2 * D]).then_inc(s_pc[1], 1)


def edge_phase(nc, g, dr, a3):
    S, T = 4, 1
    STEP = S * T
    with Phase(nc, "edge") as ph:
        idx = [ph.sb(f"idx{s}", [128, T], I32) for s in range(S)]
        rows = [[ph.sb(f"rows{s}{i}", [128, D]) for i in range(T)] for s in range(S)]
        hot = [ph.sb(f"hot{s}", [128, T, B + 1]) for s in range(S)]
        hot_t = [ph.sb(f"hot_t{s}", [B + 1, T * 128]) for s in range(S)]
        act = [ph.sb(f"act{s}", [128, T * D]) for s in range(S)]
        lane_id = ph.sb("lane_id", [128, B])
        ps = ph.ps()
        s_lane = ph.sem("lane")
        s_idx = [ph.sem(f"idx{s}") for s in range(S)]
        s_rows = [[ph.sem(f"rows{s}{i}") for i in range(T)] for s in range(S)]
        s_hot = [ph.sem(f"hot{s}") for s in range(S)]
        s_tr = [ph.sem(f"tr{s}") for s in range(S)]
        s_hot_t = [ph.sem(f"hot_t{s}") for s in range(S)]
        s_pre = [ph.sem(f"pre{s}") for s in range(S)]
        s_act = [ph.sem(f"act{s}") for s in range(S)]
        s_sum = [ph.sem(f"sum{s}") for s in range(S)]
        s_q = ph.sem("q")
        s_shift = ph.sem("shift")
        s_blk = ph.sem("blk")
        s_out = ph.sem("out")
        s_tick = ph.sem("tick")
        block = ph.ctx.enter_context(nc.Block())

        def tiles(eng, d, body):
            lo, hi = tile_range(eng, g, d + 256)
            body(lo, True)
            with eng.Fori(lo + STEP, hi, STEP) as t:
                body(t, False)

        @block.gpsimd
        def _(pool):
            pool.iota(lane_id[:], [[1, B]], base=0, channel_multiplier=0,
                      allow_small_or_imprecise_dtypes=True).then_inc(s_lane, 1)
            rounds = Counter(pool)

            def gather(t, first):
                n = rounds.next()
                for s in range(S):
                    pool.wait_ge(s_pre[s], n)
                    pool.sem_inc(s_tick, 1)
                    pool.tensor_copy(idx[s][:], g.src_idx[:, bass.ds(t + s * T, T)]).then_inc(s_idx[s], 1)
                for s in range(S):
                    pool.wait_ge(s_idx[s], n)
                    pool.sem_inc(s_tick, 1)
                    for i in range(T):
                        pool.indirect_dma_start(rows[s][i][:], None, dr.table,
                                                bass.IndirectOffsetOnAxis(ap=idx[s][:, i:i + 1], axis=0)
                                                ).then_inc(s_rows[s][i], 16)

            with pool.Fori(0, NB) as d:
                tiles(pool, d, gather)

        @block.vector
        def _(v):
            rounds = Counter(v)
            v.wait_ge(s_lane, 1)

            def one_hot(t, first):
                n = rounds.next()
                for s in range(S):
                    v.wait_ge(s_sum[s], n)
                    for i in range(T):
                        at = bass.ds(t + (s * T + i), 1)
                        v.tensor_scalar(hot[s][:, i, 0:B], lane_id[:], g.dst[:, at], None, ALU.is_equal)
                        last = v.tensor_copy(hot[s][:, i, B:B + 1], g.ea[:, at])
                    last.then_inc(s_hot[s], 1)

            def block_of(d):
                tiles(v, d, one_hot)

            block_of(0)
            with v.Fori(1, NB) as d:
                so_far = v.snap(rounds.reg)
                for s in range(S):
                    v.wait_ge(s_hot[s], so_far)
                v.tensor_scalar(g.dst[:], g.dst[:], -float(B), None, ALU.add).then_inc(s_shift, 1)
                v.wait_ge(s_shift, v.snap(d))
                block_of(d)

        @block.tensor
        def _(pe):
            rounds = Counter(pe)
            for s in range(S):
                pe.sem_inc(s_sum[s], 1)
                pe.sem_inc(s_pre[s], 1)

            def messages(t, first):
                n = rounds.next()
                landed = pe.snap(n * 16)
                for s in range(S):
                    pe.wait_ge(s_hot[s], n)
                    for i in range(T):
                        last = pe.transpose(ps[0:B + 1, s, i * 128:(i + 1) * 128], hot[s][:, i, :], g.ident[:])
                    last.then_inc(s_tr[s], 1)
                for s in range(S):
                    pe.wait_ge(s_hot_t[s], n)
                    for i in range(T):
                        at = slice(128, 256)
                        pe.wait_ge(s_rows[s][i], landed)
                        pe.matmul(ps[:, s, at], hot_t[s][:, i * 128:(i + 1) * 128], a3.q[:], start=True, stop=False)
                        last = pe.matmul(ps[:, s, at], g.ident[:], rows[s][i][:], start=False, stop=True)
                    last.then_inc(s_pre[s], 1)
                for s in range(S):
                    pe.wait_ge(s_act[s], n)
                    for i in range(T):
                        last = pe.matmul(ps[:, 4, 0:B], act[s][:, i * D:(i + 1) * D], hot[s][:, i, 0:B],
                                         start=first and s == 0 and i == 0, stop=False, skip_group_check=True)
                    last.then_inc(s_sum[s], 1)

            with pe.Fori(0, NB) as d:
                pe.wait_ge(s_q, d + 1)
                tiles(pe, d, messages)
                pe.drain().then_inc(s_blk, 1)

        @block.scalar
        def _(a):
            rounds = Counter(a)

            def steps(t, first):
                n = rounds.next()
                for s in range(S):
                    a.wait_ge(s_tr[s], n)
                    a.activation(hot_t[s][:], ps[0:B + 1, s, 0:T * 128], ACT.Copy).then_inc(s_hot_t[s], 1)
                for s in range(S):
                    a.wait_ge(s_pre[s], n + 1)
                    a.activation(act[s][:], ps[:, s, 128:256], ACT.Relu).then_inc(s_act[s], 1)

            with a.Fori(0, NB) as d:
                a.activation(a3.q[0:B, :], a3.q_all[:, bass.ds(d, 1), :].rearrange("p a k -> p (a k)"),
                             ACT.Copy).then_inc(s_q, 1)
                tiles(a, d, steps)
                a.wait_ge(s_blk, d + 1)
                a.activation(a3.agg_t[:, bass.ds(d * B, B)], ps[:, 4, 0:B], ACT.Copy).then_inc(s_out, 1)
                a.wait_ge(s_out, d + 1)


def update_phase(nc, g, io, a3, out):
    with Phase(nc, "upd") as ph:
        mw2 = ph.sb("mw2", [D, D])
        mw2_t = ph.sb("mw2_t", [D, D])
        mb2 = ph.sb("mb2", [D, 1])
        uw1 = ph.sb("uw1", [D, 2, D])
        ub1 = ph.sb("ub1", [D, 1])
        uw2 = ph.sb("uw2", [D, D])
        ub2 = ph.sb("ub2", [B, D])
        joined = ph.sb("joined", [D, D])
        bias = ph.sb("bias", [B, D])
        diag = [ph.sb(f"diag{i}", [B, 4, B]) for i in range(2)]
        u = [ph.sb(f"u{i}", [D, 4 * B]) for i in range(2)]
        ps = ph.ps()
        s_in = ph.sem("in")
        s_t = ph.sem("t")
        s_tc = ph.sem("tc")
        s_j = ph.sem("j")
        s_jc = ph.sem("jc")
        s_diag = ph.sem("diag")
        s_u = ph.sem("u")
        s_uc = ph.sem("uc")
        s_o = ph.sem("o")
        s_oc = ph.sem("oc")
        s_x = ph.sem("x")
        s_out = ph.sem("out")
        block = ph.ctx.enter_context(nc.Block())

        @block.sync
        def _(sp):
            sp.dma_start(mw2[:], io["mw2"]).then_inc(s_in, 16)
            sp.dma_start(mb2[:], io["mb2"].rearrange("(k a) -> k a", a=1)).then_inc(s_in, 16)
            sp.dma_start(uw1[:], io["uw1"].rearrange("(a p) k -> p a k", p=D)).then_inc(s_in, 16)
            sp.dma_start(ub1[:], io["ub1"].rearrange("(k a) -> k a", a=1)).then_inc(s_in, 16)
            sp.dma_start(uw2[:], io["uw2"]).then_inc(s_in, 16)
            sp.dma_start(ub2[:], io["ub2"].rearrange("(a k) -> a k", a=1).to_broadcast([B, D])).then_inc(s_in, 16)
            sp.wait_ge(s_x, 1)
            sp.dma_start(out.rearrange("(b p) d -> p b d", p=B), g.x[:]).then_inc(s_out, 16)
            sp.wait_ge(s_out, 16)

        @block.tensor
        def _(pe):
            pe.wait_ge(s_in, 96)
            pe.transpose(ps[:, 6, 0:D], mw2[:], g.ident[:]).then_inc(s_t, 1)
            pe.wait_ge(s_tc, 1)
            pe.matmul(ps[:, 6, 0:D], mw2_t[:], uw1[:, 1, :], start=True, stop=True)
            pe.matmul(ps[0:B, 7, 0:D], mb2[:].to_broadcast([D, B]), uw1[:, 1, :], start=True, stop=True).then_inc(s_j, 1)
            pe.wait_ge(s_jc, 1)
            for k, (b0, n) in enumerate(GROUPS):
                at = slice(b0 * B, (b0 + n) * B)
                p = k % 2
                if k >= 2:
                    pe.wait_ge(s_uc, k - 1)
                pe.matmul(ps[:, p, 0:n * B], uw1[:, 0, :], a3.h_t[:, at], start=True, stop=False)
                pe.matmul(ps[:, p, 0:n * B], joined[:], a3.agg_t[:, at], start=False, stop=False)
                pe.wait_ge(s_diag, k + 1)
                pe.matmul(ps[:, p, 0:n * B], bias[:], diag[p][:, 0:n, :].rearrange("p a k -> p (a k)"), start=False,
                          stop=True).then_inc(s_u, 1)
                pe.wait_ge(s_uc, k + 1)
                if k >= 2:
                    pe.wait_ge(s_oc, k - 1)
                for j in range(n):
                    last = pe.matmul(ps[0:B, 2 + p, j * D:(j + 1) * D], u[p][:, j * B:(j + 1) * B], uw2[:],
                                     start=True, stop=True)
                last.then_inc(s_o, 1)

        @block.scalar
        def _(a):
            a.wait_ge(s_in, 96)
            for k, (b0, n) in enumerate(GROUPS):
                a.wait_ge(s_u, k + 1)
                if k >= 2:
                    a.wait_ge(s_o, k - 1)
                a.activation(u[k % 2][:, 0:n * B], ps[:, k % 2, 0:n * B], ACT.Relu, bias=ub1[:]).then_inc(s_uc, 1)

        @block.vector
        def _(v):
            v.wait_ge(s_t, 1)
            v.tensor_copy(mw2_t[:], ps[:, 6, 0:D]).then_inc(s_tc, 1)
            v.wait_ge(s_j, 1)
            v.tensor_copy(joined[:], ps[:, 6, 0:D])
            v.tensor_copy(bias[:], ps[0:B, 7, 0:D]).then_inc(s_jc, 1)
            v.wait_ge(s_in, 96)
            v.tensor_tensor(g.x[:], g.x[:], g.h[:, :, 0:D], ALU.add).then_inc(s_tc, 1)
            v.wait_ge(s_tc, 2)
            v.tensor_tensor(g.x[:], g.x[:], ub2[:].unsqueeze(1).to_broadcast([B, NB, D]), ALU.add).then_inc(s_tc, 1)
            v.wait_ge(s_tc, 3)

            def diagonals(k):
                b0, n = GROUPS[k]
                if k >= 2:
                    v.wait_ge(s_u, k - 1)
                for j in range(n):
                    last = v.tensor_scalar(diag[k % 2][:, j, :], g.ident[0:B, 0:B], g.deg[:, b0 + j:b0 + j + 1], None,
                                           ALU.mult)
                last.then_inc(s_diag, 1)

            diagonals(0)
            for k, (b0, n) in enumerate(GROUPS):
                if k + 1 < len(GROUPS):
                    diagonals(k + 1)
                v.wait_ge(s_o, k + 1)
                v.tensor_tensor(g.x[:, b0:b0 + n, :], g.x[:, b0:b0 + n, :],
                                ps[0:B, 2 + k % 2, 0:n * D].rearrange("p (a k) -> p a k", k=D),
                                ALU.add).then_inc(s_oc, 1)
            v.wait_ge(s_oc, len(GROUPS))
            v.sem_inc(s_x, 1)


def load_phase(nc, name, pairs):
    with Phase(nc, name) as ph:
        s_in = ph.sem("in")
        block = ph.ctx.enter_context(nc.Block())

        @block.sync
        def _(sp):
            for out, in_ in pairs:
                sp.dma_start(out, in_).then_inc(s_in, 16)
            sp.wait_ge(s_in, 16 * len(pairs))


def layers(nc, g, dr, io, out):
    with ExitStack() as ctx:
        def sb(name, shape, dt=F32):
            return ctx.enter_context(nc.sbuf_tensor(name, shape, dt))

        w = Obj()
        w.m = sb("w_m", [D, 2, 3 * D])
        w.whh_t = sb("w_whh_t", [D, 3 * D])
        w.brow = sb("w_brow", [1, 3 * D])
        w.bhh = sb("w_bhh", [1, 3 * D])
        w.alpha = sb("w_alpha", [B, 4])
        w.tmp = sb("w_tmp", [B, 2])
        w.r_src = sb("w_r_src", [B, NB])
        w.r_dst = sb("w_r_dst", [B, NB])
        w.pos = sb("w_pos", [B, NB])
        w.neg = sb("w_neg", [B, NB])
        y = sb("y", [B, NB, D])
        weights_phase(nc, g, io, w)
        spmm_t_phase(nc, g, dr, "back", g.h, y, w.r_src[:], None)
        gru_phase(nc, g, w, y)
        norm_phase(nc, g, "norm1")
        with Phase(nc, "alpha0") as ph:
            block = ph.ctx.enter_context(nc.Block())

            @block.vector
            def _(v):
                v.scalar_tensor_tensor(g.x[:], g.h[:, :, 0:D], w.alpha[:, 0:1], g.x[:], ALU.mult, ALU.add)
        for k in range(1, 4):
            spmm_t_phase(nc, g, dr, f"hop{k}", g.h if k == 1 else y, y, None, w.alpha[:, k:k + 1])
        norm_phase(nc, g, "norm2")
    with ExitStack() as ctx:
        def sb(name, shape, dt=F32):
            return ctx.enter_context(nc.sbuf_tensor(name, shape, dt))

        a2 = Obj()
        a2.ks = sb("a_ks", [B, NB, HEADS * D])
        a2.qs_t = sb("a_qs_t", [D, HEADS, N])
        a2.rden = sb("a_rden", [B, NB * HEADS])
        a2.t = sb("a_t", [B, NB, HEADS * D + 1])
        a2.kv = sb("a_kv", [D, HEADS * D])
        a2.vsum = sb("a_vsum", [1, HEADS * D])
        a2.half_inv = sb("a_half_inv", [B, NB])
        a2.most = sb("a_most", [B, 1])
        a2.nparts = sb("a_nparts", [1, 1], I32)
        query_key_phase(nc, g, io, a2)
        a2.xp = sb("a_xp", [B, NB, 3, HEADS * D + 1], BF16)
        a2.y = g.n1[:, :, 0:D]
        a2.wo = sb("a_wo", [D, HEADS * (ORDER + 1), D])
        a2.wob = sb("a_wob", [B, D])
        parts_flag_phase(nc, g, a2)
        load_phase(nc, "loadwo", [(a2.wo[:], io["Wo_w"].rearrange("(t p) k -> p t k", p=D)),
                                  (a2.wob[:], io["Wo_b"].rearrange("(a k) -> a k", a=1).to_broadcast([B, D]))])
        for k in range(ORDER):
            term_phase(nc, g, a2, k, False)
            count_phase(nc, g, dr, a2, k)
            combine_phase(nc, g, a2, k)
        term_phase(nc, g, a2, ORDER, True)
        norm_phase(nc, g, "norm3")
    with ExitStack() as ctx:
        def sb(name, shape, dt=F32):
            return ctx.enter_context(nc.sbuf_tensor(name, shape, dt))

        a3 = Obj()
        a3.h_t = sb("m_h_t", [D, N])
        a3.agg_t = sb("m_agg_t", [D, N])
        a3.q_all = sb("m_q_all", [B, NB, D])
        a3.q = sb("m_q", [B + 1, D])
        message_table_phase(nc, g, dr, io, a3)
        edge_phase(nc, g, dr, a3)
        update_phase(nc, g, io, a3, out)


_INS = {'x': 'x', 'src': 'src', 'dst': 'dst', 'edge_weight': 'w', 'edge_weight1': 'ea', 'L0_gnn_W1': 'W1',
        'L0_gnn_W2': 'W2', 'L0_gnn_w_ih': 'w_ih', 'L0_gnn_w_hh': 'w_hh', 'L0_gnn_b_ih': 'b_ih',
        'L0_gnn_b_hh': 'b_hh', 'L1_gnn_alpha_logits': 'alpha', 'L2_gnn_Wq_w': 'Wq_w', 'L2_gnn_Wq_b': 'Wq_b',
        'L2_gnn_Wk_w': 'Wk_w', 'L2_gnn_Wk_b': 'Wk_b', 'L2_gnn_Wo_w': 'Wo_w', 'L2_gnn_Wo_b': 'Wo_b',
        'L3_gnn_msg_w1': 'mw1', 'L3_gnn_msg_b1': 'mb1', 'L3_gnn_msg_w2': 'mw2', 'L3_gnn_msg_b2': 'mb2',
        'L3_gnn_upd_w1': 'uw1', 'L3_gnn_upd_b1': 'ub1', 'L3_gnn_upd_w2': 'uw2', 'L3_gnn_upd_b2': 'ub2'}


def kernel(**inputs):
    import numpy as np
    import concourse.bacc as bacc
    from concourse.bass_utils import run_bass_kernel_spmd
    nc = bacc.Bacc("TRN2", target_bir_lowering=False, num_devices=1)
    arrays, io = {}, {}
    for name, short in _INS.items():
        a = np.ascontiguousarray(inputs[name])
        if name == 'edge_weight1':
            a = a.reshape(-1)
        arrays[name + "_dram"] = a
        io[short] = nc.dram_tensor(name + "_dram", a.shape, mybir.dt.from_np(a.dtype), kind="ExternalInput").ap()
    out = nc.dram_tensor("out_dram", (N, D), F32, kind="ExternalOutput").ap()
    program(nc, io, out)
    r = run_bass_kernel_spmd(nc, [arrays], core_ids=[0])
    return r.results[0]["out_dram"]
```

```python
import concourse.bass as bass
from concourse import mybir
from contextlib import ExitStack

F32 = mybir.dt.float32
F16 = mybir.dt.float16
BF16 = mybir.dt.bfloat16
I32 = mybir.dt.int32
ALU = mybir.AluOpType
ACT = mybir.ActivationFunctionType
AX = mybir.AxisListType

N = 3125
E = 100000
D = 128
B = 125
NB = N // B
WIN = 25
WPB = B // WIN
NW = N // WIN
TE = 128
CT = 7
NT = CT * 128
PAD = 4000
FAR = 100000.0
KW = WIN * NB
KEVEN = KW + 1
HEADS = 2
ORDER = 4
EPS = 1e-5
CHUNKS = [(c, min(512, N - c)) for c in range(0, N, 512)]
GROUPS = [(g, min(4, NB - g)) for g in range(0, NB, 4)]


class Counter:

    def __init__(self, eng):
        self.eng = eng
        self.reg = eng.alloc_register()
        eng.reg_mov(self.reg, 0)

    def next(self):
        self.eng.reg_add(self.reg, self.reg, 1)
        return self.eng.snap(self.reg)


class Chain:

    def __init__(self, eng, sem):
        self.eng, self.sem, self.n = eng, sem, 0

    def __call__(self, ins):
        self.n += 1
        ins.then_inc(self.sem, 1)
        self.eng.wait_ge(self.sem, self.n)


class Phase:

    used = []

    def __init__(self, nc, name):
        self.nc, self.name, self.ctx, self.sems = nc, name, ExitStack(), []

    def __enter__(self):
        self.ctx.__enter__()
        return self

    def __exit__(self, *a):
        done = self.ctx.__exit__(*a)
        self.used.extend(self.sems)
        if len(self.used) > 80:
            self.nc.clear_and_free_semaphores(list(self.used))
            self.nc.all_engine_barrier()
            self.used.clear()
        return done

    def sb(self, name, shape, dt=F32):
        return self.ctx.enter_context(self.nc.sbuf_tensor(f"{self.name}_{name}", shape, dt))

    def ps(self, name="ps"):
        return self.ctx.enter_context(self.nc.psum_tensor(f"{self.name}_{name}", [128, 8, 512], F32))

    def sem(self, name):
        sem = self.nc.alloc_semaphore(f"{self.name}_{name}")
        self.sems.append(sem)
        return sem


def bc(ap, n):
    return ap.unsqueeze(2).to_broadcast([ap.shape[0], ap.shape[1], n])


class Ahead:

    def __init__(self, eng, g, at):
        self.eng = eng
        self.regs = [eng.alloc_register(name=f"ahead{at}_{i}") for i in range(2)]
        self.keep(*tile_range(eng, g, at))

    def keep(self, lo, hi):
        for r, val in zip(self.regs, (lo, hi)):
            self.eng.reg_mov(r, val)

    def range(self):
        return [self.eng.snap(r, min_val=0, max_val=E // TE + 1) for r in self.regs]


def tile_range(eng, g, at):
    lo = eng.value_load(g.bounds[0:1, bass.ds(at, 1)], min_val=0, max_val=E // TE + 1)
    hi = eng.value_load(g.bounds[0:1, bass.ds(at + 128, 1)], min_val=0, max_val=E // TE + 1)
    return lo, hi


def setup_phase(nc, g, io):
    with Phase(nc, "setup") as ph:
        raw = [ph.sb(f"raw{i}", [128, CT, 128], dt) for i, dt in enumerate((I32, I32, F32, F32))]
        dst_q = ph.sb("dst_q", [128, CT, 128])
        src_q = ph.sb("src_q", [128, CT, 128])
        src_t = ph.sb("src_t", [128, NT])
        w_t = ph.sb("w_t", [128, NT])
        t1 = ph.sb("t1", [128, NT])
        ti = ph.sb("ti", [128, NT], I32)
        tb = ph.sb("tb", [128, NT], BF16)
        mx = ph.sb("mx", [128, 2, CT])
        diag = ph.sb("diag", [128, 2, CT, 128])
        ones = ph.sb("ones", [128, 128])
        mxb = ph.sb("mxb", [128, 2, NT])
        pid = ph.sb("pid", [128, NT])
        thr = ph.sb("thr", [128, 4])
        pt = ph.sb("pt", [128, NT])
        lim = ph.sb("lim", [128, 4])
        ps = ph.ps()
        s_pad = ph.sem("pad")
        s_in = ph.sem("in")
        s_x = ph.sem("x")
        s_const = ph.sem("const")
        s_f = ph.sem("f")
        s_tr = ph.sem("tr")
        s_diag = ph.sem("diag")
        s_copied = ph.sem("copied")
        s_bc = ph.sem("bc")
        s_lim = ph.sem("lim")
        s_row = ph.sem("row")
        s_d = ph.sem("d")
        block = ph.ctx.enter_context(nc.Block())
        full = E // TE
        rows, tail = full - 128 * (CT - 1), E - full * TE

        @block.sync
        def _(sp):
            sp.wait_ge(s_pad, 4)
            for r, a in zip(raw, (io["dst"], io["src"], io["w"], io["ea"])):
                sp.dma_start(r[:, 0:CT - 1, :],
                             a[0:128 * (CT - 1) * TE].rearrange("(c q p) -> q c p", q=128, p=TE)).then_inc(s_in, 16)
                sp.dma_start(r[0:rows, CT - 1, :],
                             a[128 * (CT - 1) * TE:full * TE].rearrange("(q p) -> q p", p=TE)).then_inc(s_in, 16)
                sp.dma_start(r[rows:rows + 1, CT - 1, 0:tail],
                             a[full * TE:E].rearrange("(q p) -> q p", q=1)).then_inc(s_in, 16)
            sp.dma_start(g.x[:], io["x"].rearrange("(b p) d -> p b d", p=B)).then_inc(s_x, 16)
            sp.wait_ge(s_x, 16)

        @block.gpsimd
        def _(pool):
            pool.memset(raw[0][:], PAD).then_inc(s_pad, 1)
            for r in raw[1:]:
                pool.memset(r[:], 0).then_inc(s_pad, 1)
            pool.memset(g.ident[:], 0.0).then_inc(s_const, 1)
            pool.wait_ge(s_const, 1)
            pool.affine_select(out=g.ident[:], in_=g.ident[:], compare_op=ALU.not_equal, fill=1.0, base=0,
                               pattern=[[-1, 128]], channel_multiplier=1).then_inc(s_const, 1)
            pool.iota(g.key_id[:], [[1, KEVEN]], base=0, channel_multiplier=0,
                      allow_small_or_imprecise_dtypes=True).then_inc(s_const, 1)
            pool.iota(pid[:], [[1, NT]], base=0, channel_multiplier=0,
                      allow_small_or_imprecise_dtypes=True).then_inc(s_const, 1)
            for i, (base, step) in enumerate(((0, WIN), (WIN - 1, WIN), (0, B), (B - 1, B))):
                pool.iota(thr[:, i:i + 1], [[0, 1]], base=base, channel_multiplier=step,
                          allow_small_or_imprecise_dtypes=True).then_inc(s_const, 1)
            pool.iota(g.win_base[:], [[-KW, NW]], base=0, channel_multiplier=0,
                      allow_small_or_imprecise_dtypes=True)
            pool.iota(g.block_base[:], [[-B, NB]], base=0, channel_multiplier=0,
                      allow_small_or_imprecise_dtypes=True)
            pool.memset(ones[:], 1.0).then_inc(s_const, 1)
            pool.memset(g.h[:, :, D:D + 1], 1.0).then_inc(s_const, 1)

        @block.tensor
        def _(pe):
            pe.wait_ge(s_const, 10)
            pe.wait_ge(s_in, 192)
            pe.wait_ge(s_f, 2)
            for i, a in enumerate((dst_q, src_q, raw[2], raw[3])):
                for c in range(CT):
                    last = pe.transpose(ps[:, 2 * i + c // 4, (c % 4) * 128:(c % 4) * 128 + 128], a[:, c, :], g.ident[:])
                last.then_inc(s_tr, 1)
            pe.wait_ge(s_diag, 2)
            pe.wait_ge(s_copied, 1)
            for i in range(2):
                for c in range(CT):
                    last = pe.matmul(ps[:, 2 * i + c // 4, (c % 4) * 128:(c % 4) * 128 + 128], ones[:],
                                     diag[:, i, c, :], start=True, stop=True)
            last.then_inc(s_bc, 1)
            pe.wait_ge(s_lim, 1)
            for i in range(4):
                last = pe.transpose(ps[0:1, 4, i * 128:(i + 1) * 128], lim[:, i:i + 1], g.ident[:])
            last.then_inc(s_row, 1)

        @block.vector
        def _(v):
            do = Chain(v, s_d)
            v.wait_ge(s_in, 192)
            v.tensor_copy(dst_q[:], raw[0][:]).then_inc(s_f, 1)
            v.tensor_copy(src_q[:], raw[1][:]).then_inc(s_f, 1)
            v.wait_ge(s_f, 2)
            v.tensor_reduce(mx[:, 0, :], dst_q[:], AX.X, ALU.max)
            do(v.tensor_reduce(mx[:, 1, :], dst_q[:], AX.X, ALU.min))
            v.wait_ge(s_const, 10)
            for i in range(2):
                for c in range(CT):
                    last = v.tensor_scalar(diag[:, i, c, :], g.ident[:], mx[:, i, c:c + 1], None, ALU.mult)
                last.then_inc(s_diag, 1)
            v.wait_ge(s_tr, 4)
            for i, a in enumerate((g.dst, src_t, w_t, g.ea)):
                v.tensor_copy(a[:, 0:512], ps[:, 2 * i, :])
                last = v.tensor_copy(a[:, 512:NT], ps[:, 2 * i + 1, 0:NT - 512])
            last.then_inc(s_copied, 1)
            v.wait_ge(s_copied, 1)
            blk, lane = g.key, g.lane
            do(v.tensor_scalar(ti[:], src_t[:], 1.0 / B, None, ALU.mult))
            do(v.tensor_copy(blk[:], ti[:]))
            do(v.scalar_tensor_tensor(lane[:], blk[:], -float(B), src_t[:], ALU.mult, ALU.add))
            do(v.tensor_scalar(t1[:], lane[:], 0.0, None, ALU.is_lt))
            do(v.tensor_tensor(blk[:], blk[:], t1[:], ALU.subtract))
            do(v.scalar_tensor_tensor(lane[:], t1[:], float(B), lane[:], ALU.mult, ALU.add))
            do(v.tensor_scalar(t1[:], lane[:], float(B), None, ALU.is_ge))
            do(v.tensor_tensor(blk[:], blk[:], t1[:], ALU.add))
            do(v.scalar_tensor_tensor(lane[:], t1[:], -float(B), lane[:], ALU.mult, ALU.add))
            do(v.scalar_tensor_tensor(g.key[:], g.dst[:], float(NB), blk[:], ALU.mult, ALU.add))
            do(v.tensor_copy(g.src_idx[:], src_t[:]))
            for i in range(3):
                do(v.tensor_copy(tb[:], w_t[:]))
                do(v.tensor_copy(g.wpart[i][:], tb[:]))
                if i < 2:
                    do(v.tensor_tensor(w_t[:], w_t[:], g.wpart[i][:], ALU.subtract))
            v.wait_ge(s_bc, 1)
            for i in range(2):
                v.tensor_copy(mxb[:, i, 0:512], ps[:, 2 * i, :])
                last = v.tensor_copy(mxb[:, i, 512:NT], ps[:, 2 * i + 1, 0:NT - 512])
            do(last)
            for k in range(2):
                do(v.tensor_scalar(pt[:], mxb[:, 0, :], thr[:, 2 * k:2 * k + 1], FAR, ALU.is_lt, ALU.mult))
                do(v.tensor_tensor(pt[:], pt[:], pid[:], ALU.add))
                do(v.tensor_reduce(lim[:, 2 * k:2 * k + 1], pt[:], AX.X, ALU.min))
                do(v.tensor_scalar(pt[:], mxb[:, 1, :], thr[:, 2 * k + 1:2 * k + 2], -FAR, ALU.is_gt, ALU.mult))
                do(v.tensor_tensor(pt[:], pt[:], pid[:], ALU.add))
                do(v.tensor_reduce(lim[:, 2 * k + 1:2 * k + 2], pt[:], AX.X, ALU.max))
                do(v.tensor_scalar(lim[:, 2 * k + 1:2 * k + 2], lim[:, 2 * k + 1:2 * k + 2], 1.0, 0.0,
                                   ALU.add, ALU.max))
            v.memset(t1[:, 0:1], 0.0).then_inc(s_lim, 1)
            v.wait_ge(s_row, 1)
            v.tensor_copy(g.bounds[:], ps[0:1, 4, :])


def norm_phase(nc, g, name):
    with Phase(nc, name) as ph:
        xc = ph.sb("xc", [B, NB, D])
        sq = ph.sb("sq", [B, NB, D])
        m = ph.sb("m", [B, NB])
        r = ph.sb("r", [B, NB])
        s_v = ph.sem("v")
        s_sd = ph.sem("sd")
        s_h = ph.sem("h")
        s_d = ph.sem("d")
        block = ph.ctx.enter_context(nc.Block())

        @block.vector
        def _(v):
            do = Chain(v, s_d)
            do(v.tensor_reduce(m[:], g.x[:], AX.X, ALU.add))
            do(v.tensor_scalar(m[:], m[:], 1.0 / D, None, ALU.mult))
            do(v.tensor_tensor(xc[:], g.x[:], bc(m[:], D), ALU.subtract))
            do(v.tensor_tensor(sq[:], xc[:], xc[:], ALU.mult))
            do(v.tensor_reduce(r[:], sq[:], AX.X, ALU.add))
            v.tensor_scalar(r[:], r[:], 1.0 / D, EPS, ALU.mult, ALU.add).then_inc(s_v, 1)
            v.wait_ge(s_sd, 1)
            do(v.reciprocal(m[:], r[:]))
            v.tensor_tensor(sq[:], xc[:], bc(m[:], D), ALU.mult).then_inc(s_h, 1)

        @block.scalar
        def _(a):
            a.wait_ge(s_v, 1)
            a.activation(r[:], r[:], ACT.Sqrt).then_inc(s_sd, 1)
            a.wait_ge(s_h, 1)
            a.activation(g.h[:, :, 0:D], sq[:], ACT.Relu)


def build_phase(nc, g, dr):
    with Phase(nc, "build") as ph:
        left = [ph.sb(f"left{s}", [128, 4, 128], BF16) for s in range(2)]
        right = [ph.sb(f"right{s}", [128, KEVEN], BF16) for s in range(2)]
        stage = [ph.sb(f"stage{j}", [B, 2, WIN, NB]) for j in range(WPB)]
        adj = ph.sb("adj", [B, NB, B])
        cnt = [ph.sb(f"cnt{i}", [B, NB, B], BF16) for i in range(2)]
        adj_t = ph.sb("adj_t", [B, N])
        rowsum = ph.sb("rowsum", [B, NB])
        ps = ph.ps()
        s_lane = [ph.sem(f"lane{s}") for s in range(2)]
        s_ready = [ph.sem(f"ready{s}") for s in range(2)]
        s_scaled = [ph.sem(f"scaled{s}") for s in range(2)]
        s_half = [ph.sem(f"half{s}") for s in range(2)]
        s_free = [ph.sem(f"free{s}") for s in range(2)]
        s_staged = ph.sem("staged")
        s_unstaged = ph.sem("unstaged")
        s_pool = ph.sem("pool")
        s_adj = ph.sem("adj")
        s_tr = ph.sem("tr")
        s_trc = ph.sem("trc")
        s_n1 = ph.sem("n1")
        s_n1c = ph.sem("n1c")
        s_sum = ph.sem("sum")
        s_sumadd = ph.sem("sumadd")
        s_adjout = ph.sem("adjout")
        s_cntout = ph.sem("cntout")
        s_tick = ph.sem("tick")
        block = ph.ctx.enter_context(nc.Block())
        NG = len(GROUPS)
        COUNT = 3
        FINISH = 2
        PIECES = [[(0, 0, 500), (1, 0, KW - 500)], [(1, KW - 500, 500), (2, 0, 2 * KW - 1000)]]

        def windows(eng, step, between, d, ahead, parity=0):
            lo, hi = ahead.range()
            for j in range(WPB):
                w = d * WPB + j
                step(lo, w, j, True)
                between(w, j)
                lo_next, hi_next = tile_range(eng, g, w + 1)
                with eng.Fori(lo + 2, hi, 2) as t:
                    step(t, w, j, False)
                lo, hi = lo_next, hi_next
            ahead.keep(lo, hi)

        @block.vector
        def _(v):
            rounds = Counter(v)
            ahead = Ahead(v, g, 0)

            def factors(t, w, j, first):
                n = rounds.next()
                for s in range(2):
                    at = bass.ds(t + s, 1)
                    v.wait_ge(s_half[s], n)
                    v.tensor_scalar(left[s][:, COUNT, :], g.key_id[:, 0:128], g.lane[:, at], None,
                                    ALU.is_equal).then_inc(s_lane[s], 1)
                    v.tensor_scalar(left[s][:, 0, :], g.key_id[:, 0:128], g.lane[:, at], g.wpart[0][:, at],
                                    ALU.is_equal, ALU.mult)
                    v.wait_ge(s_free[s], n)
                    v.tensor_scalar(right[s][:], g.key_id[:], g.key[:, at], g.win_base[:, bass.ds(w, 1)],
                                    ALU.subtract, ALU.is_equal).then_inc(s_ready[s], 1)

            def row_sums(d):
                v.wait_ge(s_adj, d + 1)
                v.wait_ge(s_sumadd, d + 1)
                v.tensor_reduce(rowsum[:], adj[:], AX.X, ALU.add).then_inc(s_sum, 1)
                v.wait_ge(s_sum, d + 1)
                v.tensor_tensor(g.wsum_src[:], g.wsum_src[:], rowsum[:], ALU.add).then_inc(s_sumadd, 1)

            v.memset(g.wsum_src[:], 0.0).then_inc(s_sumadd, 1)
            windows(v, factors, lambda w, j: None, 0, ahead)
            with v.Fori(1, NB) as d:
                def between(w, j):
                    if j == FINISH:
                        row_sums(d - 1)
                windows(v, factors, between, d, ahead)
            row_sums(NB - 1)

        @block.tensor
        def _(pe):
            rounds = Counter(pe)
            ahead = Ahead(pe, g, 0)
            for s in range(2):
                pe.sem_inc(s_half[s], 1)
                pe.sem_inc(s_free[s], 1)

            def products(bank, start):
                n = rounds.next()
                for s in range(2):
                    pe.wait_ge(s_ready[s], n)
                    pe.wait_ge(s_scaled[s], n)
                    for k in (0, COUNT, 1, 2):
                        col = 0
                        for off, c0, c1 in PIECES[k == COUNT]:
                            opens = start and s == 0 and ((k == 0) or (off == 2))
                            last = pe.matmul(ps[0:B, bank + off, c0:c1], left[s][:, k, 0:B],
                                             right[s][:, col:col + c1 - c0], start=opens, stop=False,
                                             skip_group_check=True)
                            col += c1 - c0
                        if k == COUNT:
                            last.then_inc(s_half[s], 1)
                    last.then_inc(s_free[s], 1)

            def finish(d):
                pe.wait_ge(s_adj, d + 1)
                pe.wait_ge(s_n1c, d + 1)
                for i, (b0, n) in enumerate(GROUPS):
                    if i >= 2:
                        pe.wait_ge(s_trc, d * NG + (i - 1))
                    for k in range(n):
                        last = pe.transpose(ps[0:B, 6 + i % 2, k * B:(k + 1) * B], adj[:, b0 + k, :], g.ident[0:B, 0:B])
                    last.then_inc(s_tr, 1)
                pe.wait_ge(s_trc, d * NG + (NG - 1))
                for k in range(NB):
                    last = pe.matmul(ps[0:B, 7, 0:D + 1], adj[:, k, :], g.h[:, k, :], start=k == 0, stop=k == NB - 1)
                last.then_inc(s_n1, 1)

            def block_of(d, parity):
                def step(t, w, j, first):
                    if first and (j == FINISH) and parity is not None:
                        finish(d - 1)
                    if first and (parity is not None or j >= 2):
                        pe.wait_ge(s_staged, w - 1)
                    products(3 * ((j + (parity or 0)) % 2), first)

                windows(pe, step, lambda w, j: None, d, ahead)

            block_of(0, None)
            with pe.Fori(0, NB // 2) as pair:
                d = pair * 2 + 1
                block_of(d, 1)
                block_of(d + 1, 0)
            finish(NB - 1)

        @block.scalar
        def _(a):
            rounds = Counter(a)
            ahead = Ahead(a, g, 0)
            a.sem_inc(s_n1c, 1)

            def scaled(t, w, j, first):
                n = rounds.next()
                for s in range(2):
                    at = bass.ds(t + s, 1)
                    a.wait_ge(s_lane[s], n)
                    a.wait_ge(s_free[s], n)
                    a.activation(left[s][:, 1, :], left[s][:, COUNT, :], ACT.Copy, scale=g.wpart[1][:, at])
                    a.activation(left[s][:, 2, :], left[s][:, COUNT, :], ACT.Copy,
                                 scale=g.wpart[2][:, at]).then_inc(s_scaled[s], 1)

            def staged(w, j, parity, reuse, rounds_done):
                a.wait_ge(s_free[1], rounds_done)
                if reuse:
                    a.wait_ge(s_unstaged, w - (WPB - 2))
                flat = stage[j][:].rearrange("p a k h -> p (a k h)")
                bank = 3 * ((j + parity) % 2)
                for i in range(2):
                    col = i * KW
                    for k, (off, c0, c1) in enumerate(PIECES[i]):
                        sums = {"accum_out": g.winsum[:, bass.ds(w * 2 + k, 1)]} if i else {}
                        last = a.activation(flat[:, col:col + c1 - c0], ps[0:B, bank + off, c0:c1], ACT.Copy, **sums)
                        col += c1 - c0
                last.then_inc(s_staged, 1)

            def finish(d):
                a.wait_ge(s_adjout, d * 16 + 1)
                for i, (b0, n) in enumerate(GROUPS):
                    a.wait_ge(s_tr, d * NG + (i + 1))
                    a.activation(adj_t[:, b0 * B:(b0 + n) * B], ps[0:B, 6 + i % 2, 0:n * B], ACT.Copy).then_inc(s_trc, 1)
                a.wait_ge(s_n1, d + 1)
                a.activation(g.n1[:, bass.ds(d, 1), :].rearrange("p a k -> p (a k)"), ps[0:B, 7, 0:D + 1],
                             ACT.Copy).then_inc(s_n1c, 1)

            def block_of(d, parity):
                def between(w, j):
                    done = a.snap(rounds.reg)
                    if j > 0:
                        staged(w - 1, j - 1, parity or 0, parity is not None, done)
                    elif parity is not None:
                        staged(w - 1, WPB - 1, 1 - parity, True, done)
                    if j == FINISH and parity is not None:
                        finish(d - 1)

                windows(a, scaled, between, d, ahead)

            block_of(0, None)
            with a.Fori(0, NB // 2) as pair:
                d = pair * 2 + 1
                block_of(d, 1)
                block_of(d + 1, 0)
            staged(NW - 1, WPB - 1, 0, True, rounds.next())
            finish(NB - 1)

        @block.gpsimd
        def _(pool):
            def unstage(w, j):
                pool.wait_ge(s_staged, w + 1)
                pool.sem_inc(s_tick, 1)
                cols = lambda t: t[:, :, j * WIN:(j + 1) * WIN].rearrange("p h k -> p k h")
                pool.tensor_copy(cols(cnt[0]), stage[j][:, 1, :, :]).then_inc(s_pool, 1)
                pool.tensor_copy(cols(adj), stage[j][:, 0, :, :])
                pool.wait_ge(s_pool, w + 1)
                pool.tensor_tensor(cols(cnt[1]), stage[j][:, 1, :, :], cols(cnt[0]), ALU.subtract).then_inc(s_unstaged, 1)

            def block_of(d, first):
                if not first:
                    pool.wait_ge(s_n1, d)
                    pool.wait_ge(s_sum, d)
                    pool.wait_ge(s_cntout, d * 32)
                for j in range(WPB):
                    unstage(d * WPB + j, j)
                pool.wait_ge(s_unstaged, d * WPB + (WPB + 1))
                pool.sem_inc(s_adj, 1)

            pool.sem_inc(s_unstaged, 1)
            block_of(0, True)
            with pool.Fori(1, NB) as d:
                block_of(d, False)

        @block.sync
        def _(sp):
            sp.sem_inc(s_adjout, 1)
            with sp.Fori(0, NB) as d:
                built, moved = sp.snap(d + 1), sp.snap(d * NG + NG)
                sp.wait_ge(s_adj, built)
                sp.sem_inc(s_tick, 1)
                for i in range(2):
                    sp.dma_start(dr.cnt[i, bass.ds(d, 1), :, :].rearrange("a p n -> p (a n)"),
                                 cnt[i][:].rearrange("p h k -> p (h k)")).then_inc(s_cntout, 16)
                sp.wait_ge(s_trc, moved)
                sp.sem_inc(s_tick, 1)
                sp.dma_start(dr.adj_t[bass.ds(d, 1), :, :].rearrange("a p n -> p (a n)"), adj_t[:]).then_inc(s_adjout, 16)
            sp.wait_ge(s_cntout, NB * 32)
            sp.wait_ge(s_adjout, NB * 16 + 1)


class Obj:
    pass


def program(nc, io, out):
    ctx = ExitStack()
    Phase.used.clear()
    with ctx:
        def sb(name, shape, dt=F32):
            return ctx.enter_context(nc.sbuf_tensor(name, shape, dt))

        g, dr = Obj(), Obj()
        dr.cnt = nc.dram_tensor("cnt_panels", (2, NB, B, N), BF16, kind="Internal").ap()
        dr.adj_t = nc.dram_tensor("adj_rows", (NB, B, N), F32, kind="Internal").ap()
        dr.table = nc.dram_tensor("src_table", (N, D), F32, kind="Internal").ap()
        g.x = sb("x", [B, NB, D])
        g.h = sb("h", [B, NB, D + 1])
        g.ident = sb("ident", [128, 128])
        g.dst = sb("dst", [128, NT])
        g.src_idx = sb("src_idx", [128, NT], I32)
        g.ea = sb("ea", [128, NT])
        g.block_base = sb("block_base", [128, NB])
        g.bounds = sb("bounds", [1, 512], I32)
        g.n1 = sb("n1", [B, NB, D + 1])
        g.wsum_src = sb("wsum_src", [B, NB])
        g.winsum = sb("winsum", [B, 2 * NW])
        g.deg = sb("deg", [B, NB])
        with ExitStack() as building:
            def sb2(name, shape, dt=F32):
                return building.enter_context(nc.sbuf_tensor(name, shape, dt))

            g.key_id = sb2("key_id", [128, KEVEN], F16)
            g.key = sb2("key", [128, NT])
            g.win_base = sb2("win_base", [128, NW])
            g.lane = sb2("lane", [128, NT])
            g.wpart = [sb2(f"wpart{i}", [128, NT]) for i in range(3)]
            setup_phase(nc, g, io)
            norm_phase(nc, g, "norm0")
            build_phase(nc, g, dr)
        layers(nc, g, dr, io, out)


def chunk_copies(eng_a, eng_v, k):
    return eng_a if k % 2 == 0 else eng_v


def spmm_t_phase(nc, g, dr, name, y_in, y_out, scale, alpha, src_scale=None):
    R = 5
    with Phase(nc, name) as ph:
        rows = [ph.sb(f"rows{i}", [B, N]) for i in range(R)]
        y_one = [ph.sb(f"y_one{i}", [B, D]) for i in range(R)]
        y_t = ph.sb("y_t", [D, N])
        ps = ph.ps()
        s_row = [ph.sem(f"row{i}") for i in range(R)]
        s_used = [ph.sem(f"used{i}") for i in range(R)]
        s_one = [ph.sem(f"one{i}") for i in range(R)]
        s_tick = ph.sem("tick")
        s_sum = ph.sem("sum")
        s_tc = [ph.sem(f"tc{i}") for i in range(2)]
        s_tr = ph.sem("tr")
        s_d = ph.sem("d")
        block = ph.ctx.enter_context(nc.Block())

        @block.sync
        def _(sp):
            def load(o, i):
                sp.dma_start(rows[i][:], dr.adj_t[bass.ds(o * R + i, 1), :, :].rearrange("a p n -> p (a n)")).then_inc(s_row[i], 16)

            for i in range(R):
                load(0, i)
            with sp.Fori(1, NB // R) as o:
                for i in range(R):
                    sp.wait_ge(s_used[i], sp.snap(o))
                    sp.sem_inc(s_tick, 1)
                    load(o, i)

        @block.scalar
        def _(a):
            def one(o, i):
                a.activation(y_one[i][:], y_in[:, bass.ds(o * R + i, 1), 0:D].rearrange("p a k -> p (a k)"),
                             ACT.Copy).then_inc(s_one[i], 1)

            for i in range(R):
                one(0, i)
            with a.Fori(1, NB // R) as o:
                for i in range(R):
                    a.wait_ge(s_used[i], a.snap(o))
                    one(o, i)
            a.wait_ge(s_sum, 1)
            for k, (c, n) in enumerate(CHUNKS):
                if k % 2 == 0:
                    a.activation(y_t[:, c:c + n], ps[:, k, 0:n], ACT.Copy).then_inc(s_tc[0], 1)

        @block.tensor
        def _(pe):
            def product(o, i, first):
                pe.wait_ge(s_row[i], o * 16 + 16)
                pe.wait_ge(s_one[i], o + 1)
                for k, (c, n) in enumerate(CHUNKS):
                    last = pe.matmul(ps[:, k, 0:n], y_one[i][:], rows[i][:, c:c + n], start=first, stop=False,
                                     skip_group_check=True)
                return last

            for i in range(R):
                product(0, i, i == 0).then_inc(s_used[i], 1)
            with pe.Fori(1, NB // R) as o:
                for i in range(R):
                    product(o, i, False).then_inc(s_used[i], 1)
            pe.drain().then_inc(s_sum, 1)
            pe.wait_ge(s_tc[0], 4)
            pe.wait_ge(s_tc[1], 3)
            for k, (b0, n) in enumerate(GROUPS):
                for j in range(n):
                    last = pe.transpose(ps[0:B, k, j * D:(j + 1) * D], y_t[:, (b0 + j) * B:(b0 + j + 1) * B], g.ident[:])
                last.then_inc(s_tr, 1)

        @block.vector
        def _(v):
            do = Chain(v, s_d)
            v.wait_ge(s_sum, 1)
            for k, (c, n) in enumerate(CHUNKS):
                if k % 2 == 1:
                    v.tensor_copy(y_t[:, c:c + n], ps[:, k, 0:n]).then_inc(s_tc[1], 1)
            for k, (b0, n) in enumerate(GROUPS):
                v.wait_ge(s_tr, k + 1)
                last = v.tensor_copy(y_out[:, b0:b0 + n, 0:D], ps[0:B, k, 0:n * D].rearrange("p (a k) -> p a k", k=D))
            do(last)
            if scale is not None:
                do(v.tensor_tensor(y_out[:, :, 0:D], y_out[:, :, 0:D], bc(scale, D), ALU.mult))
            if alpha is not None:
                do(v.scalar_tensor_tensor(g.x[:], y_out[:, :, 0:D], alpha, g.x[:], ALU.mult, ALU.add))


def transposed(pe, ps, bank, in_, ident, blocks, sem):
    for j, b in enumerate(blocks):
        last = pe.transpose(ps[:, bank, j * B:(j + 1) * B], in_(b), ident[0:B, 0:B])
    last.then_inc(sem, 1)


def weights_phase(nc, g, io, w):
    with Phase(nc, "gruw") as ph:
        w12 = [ph.sb(f"w{i}", [D, D]) for i in range(2)]
        wih = ph.sb("wih", [128, 3, 2 * D])
        whh = ph.sb("whh", [128, 3, D])
        wih_t = ph.sb("wih_t", [128, 2, 3 * D])
        bih = ph.sb("bih", [1, 3 * D])
        ps = ph.ps()
        s_in = ph.sem("in")
        s_tr = ph.sem("tr")
        s_c = ph.sem("c")
        s_m = ph.sem("m")
        s_d = ph.sem("d")
        block = ph.ctx.enter_context(nc.Block())

        @block.sync
        def _(sp):
            sp.dma_start(w12[0][:], io["W1"]).then_inc(s_in, 16)
            sp.dma_start(w12[1][:], io["W2"]).then_inc(s_in, 16)
            sp.dma_start(wih[:], io["w_ih"].rearrange("(t p) k -> p t k", p=128)).then_inc(s_in, 16)
            sp.dma_start(whh[:], io["w_hh"].rearrange("(t p) k -> p t k", p=128)).then_inc(s_in, 16)
            sp.dma_start(bih[:], io["b_ih"].rearrange("(a k) -> a k", a=1)).then_inc(s_in, 16)
            sp.dma_start(w.bhh[:], io["b_hh"].rearrange("(a k) -> a k", a=1)).then_inc(s_in, 16)
            sp.dma_start(w.alpha[:], io["alpha"].rearrange("(a k) -> a k", a=1).to_broadcast([B, 4])).then_inc(s_in, 16)

        @block.tensor
        def _(pe):
            pe.wait_ge(s_in, 112)
            for i in range(2):
                for t in range(3):
                    last = pe.transpose(ps[:, i, t * D:(t + 1) * D], wih[:, t, i * D:(i + 1) * D], g.ident[:])
                last.then_inc(s_tr, 1)
            for t in range(3):
                last = pe.transpose(ps[:, 2, t * D:(t + 1) * D], whh[:, t, :], g.ident[:])
            last.then_inc(s_tr, 1)
            pe.wait_ge(s_c, 3)
            for i in range(2):
                last = pe.matmul(ps[:, 3 + i, 0:3 * D], w12[i][:], wih_t[:, i, :], start=True, stop=True)
            last.then_inc(s_m, 1)

        @block.vector
        def _(v):
            v.wait_ge(s_tr, 3)
            for i in range(2):
                v.tensor_copy(wih_t[:, i, :], ps[:, i, 0:3 * D]).then_inc(s_c, 1)
            v.tensor_copy(w.whh_t[:], ps[:, 2, 0:3 * D]).then_inc(s_c, 1)
            do = Chain(v, s_d)
            do(v.tensor_tensor(w.brow[:, 0:2 * D], bih[:, 0:2 * D], w.bhh[:, 0:2 * D], ALU.add))
            do(v.tensor_copy(w.brow[:, 2 * D:3 * D], bih[:, 2 * D:3 * D]))
            v.wait_ge(s_m, 1)
            for i in range(2):
                v.tensor_copy(w.m[:, i, :], ps[:, 3 + i, 0:3 * D])
            do(v.tensor_reduce(w.tmp[:, 0:1], w.alpha[:], AX.X, ALU.max))
            v.tensor_scalar(w.alpha[:], w.alpha[:], w.tmp[:, 0:1], None, ALU.subtract).then_inc(s_c, 1)
            v.wait_ge(s_c, 5)
            do(v.tensor_reduce(w.tmp[:, 0:1], w.alpha[:], AX.X, ALU.add))
            do(v.reciprocal(w.tmp[:, 1:2], w.tmp[:, 0:1]))
            do(v.tensor_scalar(w.alpha[:], w.alpha[:], w.tmp[:, 1:2], None, ALU.mult))
            for sums, out in ((g.wsum_src[:], w.r_src[:]), (g.n1[:, :, D], w.r_dst[:])):
                do(v.tensor_scalar(w.pos[:], sums, 0.0, None, ALU.is_gt))
                do(v.tensor_tensor(out, sums, w.pos[:], ALU.mult))
                do(v.tensor_scalar(w.neg[:], w.pos[:], -1.0, 1.0, ALU.mult, ALU.add))
                do(v.tensor_tensor(out, out, w.neg[:], ALU.add))
                do(v.reciprocal(out, out))
                do(v.tensor_tensor(out, out, w.pos[:], ALU.mult))
            do(v.tensor_tensor(g.n1[:, :, 0:D], g.n1[:, :, 0:D], bc(w.r_dst[:], D), ALU.mult))

        @block.scalar
        def _(a):
            a.wait_ge(s_c, 4)
            a.activation(w.alpha[:], w.alpha[:], ACT.Exp).then_inc(s_c, 1)


def gru_phase(nc, g, w, n2):
    with Phase(nc, "gru") as ph:
        tr = [ph.sb(f"tr{i}", [D, N]) for i in range(3)]
        rz = ph.sb("rz", [B, NB, 2 * D])
        t = ph.sb("t", [B, NB, D])
        ones = ph.sb("ones", [1, B])
        ps = ph.ps()
        s_one = ph.sem("one")
        s_tr = ph.sem("tr")
        s_c = [ph.sem(f"c{i}") for i in range(2)]
        s_g = ph.sem("g")
        s_sig = ph.sem("sig")
        s_t = ph.sem("t")
        s_nn = ph.sem("nn")
        s_d = ph.sem("d")
        block = ph.ctx.enter_context(nc.Block())
        jobs = [(i, b0, n) for i in range(3) for b0, n in GROUPS]
        srcs = [g.n1, n2, g.h]
        even, odd = (len(jobs) + 1) // 2, len(jobs) // 2

        @block.tensor
        def _(pe):
            for k, (i, b0, n) in enumerate(jobs):
                if k >= 8:
                    pe.wait_ge(s_c[k % 2], (k - 8) // 2 + 1)
                transposed(pe, ps, k % 8, lambda b: srcs[i][:, b, 0:D], g.ident, range(b0, b0 + n), s_tr)
            pe.wait_ge(s_c[0], even)
            pe.wait_ge(s_c[1], odd)
            pe.wait_ge(s_one, 1)
            for b in range(NB):
                at = slice(b * B, (b + 1) * B)
                p, q = 2 * (b % 3), 2 * (b % 3) + 1
                if b >= 3:
                    pe.wait_ge(s_t, b - 2)
                pe.matmul(ps[0:B, p, 0:3 * D], tr[0][:, at], w.m[:, 0, :], start=True, stop=False)
                pe.matmul(ps[0:B, p, 0:3 * D], tr[1][:, at], w.m[:, 1, :], start=False, stop=False)
                pe.matmul(ps[0:B, p, 0:2 * D], tr[2][:, at], w.whh_t[:, 0:2 * D], start=False, stop=False)
                pe.matmul(ps[0:B, p, 0:3 * D], ones[:], w.brow[:], start=False, stop=True)
                pe.matmul(ps[0:B, q, 0:D], tr[2][:, at], w.whh_t[:, 2 * D:3 * D], start=True, stop=False)
                pe.matmul(ps[0:B, q, 0:D], ones[:], w.bhh[:, 2 * D:3 * D], start=False, stop=True).then_inc(s_g, 1)

        @block.scalar
        def _(a):
            for k, (i, b0, n) in enumerate(jobs):
                if k % 2 == 0:
                    a.wait_ge(s_tr, k + 1)
                    a.activation(tr[i][:, b0 * B:(b0 + n) * B], ps[:, k % 8, 0:n * B], ACT.Copy).then_inc(s_c[0], 1)
            for b in range(NB):
                a.wait_ge(s_g, b + 1)
                a.activation(rz[:, b, :], ps[0:B, 2 * (b % 3), 0:2 * D], ACT.Sigmoid).then_inc(s_sig, 1)
            a.wait_ge(s_t, NB)
            a.activation(t[:], t[:], ACT.Tanh).then_inc(s_nn, 1)

        @block.vector
        def _(v):
            v.memset(ones[:], 1.0).then_inc(s_one, 1)
            for k, (i, b0, n) in enumerate(jobs):
                if k % 2 == 1:
                    v.wait_ge(s_tr, k + 1)
                    v.tensor_copy(tr[i][:, b0 * B:(b0 + n) * B], ps[:, k % 8, 0:n * B]).then_inc(s_c[1], 1)
            do = Chain(v, s_d)
            for b in range(NB):
                v.wait_ge(s_sig, b + 1)
                do(v.tensor_tensor(t[:, b, :], rz[:, b, 0:D], ps[0:B, 2 * (b % 3) + 1, 0:D], ALU.mult))
                v.tensor_tensor(t[:, b, :], t[:, b, :], ps[0:B, 2 * (b % 3), 2 * D:3 * D], ALU.add).then_inc(s_t, 1)
            v.wait_ge(s_nn, 1)
            do(v.tensor_tensor(rz[:, :, 0:D], g.h[:, :, 0:D], t[:], ALU.subtract))
            do(v.tensor_tensor(rz[:, :, 0:D], rz[:, :, 0:D], rz[:, :, D:2 * D], ALU.mult))
            do(v.tensor_tensor(g.x[:], g.x[:], t[:], ALU.add))
            do(v.tensor_tensor(g.x[:], g.x[:], rz[:, :, 0:D], ALU.add))


def query_key_phase(nc, g, io, a2):
    with Phase(nc, "qk") as ph:
        h_t = ph.sb("h_t", [D, N])
        wqk = ph.sb("wqk", [D, 2, HEADS * D])
        bqk = ph.sb("bqk", [1, 2, HEADS * D])
        q = ph.sb("q", [B, NB, HEADS * D])
        sq = ph.sb("sq", [B, 2, HEADS * D])
        nrm = ph.sb("nrm", [B, 2, NB, HEADS])
        inv = ph.sb("inv", [B, 2, NB, HEADS])
        ones = ph.sb("ones", [B, 1])
        onerow = ph.sb("onerow", [1, B])
        ksum = ph.sb("ksum", [D, HEADS])
        ps = ph.ps()
        s_in = ph.sem("in")
        s_one = ph.sem("one")
        s_tr = ph.sem("tr")
        s_c = [ph.sem(f"c{i}") for i in range(2)]
        s_q = ph.sem("q")
        s_qc = ph.sem("qc")
        s_sq = ph.sem("sq")
        s_n = ph.sem("n")
        s_unit = ph.sem("unit")
        s_qt = ph.sem("qt")
        s_qtc = [ph.sem(f"qtc{i}") for i in range(2)]
        s_ks = ph.sem("ks")
        s_ksc = ph.sem("ksc")
        s_den = ph.sem("den")
        s_d = ph.sem("d")
        block = ph.ctx.enter_context(nc.Block())
        jobs = [(h, b0, n) for h in range(HEADS) for b0, n in GROUPS]

        @block.sync
        def _(sp):
            for i, n in enumerate(("Wq", "Wk")):
                sp.dma_start(wqk[:, i, :], io[n + "_w"]).then_inc(s_in, 16)
                sp.dma_start(bqk[:, i, :], io[n + "_b"].rearrange("(a k) -> a k", a=1)).then_inc(s_in, 16)

        @block.tensor
        def _(pe):
            for k, (b0, n) in enumerate(GROUPS):
                transposed(pe, ps, k, lambda b: g.h[:, b, 0:D], g.ident, range(b0, b0 + n), s_tr)
            pe.wait_ge(s_c[0], 4)
            pe.wait_ge(s_c[1], 3)
            pe.wait_ge(s_in, 64)
            pe.wait_ge(s_one, 2)
            for b in range(NB):
                if b >= 4:
                    pe.wait_ge(s_qc, b - 3)
                for i in range(2):
                    at = slice(i * HEADS * D, (i + 1) * HEADS * D)
                    pe.matmul(ps[0:B, b % 4, at], h_t[:, b * B:(b + 1) * B], wqk[:, i, :], start=True, stop=False)
                    last = pe.matmul(ps[0:B, b % 4, at], onerow[:], bqk[:, i, :], start=False, stop=True)
                last.then_inc(s_q, 1)
            pe.wait_ge(s_unit, 2)
            pe.wait_ge(s_qc, NB)
            for h in range(HEADS):
                for b in range(NB):
                    last = pe.matmul(ps[:, 7, h:h + 1], a2.ks[:, b, h * D:(h + 1) * D], ones[:], start=b == 0,
                                     stop=b == NB - 1)
            last.then_inc(s_ks, 1)
            for k, (h, b0, n) in enumerate(jobs):
                if k >= 4:
                    pe.wait_ge(s_qtc[k % 2], (k - 4) // 2 + 1)
                transposed(pe, ps, k % 4, lambda b: q[:, b, h * D:(h + 1) * D], g.ident, range(b0, b0 + n), s_qt)
            pe.wait_ge(s_qtc[0], 7)
            pe.wait_ge(s_qtc[1], 7)
            pe.wait_ge(s_ksc, 1)
            for b in range(NB):
                for h in range(HEADS):
                    last = pe.matmul(ps[0:B, 6, b * HEADS + h:b * HEADS + h + 1], a2.qs_t[:, h, b * B:(b + 1) * B],
                                     ksum[:, h:h + 1], start=True, stop=True)
            last.then_inc(s_den, 1)

        @block.scalar
        def _(a):
            for k, (b0, n) in enumerate(GROUPS):
                if k % 2 == 0:
                    a.wait_ge(s_tr, k + 1)
                    a.activation(h_t[:, b0 * B:(b0 + n) * B], ps[:, k, 0:n * B], ACT.Copy).then_inc(s_c[0], 1)
            for b in range(NB):
                a.wait_ge(s_q, b + 1)
                if b:
                    a.wait_ge(s_sq, b)
                for i in range(2):
                    for h in range(HEADS):
                        at = (i * HEADS + h) * D
                        last = a.activation(sq[:, i, h * D:(h + 1) * D], ps[0:B, b % 4, at:at + D], ACT.Square,
                                            accum_out=nrm[:, i, b, h:h + 1])
                last.then_inc(s_sq, 1)
            a.wait_ge(s_sq, NB)
            a.activation(nrm[:], nrm[:], ACT.Sqrt).then_inc(s_n, 1)
            for k, (h, b0, n) in enumerate(jobs):
                if k % 2 == 0:
                    a.wait_ge(s_qt, k + 1)
                    a.activation(a2.qs_t[:, h, b0 * B:(b0 + n) * B], ps[:, k % 4, 0:n * B], ACT.Copy).then_inc(s_qtc[0], 1)

        @block.vector
        def _(v):
            do = Chain(v, s_d)
            v.memset(ones[:], 1.0).then_inc(s_one, 1)
            v.memset(onerow[:], 1.0).then_inc(s_one, 1)
            for k, (b0, n) in enumerate(GROUPS):
                if k % 2 == 1:
                    v.wait_ge(s_tr, k + 1)
                    v.tensor_copy(h_t[:, b0 * B:(b0 + n) * B], ps[:, k, 0:n * B]).then_inc(s_c[1], 1)
            for b in range(NB):
                v.wait_ge(s_sq, b + 1)
                v.tensor_copy(q[:, b, :], ps[0:B, b % 4, 0:HEADS * D])
                v.tensor_copy(a2.ks[:, b, :], ps[0:B, b % 4, HEADS * D:2 * HEADS * D]).then_inc(s_qc, 1)
            v.wait_ge(s_qc, NB)
            v.wait_ge(s_n, 1)
            do(v.reciprocal(inv[:], nrm[:]))
            for i, t in enumerate((q, a2.ks)):
                heads = t[:].rearrange("p b (h k) -> p (b h) k", h=HEADS)
                v.tensor_tensor(heads, heads, bc(inv[:, i, :, :].rearrange("p b h -> p (b h)"), D),
                                ALU.mult).then_inc(s_unit, 1)
            v.wait_ge(s_ks, 1)
            v.tensor_copy(ksum[:], ps[:, 7, 0:HEADS]).then_inc(s_ksc, 1)
            for k, (h, b0, n) in enumerate(jobs):
                if k % 2 == 1:
                    v.wait_ge(s_qt, k + 1)
                    v.tensor_copy(a2.qs_t[:, h, b0 * B:(b0 + n) * B], ps[:, k % 4, 0:n * B]).then_inc(s_qtc[1], 1)
            v.wait_ge(s_den, 1)
            do(v.tensor_scalar(a2.rden[:], ps[0:B, 6, 0:NB * HEADS], float(N), None, ALU.add))
            do(v.reciprocal(a2.rden[:], a2.rden[:]))
            for h in range(HEADS):
                v.tensor_copy(a2.t[:, :, h * D:(h + 1) * D], g.h[:, :, 0:D])
            do(v.tensor_reduce(a2.most[:], g.winsum[:], AX.X, ALU.max))


def parts_flag_phase(nc, g, a2):
    with Phase(nc, "flag") as ph:
        row = ph.sb("row", [1, B])
        most = ph.sb("most", [1, 1])
        ps = ph.ps()
        s_t = ph.sem("t")
        s_d = ph.sem("d")
        block = ph.ctx.enter_context(nc.Block())

        @block.tensor
        def _(pe):
            pe.transpose(ps[0:1, 0, 0:B], a2.most[:], g.ident[0:B, 0:B]).then_inc(s_t, 1)

        @block.vector
        def _(v):
            do = Chain(v, s_d)
            v.wait_ge(s_t, 1)
            do(v.tensor_copy(row[:], ps[0:1, 0, 0:B]))
            do(v.tensor_reduce(most[:], row[:], AX.X, ALU.max))
            do(v.tensor_scalar(most[:], most[:], 256.0, 1.0, ALU.is_gt, ALU.add))
            do(v.tensor_copy(a2.nparts[:], most[:]))
            do(v.memset(a2.xp[:, :, 0, HEADS * D:HEADS * D + 1], 1.0))


def term_phase(nc, g, a2, k, last_term):
    with Phase(nc, f"term{k}") as ph:
        t_t = ph.sb("t_t", [D, 4, 4 * B])
        rest = ph.sb("rest", [B, 5, HEADS * D])
        ones = ph.sb("ones", [B, 1])
        ps = ph.ps()
        s_one = ph.sem("one")
        s_tr = ph.sem("tr")
        s_tc = ph.sem("tc")
        s_y = ph.sem("y")
        s_yc = ph.sem("yc")
        s_kv = ph.sem("kv")
        s_d = ph.sem("d")
        s_p = ph.sem("p")
        block = ph.ctx.enter_context(nc.Block())
        W = HEADS * D

        @block.tensor
        def _(pe):
            pe.wait_ge(s_one, 1)
            if not last_term:
                for h in range(HEADS):
                    for b in range(NB):
                        pe.matmul(ps[:, 6, h * D:(h + 1) * D], a2.ks[:, b, h * D:(h + 1) * D],
                                  a2.t[:, b, h * D:(h + 1) * D], start=b == 0, stop=b == NB - 1)
                for b in range(NB):
                    last = pe.matmul(ps[0:1, 7, 0:W], ones[:], a2.t[:, b, 0:W], start=b == 0, stop=b == NB - 1)
                last.then_inc(s_kv, 1)

            def project(i, b0, n):
                pe.wait_ge(s_tc, 2 * i + 2)
                if i >= 2:
                    pe.wait_ge(s_yc, i - 1)
                for j in range(n):
                    for h in range(HEADS):
                        last = pe.matmul(ps[0:B, 4 + i % 2, j * D:(j + 1) * D],
                                         t_t[:, 2 * (i % 2) + h, j * B:(j + 1) * B],
                                         a2.wo[:, h * (ORDER + 1) + k, :], start=h == 0, stop=h == HEADS - 1)
                last.then_inc(s_y, 1)

            for i, (b0, n) in enumerate(GROUPS):
                for h in range(HEADS):
                    transposed(pe, ps, 2 * (i % 2) + h, lambda b: a2.t[:, b, h * D:(h + 1) * D], g.ident,
                               range(b0, b0 + n), s_tr)
                if i:
                    project(i - 1, *GROUPS[i - 1])
            project(len(GROUPS) - 1, *GROUPS[-1])

        @block.scalar
        def _(a):
            for i, (b0, n) in enumerate(GROUPS):
                for h in range(HEADS):
                    a.wait_ge(s_tr, 2 * i + h + 1)
                    if i >= 2:
                        a.wait_ge(s_y, i - 1)
                    a.activation(t_t[:, 2 * (i % 2) + h, 0:n * B], ps[:, 2 * (i % 2) + h, 0:n * B],
                                 ACT.Copy).then_inc(s_tc, 1)

        @block.gpsimd
        def _(pool):
            pool.memset(ones[:], 1.0).then_inc(s_one, 1)

        @block.vector
        def _(v):
            do = Chain(v, s_d)
            for i, (b0, n) in enumerate(GROUPS):
                if not last_term and i < 5:
                    at = slice(5 * i, 5 * i + 5)
                    do(v.tensor_copy(a2.xp[:, at, 0, 0:W], a2.t[:, at, 0:W]))
                    do(v.tensor_tensor(rest[:], a2.t[:, at, 0:W], a2.xp[:, at, 0, 0:W], ALU.subtract))
                    do(v.tensor_copy(a2.xp[:, at, 1, 0:W], rest[:]))
                    do(v.tensor_tensor(rest[:], rest[:], a2.xp[:, at, 1, 0:W], ALU.subtract))
                    do(v.tensor_copy(a2.xp[:, at, 2, 0:W], rest[:]))
                v.wait_ge(s_y, i + 1)
                blocks = ps[0:B, 4 + i % 2, 0:n * D].rearrange("p (a k) -> p a k", k=D)
                if k == 0:
                    v.tensor_copy(a2.y[:, b0:b0 + n, :], blocks).then_inc(s_yc, 1)
                else:
                    v.tensor_tensor(a2.y[:, b0:b0 + n, :], a2.y[:, b0:b0 + n, :], blocks, ALU.add).then_inc(s_yc, 1)
            if not last_term:
                v.wait_ge(s_kv, 1)
                v.tensor_copy(a2.kv[:], ps[:, 6, 0:W])
                do(v.tensor_copy(a2.vsum[:], ps[0:1, 7, 0:W]))
            else:
                v.wait_ge(s_yc, len(GROUPS))
                do(v.tensor_tensor(a2.y[:], a2.y[:], a2.wob[:].unsqueeze(1).to_broadcast([B, NB, D]), ALU.add))
                do(v.scalar_tensor_tensor(g.x[:], a2.y[:], 1.0 / HEADS, g.x[:], ALU.mult, ALU.add))


def count_phase(nc, g, dr, a2, k):
    R = 5
    W = HEADS * D
    lo = D if k == 0 else 0
    with Phase(nc, f"count{k}") as ph:
        panel = [ph.sb(f"panel{i}", [B, N], BF16) for i in range(R)]
        ps = ph.ps()
        s_zero = ph.sem("zero")
        s_in = [ph.sem(f"in{i}") for i in range(R)]
        s_used = [ph.sem(f"used{i}") for i in range(R)]
        s_added = [ph.sem(f"added{i}") for i in range(R)]
        s_tick = ph.sem("tick")
        block = ph.ctx.enter_context(nc.Block())

        @block.gpsimd
        def _(pool):
            pool.memset(a2.t[:], 0.0).then_inc(s_zero, 1)

        @block.sync
        def _(sp):
            nparts = sp.value_load(a2.nparts[0:1, 0:1], min_val=1, max_val=2)
            rounds = Counter(sp)
            for i in range(R):
                sp.sem_inc(s_used[i], 1)
            with sp.Fori(0, nparts) as part:
                with sp.Fori(0, NB // R) as o:
                    n = rounds.next()
                    for i in range(R):
                        sp.wait_ge(s_used[i], n)
                        sp.sem_inc(s_tick, 1)
                        sp.dma_start(panel[i][:], dr.cnt[bass.ds(part, 1), bass.ds(o * R + i, 1), :, :]
                                     .rearrange("q a p n -> p (q a n)")).then_inc(s_in[i], 16)

        @block.tensor
        def _(pe):
            nparts = pe.value_load(a2.nparts[0:1, 0:1], min_val=1, max_val=2)
            rounds = Counter(pe)
            for i in range(R):
                pe.sem_inc(s_added[i], 1)
            with pe.Fori(0, nparts):
                with pe.Fori(0, NB // R):
                    n = rounds.next()
                    landed = pe.snap(n * 16)
                    for i in range(R):
                        pe.wait_ge(s_in[i], landed)
                        pe.wait_ge(s_added[i], n)
                        for b in range(NB):
                            for p in range(3):
                                hi = W + 1 if p == 0 else W
                                last = pe.matmul(ps[0:B, i, lo:hi], panel[i][:, b * B:(b + 1) * B],
                                                 a2.xp[:, b, p, lo:hi], start=b == 0 and p == 0,
                                                 stop=b == NB - 1 and p == 2, skip_group_check=True)
                        last.then_inc(s_used[i], 1)

        @block.vector
        def _(v):
            nparts = v.value_load(a2.nparts[0:1, 0:1], min_val=1, max_val=2)
            rounds = Counter(v)
            v.wait_ge(s_zero, 1)
            with v.Fori(0, nparts):
                with v.Fori(0, NB // R) as o:
                    n = rounds.next()
                    used = v.snap(n + 1)
                    for i in range(R):
                        at = a2.t[:, bass.ds(o * R + i, 1), lo:W + 1].rearrange("p a k -> p (a k)")
                        v.wait_ge(s_used[i], used)
                        v.tensor_tensor(at, at, ps[0:B, i, lo:W + 1], ALU.add).then_inc(s_added[i], 1)


def combine_phase(nc, g, a2, k):
    W = HEADS * D
    with Phase(nc, f"comb{k}") as ph:
        pos = ph.sb("pos", [B, NB])
        neg = ph.sb("neg", [B, NB])
        onerow = ph.sb("onerow", [1, B])
        ps = ph.ps()
        s_one = ph.sem("one")
        s_at = ph.sem("at")
        s_free = ph.sem("free")
        s_d = ph.sem("d")
        block = ph.ctx.enter_context(nc.Block())
        K = 8

        @block.tensor
        def _(pe):
            pe.wait_ge(s_one, 1)
            for b in range(NB):
                if b >= K:
                    pe.wait_ge(s_free, b - K + 1)
                for h in range(HEADS):
                    at = slice(h * D, (h + 1) * D)
                    pe.matmul(ps[0:B, b % K, at], a2.qs_t[:, h, b * B:(b + 1) * B], a2.kv[:, at], start=True, stop=False)
                    last = pe.matmul(ps[0:B, b % K, at], onerow[:], a2.vsum[:, at], start=False, stop=True)
                last.then_inc(s_at, 1)

        @block.vector
        def _(v):
            do = Chain(v, s_d)
            v.memset(onerow[:], 1.0).then_inc(s_one, 1)
            if k == 0:
                do(v.tensor_copy(g.deg[:], a2.t[:, :, W]))
                do(v.tensor_scalar(pos[:], g.deg[:], 0.0, None, ALU.is_gt))
                do(v.tensor_scalar(neg[:], pos[:], -1.0, 1.0, ALU.mult, ALU.add))
                do(v.tensor_tensor(neg[:], neg[:], g.deg[:], ALU.add))
                do(v.reciprocal(neg[:], neg[:]))
                do(v.scalar_tensor_tensor(a2.half_inv[:], neg[:], 0.5, pos[:], ALU.mult, ALU.mult))
                do(v.tensor_copy(a2.t[:, :, 0:D], a2.t[:, :, D:W]))
            do(v.tensor_tensor(a2.t[:, :, 0:W], a2.t[:, :, 0:W], bc(a2.half_inv[:], W), ALU.mult))
            for b in range(NB):
                v.wait_ge(s_at, b + 1)
                for h in range(HEADS):
                    at = slice(h * D, (h + 1) * D)
                    last = v.scalar_tensor_tensor(a2.t[:, b, at], ps[0:B, b % K, at],
                                                  a2.rden[:, b * HEADS + h:b * HEADS + h + 1], a2.t[:, b, at],
                                                  ALU.mult, ALU.add)
                last.then_inc(s_free, 1)


def message_table_phase(nc, g, dr, io, a3):
    with Phase(nc, "table") as ph:
        w1 = ph.sb("w1", [D, 2, D])
        b1 = ph.sb("b1", [1, 2 * D])
        onerow = ph.sb("onerow", [1, B])
        src = ph.sb("src", [B, NB, D])
        ps = ph.ps()
        s_in = ph.sem("in")
        s_one = ph.sem("one")
        s_tr = ph.sem("tr")
        s_c = [ph.sem(f"c{i}") for i in range(2)]
        s_p = ph.sem("p")
        s_pc = [ph.sem(f"pc{i}") for i in range(2)]
        s_out = ph.sem("out")
        block = ph.ctx.enter_context(nc.Block())

        @block.sync
        def _(sp):
            sp.dma_start(w1[:], io["mw1"][0:2 * D, :].rearrange("(a p) k -> p a k", p=D)).then_inc(s_in, 16)
            sp.wait_ge(s_one, 1)
            sp.dma_start(b1[:, D:2 * D], io["mb1"].rearrange("(a k) -> a k", a=1)).then_inc(s_in, 16)
            sp.dma_start(a3.q_all[B:B + 1, :, :],
                         io["mw1"][2 * D:2 * D + 1, :].unsqueeze(1).to_broadcast([1, NB, D])).then_inc(s_in, 16)
            sp.wait_ge(s_pc[0], NB)
            sp.dma_start(dr.table.rearrange("(b p) d -> p b d", p=B), src[:]).then_inc(s_out, 16)
            sp.wait_ge(s_out, 16)
            sp.wait_ge(s_in, 48)

        @block.tensor
        def _(pe):
            for k, (b0, n) in enumerate(GROUPS):
                transposed(pe, ps, k, lambda b: g.h[:, b, 0:D], g.ident, range(b0, b0 + n), s_tr)
            pe.wait_ge(s_c[0], 4)
            pe.wait_ge(s_c[1], 3)
            pe.wait_ge(s_in, 48)
            pe.wait_ge(s_one, 2)
            for b in range(NB):
                if b >= 8:
                    pe.wait_ge(s_pc[0], b - 7)
                    pe.wait_ge(s_pc[1], b - 7)
                pe.matmul(ps[0:B, b % 8, 0:2 * D], a3.h_t[:, b * B:(b + 1) * B], w1[:].rearrange("p a k -> p (a k)"),
                          start=True, stop=False)
                pe.matmul(ps[0:B, b % 8, 0:2 * D], onerow[:], b1[:], start=False, stop=True).then_inc(s_p, 1)

        @block.scalar
        def _(a):
            for k, (b0, n) in enumerate(GROUPS):
                if k % 2 == 0:
                    a.wait_ge(s_tr, k + 1)
                    a.activation(a3.h_t[:, b0 * B:(b0 + n) * B], ps[:, k, 0:n * B], ACT.Copy).then_inc(s_c[0], 1)
            for b in range(NB):
                a.wait_ge(s_p, b + 1)
                a.activation(src[:, b, :], ps[0:B, b % 8, 0:D], ACT.Copy).then_inc(s_pc[0], 1)

        @block.vector
        def _(v):
            v.memset(b1[:], 0.0).then_inc(s_one, 1)
            v.memset(onerow[:], 1.0).then_inc(s_one, 1)
            for k, (b0, n) in enumerate(GROUPS):
                if k % 2 == 1:
                    v.wait_ge(s_tr, k + 1)
                    v.tensor_copy(a3.h_t[:, b0 * B:(b0 + n) * B], ps[:, k, 0:n * B]).then_inc(s_c[1], 1)
            for b in range(NB):
                v.wait_ge(s_pc[0], b + 1)
                v.tensor_copy(a3.q_all[0:B, b, :], ps[0:B, b % 8, D:2 * D]).then_inc(s_pc[1], 1)


def edge_phase(nc, g, dr, a3):
    S = 4
    with Phase(nc, "edge") as ph:
        idx = [ph.sb(f"idx{s}", [128, 1], I32) for s in range(S)]
        rows = [ph.sb(f"rows{s}", [128, D]) for s in range(S)]
        hot = [ph.sb(f"hot{s}", [128, B + 1]) for s in range(S)]
        hot_t = [ph.sb(f"hot_t{s}", [B + 1, 128]) for s in range(S)]
        act = [ph.sb(f"act{s}", [128, D]) for s in range(S)]
        lane_id = ph.sb("lane_id", [128, B])
        ps = ph.ps()
        s_lane = ph.sem("lane")
        s_idx = [ph.sem(f"idx{s}") for s in range(S)]
        s_rows = [ph.sem(f"rows{s}") for s in range(S)]
        s_hot = [ph.sem(f"hot{s}") for s in range(S)]
        s_tr = [ph.sem(f"tr{s}") for s in range(S)]
        s_hot_t = [ph.sem(f"hot_t{s}") for s in range(S)]
        s_pre = [ph.sem(f"pre{s}") for s in range(S)]
        s_act = [ph.sem(f"act{s}") for s in range(S)]
        s_sum = [ph.sem(f"sum{s}") for s in range(S)]
        s_out = ph.sem("out")
        s_tick = ph.sem("tick")
        block = ph.ctx.enter_context(nc.Block())
        SUMS = S

        def tiles(eng, d, body):
            lo, hi = tile_range(eng, g, d + 256)
            body(lo, True)
            with eng.Fori(lo + S, hi, S) as t:
                body(t, False)

        @block.gpsimd
        def _(pool):
            pool.iota(lane_id[:], [[1, B]], base=0, channel_multiplier=0,
                      allow_small_or_imprecise_dtypes=True).then_inc(s_lane, 1)
            rounds = Counter(pool)

            def gather(t, first):
                n = rounds.next()

                def index(s):
                    pool.wait_ge(s_pre[s], n)
                    pool.sem_inc(s_tick, 1)
                    pool.tensor_copy(idx[s][:], g.src_idx[:, bass.ds(t + s, 1)]).then_inc(s_idx[s], 1)

                index(0)
                for s in range(S):
                    if s + 1 < S:
                        index(s + 1)
                    pool.wait_ge(s_idx[s], n)
                    pool.sem_inc(s_tick, 1)
                    pool.indirect_dma_start(rows[s][:], None, dr.table,
                                            bass.IndirectOffsetOnAxis(ap=idx[s][:], axis=0)).then_inc(s_rows[s], 16)

            with pool.Fori(0, NB) as d:
                tiles(pool, d, gather)

        @block.vector
        def _(v):
            rounds = Counter(v)
            v.wait_ge(s_lane, 1)

            with v.Fori(0, NB) as d:
                def one_hot(t, first):
                    n = rounds.next()
                    for s in range(S):
                        at = bass.ds(t + s, 1)
                        v.wait_ge(s_sum[s], n)
                        v.tensor_scalar(hot[s][:, 0:B], lane_id[:], g.dst[:, at], g.block_base[:, bass.ds(d, 1)],
                                        ALU.subtract, ALU.is_equal)
                        v.tensor_copy(hot[s][:, B:B + 1], g.ea[:, at]).then_inc(s_hot[s], 1)

                tiles(v, d, one_hot)

        @block.tensor
        def _(pe):
            rounds = Counter(pe)
            so_far = pe.alloc_register()
            for s in range(S):
                pe.sem_inc(s_sum[s], 1)
                pe.sem_inc(s_pre[s], 1)

            with pe.Fori(0, NB) as d:
                def turned(s, n):
                    pe.wait_ge(s_hot[s], n)
                    pe.transpose(ps[0:B + 1, s, 0:128], hot[s][:], g.ident[:]).then_inc(s_tr[s], 1)

                def before_relu(s, n, landed):
                    pe.wait_ge(s_hot_t[s], n)
                    pe.wait_ge(s_rows[s], landed)
                    pe.matmul(ps[:, s, 128:256], hot_t[s][:], a3.q_all[:, bass.ds(d, 1), :].rearrange("p a k -> p (a k)"),
                              start=True, stop=False)
                    pe.matmul(ps[:, s, 128:256], g.ident[:], rows[s][:], start=False, stop=True).then_inc(s_pre[s], 1)

                def summed(s, n, start=False, stop=False):
                    pe.wait_ge(s_act[s], n)
                    pe.matmul(ps[:, SUMS, 0:B], act[s][:], hot[s][:, 0:B], start=start, stop=stop,
                              skip_group_check=True).then_inc(s_sum[s], 1)

                def messages(t, first):
                    if not first:
                        pe.reg_mov(so_far, rounds.reg)
                    n = rounds.next()
                    landed = pe.snap(n * 16)
                    turned(0, n)
                    turned(1, n)
                    if not first:
                        summed(S - 1, pe.snap(so_far))
                    for s in range(S):
                        before_relu(s, n, landed)
                        if s + 2 < S:
                            turned(s + 2, n)
                        if s == 1 and first:
                            pe.wait_ge(s_out, d + 1)
                        if s >= 1:
                            summed(s - 1, n, start=first and s == 1)

                tiles(pe, d, messages)
                summed(S - 1, pe.snap(rounds.reg), stop=True)

        @block.scalar
        def _(a):
            rounds = Counter(a)
            a.sem_inc(s_out, 1)

            def sums_of(d, n):
                a.wait_ge(s_sum[S - 1], n)
                a.activation(a3.agg_t[:, bass.ds(d * B, B)], ps[:, SUMS, 0:B], ACT.Copy).then_inc(s_out, 1)

            def block_of(d, before):
                def steps(t, first):
                    n = rounds.next()

                    def turned(s):
                        a.wait_ge(s_tr[s], n)
                        a.activation(hot_t[s][:], ps[0:B + 1, s, 0:128], ACT.Copy).then_inc(s_hot_t[s], 1)

                    turned(0)
                    turned(1)
                    if first and before:
                        sums_of(d - 1, n)
                    for s in range(S):
                        a.wait_ge(s_pre[s], n + 1)
                        a.activation(act[s][:], ps[:, s, 128:256], ACT.Relu).then_inc(s_act[s], 1)
                        if s + 2 < S:
                            turned(s + 2)

                tiles(a, d, steps)

            block_of(0, False)
            with a.Fori(1, NB) as d:
                block_of(d, True)
            sums_of(NB - 1, rounds.next())
            a.wait_ge(s_out, NB + 1)


def update_phase(nc, g, io, a3, out):
    with Phase(nc, "upd") as ph:
        mw2 = ph.sb("mw2", [D, D])
        mw2_t = ph.sb("mw2_t", [D, D])
        mb2 = ph.sb("mb2", [D, 1])
        uw1 = ph.sb("uw1", [D, 2, D])
        ub1 = ph.sb("ub1", [D, 1])
        uw2 = ph.sb("uw2", [D, D])
        ub2 = ph.sb("ub2", [B, D])
        joined = ph.sb("joined", [D, D])
        bias = ph.sb("bias", [B, D])
        diag = [ph.sb(f"diag{i}", [B, 4, B]) for i in range(2)]
        u = [ph.sb(f"u{i}", [D, 4 * B]) for i in range(2)]
        ps = ph.ps()
        s_in = ph.sem("in")
        s_t = ph.sem("t")
        s_tc = ph.sem("tc")
        s_j = ph.sem("j")
        s_jc = ph.sem("jc")
        s_diag = ph.sem("diag")
        s_u = ph.sem("u")
        s_uc = ph.sem("uc")
        s_o = ph.sem("o")
        s_oc = ph.sem("oc")
        s_x = ph.sem("x")
        s_out = ph.sem("out")
        block = ph.ctx.enter_context(nc.Block())

        @block.sync
        def _(sp):
            sp.dma_start(mw2[:], io["mw2"]).then_inc(s_in, 16)
            sp.dma_start(mb2[:], io["mb2"].rearrange("(k a) -> k a", a=1)).then_inc(s_in, 16)
            sp.dma_start(uw1[:], io["uw1"].rearrange("(a p) k -> p a k", p=D)).then_inc(s_in, 16)
            sp.dma_start(ub1[:], io["ub1"].rearrange("(k a) -> k a", a=1)).then_inc(s_in, 16)
            sp.dma_start(uw2[:], io["uw2"]).then_inc(s_in, 16)
            sp.dma_start(ub2[:], io["ub2"].rearrange("(a k) -> a k", a=1).to_broadcast([B, D])).then_inc(s_in, 16)
            sp.wait_ge(s_x, 1)
            sp.dma_start(out.rearrange("(b p) d -> p b d", p=B), g.x[:]).then_inc(s_out, 16)
            sp.wait_ge(s_out, 16)

        @block.tensor
        def _(pe):
            pe.wait_ge(s_in, 96)
            pe.transpose(ps[:, 6, 0:D], mw2[:], g.ident[:]).then_inc(s_t, 1)
            pe.wait_ge(s_tc, 1)
            pe.matmul(ps[:, 6, 0:D], mw2_t[:], uw1[:, 1, :], start=True, stop=True)
            pe.matmul(ps[0:B, 7, 0:D], mb2[:].to_broadcast([D, B]), uw1[:, 1, :], start=True, stop=True).then_inc(s_j, 1)
            pe.wait_ge(s_jc, 1)
            for k, (b0, n) in enumerate(GROUPS):
                at = slice(b0 * B, (b0 + n) * B)
                p = k % 2
                if k >= 2:
                    pe.wait_ge(s_uc, k - 1)
                pe.matmul(ps[:, p, 0:n * B], uw1[:, 0, :], a3.h_t[:, at], start=True, stop=False)
                pe.matmul(ps[:, p, 0:n * B], joined[:], a3.agg_t[:, at], start=False, stop=False)
                pe.wait_ge(s_diag, k + 1)
                pe.matmul(ps[:, p, 0:n * B], bias[:], diag[p][:, 0:n, :].rearrange("p a k -> p (a k)"), start=False,
                          stop=True).then_inc(s_u, 1)
                pe.wait_ge(s_uc, k + 1)
                if k >= 2:
                    pe.wait_ge(s_oc, k - 1)
                for j in range(n):
                    last = pe.matmul(ps[0:B, 2 + p, j * D:(j + 1) * D], u[p][:, j * B:(j + 1) * B], uw2[:],
                                     start=True, stop=True)
                last.then_inc(s_o, 1)

        @block.scalar
        def _(a):
            a.wait_ge(s_in, 96)
            for k, (b0, n) in enumerate(GROUPS):
                a.wait_ge(s_u, k + 1)
                if k >= 2:
                    a.wait_ge(s_o, k - 1)
                a.activation(u[k % 2][:, 0:n * B], ps[:, k % 2, 0:n * B], ACT.Relu, bias=ub1[:]).then_inc(s_uc, 1)

        @block.vector
        def _(v):
            v.wait_ge(s_t, 1)
            v.tensor_copy(mw2_t[:], ps[:, 6, 0:D]).then_inc(s_tc, 1)
            v.wait_ge(s_j, 1)
            v.tensor_copy(joined[:], ps[:, 6, 0:D])
            v.tensor_copy(bias[:], ps[0:B, 7, 0:D]).then_inc(s_jc, 1)
            v.wait_ge(s_in, 96)
            v.tensor_tensor(g.x[:], g.x[:], g.h[:, :, 0:D], ALU.add).then_inc(s_tc, 1)
            v.wait_ge(s_tc, 2)
            v.tensor_tensor(g.x[:], g.x[:], ub2[:].unsqueeze(1).to_broadcast([B, NB, D]), ALU.add).then_inc(s_tc, 1)
            v.wait_ge(s_tc, 3)

            def diagonals(k):
                b0, n = GROUPS[k]
                if k >= 2:
                    v.wait_ge(s_u, k - 1)
                for j in range(n):
                    last = v.tensor_scalar(diag[k % 2][:, j, :], g.ident[0:B, 0:B], g.deg[:, b0 + j:b0 + j + 1], None,
                                           ALU.mult)
                last.then_inc(s_diag, 1)

            diagonals(0)
            for k, (b0, n) in enumerate(GROUPS):
                if k + 1 < len(GROUPS):
                    diagonals(k + 1)
                v.wait_ge(s_o, k + 1)
                v.tensor_tensor(g.x[:, b0:b0 + n, :], g.x[:, b0:b0 + n, :],
                                ps[0:B, 2 + k % 2, 0:n * D].rearrange("p (a k) -> p a k", k=D),
                                ALU.add).then_inc(s_oc, 1)
            v.wait_ge(s_oc, len(GROUPS))
            v.sem_inc(s_x, 1)


def load_phase(nc, name, pairs):
    with Phase(nc, name) as ph:
        s_in = ph.sem("in")
        block = ph.ctx.enter_context(nc.Block())

        @block.sync
        def _(sp):
            for out, in_ in pairs:
                sp.dma_start(out, in_).then_inc(s_in, 16)
            sp.wait_ge(s_in, 16 * len(pairs))


def layers(nc, g, dr, io, out):
    with ExitStack() as ctx:
        def sb(name, shape, dt=F32):
            return ctx.enter_context(nc.sbuf_tensor(name, shape, dt))

        w = Obj()
        w.m = sb("w_m", [D, 2, 3 * D])
        w.whh_t = sb("w_whh_t", [D, 3 * D])
        w.brow = sb("w_brow", [1, 3 * D])
        w.bhh = sb("w_bhh", [1, 3 * D])
        w.alpha = sb("w_alpha", [B, 4])
        w.tmp = sb("w_tmp", [B, 2])
        w.r_src = sb("w_r_src", [B, NB])
        w.r_dst = sb("w_r_dst", [B, NB])
        w.pos = sb("w_pos", [B, NB])
        w.neg = sb("w_neg", [B, NB])
        y = sb("y", [B, NB, D])
        weights_phase(nc, g, io, w)
        spmm_t_phase(nc, g, dr, "back", g.h, y, w.r_src[:], None)
        gru_phase(nc, g, w, y)
        norm_phase(nc, g, "norm1")
        with Phase(nc, "alpha0") as ph:
            block = ph.ctx.enter_context(nc.Block())

            @block.vector
            def _(v):
                v.scalar_tensor_tensor(g.x[:], g.h[:, :, 0:D], w.alpha[:, 0:1], g.x[:], ALU.mult, ALU.add)
        for k in range(1, 4):
            spmm_t_phase(nc, g, dr, f"hop{k}", g.h if k == 1 else y, y, None, w.alpha[:, k:k + 1])
        norm_phase(nc, g, "norm2")
    with ExitStack() as ctx:
        def sb(name, shape, dt=F32):
            return ctx.enter_context(nc.sbuf_tensor(name, shape, dt))

        a2 = Obj()
        a2.ks = sb("a_ks", [B, NB, HEADS * D])
        a2.qs_t = sb("a_qs_t", [D, HEADS, N])
        a2.rden = sb("a_rden", [B, NB * HEADS])
        a2.t = sb("a_t", [B, NB, HEADS * D + 1])
        a2.kv = sb("a_kv", [D, HEADS * D])
        a2.vsum = sb("a_vsum", [1, HEADS * D])
        a2.half_inv = sb("a_half_inv", [B, NB])
        a2.most = sb("a_most", [B, 1])
        a2.nparts = sb("a_nparts", [1, 1], I32)
        query_key_phase(nc, g, io, a2)
        a2.xp = sb("a_xp", [B, NB, 3, HEADS * D + 1], BF16)
        a2.y = g.n1[:, :, 0:D]
        a2.wo = sb("a_wo", [D, HEADS * (ORDER + 1), D])
        a2.wob = sb("a_wob", [B, D])
        parts_flag_phase(nc, g, a2)
        load_phase(nc, "loadwo", [(a2.wo[:], io["Wo_w"].rearrange("(t p) k -> p t k", p=D)),
                                  (a2.wob[:], io["Wo_b"].rearrange("(a k) -> a k", a=1).to_broadcast([B, D]))])
        for k in range(ORDER):
            term_phase(nc, g, a2, k, False)
            count_phase(nc, g, dr, a2, k)
            combine_phase(nc, g, a2, k)
        term_phase(nc, g, a2, ORDER, True)
        norm_phase(nc, g, "norm3")
    with ExitStack() as ctx:
        def sb(name, shape, dt=F32):
            return ctx.enter_context(nc.sbuf_tensor(name, shape, dt))

        a3 = Obj()
        a3.h_t = sb("m_h_t", [D, N])
        a3.agg_t = sb("m_agg_t", [D, N])
        a3.q_all = sb("m_q_all", [B + 1, NB, D])
        message_table_phase(nc, g, dr, io, a3)
        edge_phase(nc, g, dr, a3)
        update_phase(nc, g, io, a3, out)


_INS = {'x': 'x', 'src': 'src', 'dst': 'dst', 'edge_weight': 'w', 'edge_weight1': 'ea', 'L0_gnn_W1': 'W1',
        'L0_gnn_W2': 'W2', 'L0_gnn_w_ih': 'w_ih', 'L0_gnn_w_hh': 'w_hh', 'L0_gnn_b_ih': 'b_ih',
        'L0_gnn_b_hh': 'b_hh', 'L1_gnn_alpha_logits': 'alpha', 'L2_gnn_Wq_w': 'Wq_w', 'L2_gnn_Wq_b': 'Wq_b',
        'L2_gnn_Wk_w': 'Wk_w', 'L2_gnn_Wk_b': 'Wk_b', 'L2_gnn_Wo_w': 'Wo_w', 'L2_gnn_Wo_b': 'Wo_b',
        'L3_gnn_msg_w1': 'mw1', 'L3_gnn_msg_b1': 'mb1', 'L3_gnn_msg_w2': 'mw2', 'L3_gnn_msg_b2': 'mb2',
        'L3_gnn_upd_w1': 'uw1', 'L3_gnn_upd_b1': 'ub1', 'L3_gnn_upd_w2': 'uw2', 'L3_gnn_upd_b2': 'ub2'}


def kernel(**inputs):
    import numpy as np
    import concourse.bacc as bacc
    from concourse.bass_utils import run_bass_kernel_spmd
    nc = bacc.Bacc("TRN2", target_bir_lowering=False, num_devices=1)
    arrays, io = {}, {}
    for name, short in _INS.items():
        a = np.ascontiguousarray(inputs[name])
        if name == 'edge_weight1':
            a = a.reshape(-1)
        arrays[name + "_dram"] = a
        io[short] = nc.dram_tensor(name + "_dram", a.shape, mybir.dt.from_np(a.dtype), kind="ExternalInput").ap()
    out = nc.dram_tensor("out_dram", (N, D), F32, kind="ExternalOutput").ap()
    program(nc, io, out)
    r = run_bass_kernel_spmd(nc, [arrays], core_ids=[0])
    return r.results[0]["out_dram"]
```

```python
import concourse.bass as bass
from concourse import mybir
from contextlib import ExitStack

F32 = mybir.dt.float32
F16 = mybir.dt.float16
BF16 = mybir.dt.bfloat16
I32 = mybir.dt.int32
ALU = mybir.AluOpType
ACT = mybir.ActivationFunctionType
AX = mybir.AxisListType

N = 3125
E = 100000
D = 128
B = 125
NB = N // B
WIN = 25
WPB = B // WIN
NW = N // WIN
TE = 128
CT = 7
NT = CT * 128
PAD = 4000
FAR = 100000.0
RANGE_BITS = 10
RANGE = 1 << RANGE_BITS
KW = WIN * NB
KEVEN = KW + 1
HEADS = 2
ORDER = 4
PANELS = 5
EARLY = 2
HOPS = 3
EPS = 1e-5
BIAS_QK = 4 * D
BIAS_MESSAGE = BIAS_QK + 2 * HEADS * D
CHUNKS = [(c, min(512, N - c)) for c in range(0, N, 512)]
GROUPS = [(g, min(4, NB - g)) for g in range(0, NB, 4)]


class Counter:

    def __init__(self, eng):
        self.eng = eng
        self.reg = eng.alloc_register()
        eng.reg_mov(self.reg, 0)

    def next(self):
        self.eng.reg_add(self.reg, self.reg, 1)
        return self.eng.snap(self.reg)


class Chain:

    def __init__(self, eng, sem):
        self.eng, self.sem, self.n = eng, sem, 0

    def __call__(self, ins):
        self.n += 1
        ins.then_inc(self.sem, 1)
        self.eng.wait_ge(self.sem, self.n)


class Phase:

    used = []

    def __init__(self, nc, name):
        self.nc, self.name, self.ctx, self.sems = nc, name, ExitStack(), []

    def __enter__(self):
        self.ctx.__enter__()
        return self

    def __exit__(self, *a):
        done = self.ctx.__exit__(*a)
        self.used.extend(self.sems)
        if len(self.used) > 80:
            self.nc.clear_and_free_semaphores(list(self.used))
            self.nc.all_engine_barrier()
            self.used.clear()
        return done

    def sb(self, name, shape, dt=F32):
        return self.ctx.enter_context(self.nc.sbuf_tensor(f"{self.name}_{name}", shape, dt))

    def ps(self, name="ps"):
        return self.ctx.enter_context(self.nc.psum_tensor(f"{self.name}_{name}", [128, 8, 512], F32))

    def sem(self, name):
        sem = self.nc.alloc_semaphore(f"{self.name}_{name}")
        self.sems.append(sem)
        return sem


def bc(ap, n):
    return ap.unsqueeze(2).to_broadcast([ap.shape[0], ap.shape[1], n])


class Panels:

    def __init__(self, ph):
        self.buf = [ph.sb(f"panel{i}", [B, N], BF16) for i in range(EARLY)]
        self.s_in = [ph.sem(f"in{i}") for i in range(PANELS)]


class Ranges:

    def __init__(self, eng, g, slots):
        self.eng, self.g = eng, g
        regs = [[eng.alloc_register(name=f"range{slots}_{i}_{k}") for k in range(2)] for i in range(slots + 1)]
        self.regs, self.now = regs[:slots], regs[slots]

    def load(self, i, at):
        both = self.eng.value_load(self.g.bounds[0:1, bass.ds(at, 1)], min_val=0, max_val=NT * RANGE)
        for r, val in zip(self.regs[i], (both >> RANGE_BITS, both & (RANGE - 1))):
            self.eng.reg_mov(r, val)

    def range(self, i):
        for r, val in zip(self.now, self.regs[i]):
            self.eng.reg_mov(r, val)
        return [self.eng.snap(r, min_val=0, max_val=E // TE + 1) for r in self.now]


def setup_phase(nc, g, io):
    with Phase(nc, "setup") as ph:
        raw = [ph.sb(f"raw{i}", [128, CT, 128], dt) for i, dt in enumerate((I32, I32, F32, F32))]
        dst_q = ph.sb("dst_q", [128, CT, 128])
        src_q = ph.sb("src_q", [128, CT, 128])
        src_t = ph.sb("src_t", [128, NT])
        w_t = ph.sb("w_t", [128, NT])
        t1 = ph.sb("t1", [128, NT])
        ti = ph.sb("ti", [128, NT], I32)
        tb = ph.sb("tb", [128, NT], BF16)
        mx = ph.sb("mx", [128, 2, CT])
        diag = ph.sb("diag", [128, 2, CT, 128])
        ones = ph.sb("ones", [128, 128])
        mxb = ph.sb("mxb", [128, 2, NT])
        pid = ph.sb("pid", [128, NT])
        thr = ph.sb("thr", [128, 4])
        pt = ph.sb("pt", [128, NT])
        lim = ph.sb("lim", [128, 4])
        both = ph.sb("both", [128, 2])
        ps = ph.ps()
        s_pad = ph.sem("pad")
        s_in = ph.sem("in")
        s_x = ph.sem("x")
        s_const = ph.sem("const")
        s_f = ph.sem("f")
        s_tr = ph.sem("tr")
        s_diag = ph.sem("diag")
        s_copied = ph.sem("copied")
        s_bc = ph.sem("bc")
        s_lim = ph.sem("lim")
        s_row = ph.sem("row")
        s_d = ph.sem("d")
        norm = Norm(ph, g.x, g.h)
        block = ph.ctx.enter_context(nc.Block())

        @block.scalar
        def _(a):
            norm.scalar(a)

        full = E // TE
        rows, tail = full - 128 * (CT - 1), E - full * TE

        @block.sync
        def _(sp):
            sp.dma_start(g.x[:], io["x"].rearrange("(b p) d -> p b d", p=B)).then_inc(s_x, 16)
            sp.wait_ge(s_pad, 4)
            for r, a in zip(raw, (io["dst"], io["src"], io["w"], io["ea"])):
                sp.dma_start(r[:, 0:CT - 1, :],
                             a[0:128 * (CT - 1) * TE].rearrange("(c q p) -> q c p", q=128, p=TE)).then_inc(s_in, 16)
                sp.dma_start(r[0:rows, CT - 1, :],
                             a[128 * (CT - 1) * TE:full * TE].rearrange("(q p) -> q p", p=TE)).then_inc(s_in, 16)
                sp.dma_start(r[rows:rows + 1, CT - 1, 0:tail],
                             a[full * TE:E].rearrange("(q p) -> q p", q=1)).then_inc(s_in, 16)

        @block.gpsimd
        def _(pool):
            pool.memset(raw[0][:], PAD).then_inc(s_pad, 1)
            for r in raw[1:]:
                pool.memset(r[:], 0).then_inc(s_pad, 1)
            pool.memset(g.ident[:], 0.0).then_inc(s_const, 1)
            pool.wait_ge(s_const, 1)
            pool.affine_select(out=g.ident[:], in_=g.ident[:], compare_op=ALU.not_equal, fill=1.0, base=0,
                               pattern=[[-1, 128]], channel_multiplier=1).then_inc(s_const, 1)
            pool.iota(g.key_id[:], [[1, KEVEN]], base=0, channel_multiplier=0,
                      allow_small_or_imprecise_dtypes=True).then_inc(s_const, 1)
            pool.iota(pid[:], [[1, NT]], base=0, channel_multiplier=0,
                      allow_small_or_imprecise_dtypes=True).then_inc(s_const, 1)
            for i, (base, step) in enumerate(((0, WIN), (WIN - 1, WIN), (0, B), (B - 1, B))):
                pool.iota(thr[:, i:i + 1], [[0, 1]], base=base, channel_multiplier=step,
                          allow_small_or_imprecise_dtypes=True).then_inc(s_const, 1)
            pool.iota(g.win_base[:], [[-KW, NW]], base=0, channel_multiplier=0,
                      allow_small_or_imprecise_dtypes=True)
            pool.iota(g.block_base[:], [[-B, NB]], base=0, channel_multiplier=0,
                      allow_small_or_imprecise_dtypes=True)
            pool.memset(ones[:], 1.0).then_inc(s_const, 1)
            pool.memset(g.h[:, :, D:D + 1], 1.0).then_inc(s_const, 1)

        @block.tensor
        def _(pe):
            pe.wait_ge(s_const, 10)
            pe.wait_ge(s_in, 192)
            pe.wait_ge(s_f, 2)
            for i, a in enumerate((dst_q, src_q, raw[2], raw[3])):
                for c in range(CT):
                    last = pe.transpose(ps[:, 2 * i + c // 4, (c % 4) * 128:(c % 4) * 128 + 128], a[:, c, :], g.ident[:])
                last.then_inc(s_tr, 1)
            pe.wait_ge(s_diag, 2)
            pe.wait_ge(s_copied, 1)
            for i in range(2):
                for c in range(CT):
                    last = pe.matmul(ps[:, 2 * i + c // 4, (c % 4) * 128:(c % 4) * 128 + 128], ones[:],
                                     diag[:, i, c, :], start=True, stop=True)
            last.then_inc(s_bc, 1)
            pe.wait_ge(s_lim, 1)
            for i in range(2):
                last = pe.transpose(ps[0:1, 4, i * 128:(i + 1) * 128], both[:, i:i + 1], g.ident[:])
            last.then_inc(s_row, 1)

        @block.vector
        def _(v):
            do = Chain(v, s_d)
            v.wait_ge(s_x, 16)
            norm.vector(v)
            v.wait_ge(s_in, 192)
            v.tensor_copy(dst_q[:], raw[0][:]).then_inc(s_f, 1)
            v.tensor_copy(src_q[:], raw[1][:]).then_inc(s_f, 1)
            v.wait_ge(s_f, 2)
            v.tensor_reduce(mx[:, 0, :], dst_q[:], AX.X, ALU.max)
            do(v.tensor_reduce(mx[:, 1, :], dst_q[:], AX.X, ALU.min))
            v.wait_ge(s_const, 10)
            for i in range(2):
                for c in range(CT):
                    last = v.tensor_scalar(diag[:, i, c, :], g.ident[:], mx[:, i, c:c + 1], None, ALU.mult)
                last.then_inc(s_diag, 1)
            v.wait_ge(s_tr, 4)
            for i, a in enumerate((g.dst, src_t, w_t, g.ea)):
                v.tensor_copy(a[:, 0:512], ps[:, 2 * i, :])
                last = v.tensor_copy(a[:, 512:NT], ps[:, 2 * i + 1, 0:NT - 512])
            last.then_inc(s_copied, 1)
            v.wait_ge(s_copied, 1)
            blk, lane = g.key, g.lane
            do(v.tensor_scalar(ti[:], src_t[:], 1.0 / B, None, ALU.mult))
            do(v.tensor_copy(blk[:], ti[:]))
            do(v.scalar_tensor_tensor(lane[:], blk[:], -float(B), src_t[:], ALU.mult, ALU.add))
            do(v.tensor_scalar(t1[:], lane[:], 0.0, None, ALU.is_lt))
            do(v.tensor_tensor(blk[:], blk[:], t1[:], ALU.subtract))
            do(v.scalar_tensor_tensor(lane[:], t1[:], float(B), lane[:], ALU.mult, ALU.add))
            do(v.tensor_scalar(t1[:], lane[:], float(B), None, ALU.is_ge))
            do(v.tensor_tensor(blk[:], blk[:], t1[:], ALU.add))
            do(v.scalar_tensor_tensor(lane[:], t1[:], -float(B), lane[:], ALU.mult, ALU.add))
            do(v.scalar_tensor_tensor(g.key[:], g.dst[:], float(NB), blk[:], ALU.mult, ALU.add))
            do(v.tensor_copy(g.src_idx[:], src_t[:]))
            for i in range(3):
                do(v.tensor_copy(tb[:], w_t[:]))
                do(v.tensor_copy(g.wpart[i][:], tb[:]))
                if i < 2:
                    do(v.tensor_tensor(w_t[:], w_t[:], g.wpart[i][:], ALU.subtract))
            v.wait_ge(s_bc, 1)
            for i in range(2):
                v.tensor_copy(mxb[:, i, 0:512], ps[:, 2 * i, :])
                last = v.tensor_copy(mxb[:, i, 512:NT], ps[:, 2 * i + 1, 0:NT - 512])
            do(last)
            for k in range(2):
                do(v.tensor_scalar(pt[:], mxb[:, 0, :], thr[:, 2 * k:2 * k + 1], FAR, ALU.is_lt, ALU.mult))
                do(v.tensor_tensor(pt[:], pt[:], pid[:], ALU.add))
                do(v.tensor_reduce(lim[:, 2 * k:2 * k + 1], pt[:], AX.X, ALU.min))
                do(v.tensor_scalar(pt[:], mxb[:, 1, :], thr[:, 2 * k + 1:2 * k + 2], -FAR, ALU.is_gt, ALU.mult))
                do(v.tensor_tensor(pt[:], pt[:], pid[:], ALU.add))
                do(v.tensor_reduce(lim[:, 2 * k + 1:2 * k + 2], pt[:], AX.X, ALU.max))
                do(v.tensor_scalar(lim[:, 2 * k + 1:2 * k + 2], lim[:, 2 * k + 1:2 * k + 2], 1.0, 0.0,
                                   ALU.add, ALU.max))
                do(v.scalar_tensor_tensor(both[:, k:k + 1], lim[:, 2 * k:2 * k + 1], float(RANGE),
                                          lim[:, 2 * k + 1:2 * k + 2], ALU.mult, ALU.add))
            v.memset(t1[:, 0:1], 0.0).then_inc(s_lim, 1)
            v.wait_ge(s_row, 1)
            v.tensor_copy(g.bounds[:], ps[0:1, 4, 0:256])


class Norm:

    SQUARES = 18
    SCALED = 10

    def __init__(self, ph, x, out):
        self.x, self.out = x, out
        self.xc = ph.sb("norm_xc", [B, NB, D])
        self.sq = ph.sb("norm_sq", [B, NB, D])
        self.m = ph.sb("norm_m", [B, NB])
        self.var = ph.sb("norm_var", [B, NB])
        self.r = ph.sb("norm_r", [B, NB])
        self.s_mean, self.s_var, self.s_v, self.s_sd, self.s_r, self.s_d = (
            ph.sem(n) for n in ("norm_mean", "norm_var", "norm_v", "norm_sd", "norm_r", "norm_d"))
        self.s_done = [ph.sem(f"norm{i}") for i in range(2)]

    def wait(self, eng):
        for sem in self.s_done:
            eng.wait_ge(sem, 1)

    def vector(self, v):
        x, xc, sq, m, var, r = self.x, self.xc, self.sq, self.m, self.var, self.r
        own = slice(self.SQUARES, NB)
        do = Chain(v, self.s_d)
        do(v.tensor_reduce(m[:], x[:], AX.X, ALU.add))
        v.tensor_scalar(m[:], m[:], -1.0 / D, None, ALU.mult).then_inc(self.s_mean, 1)
        v.wait_ge(self.s_mean, 1)
        do(v.tensor_tensor(xc[:], x[:], bc(m[:], D), ALU.add))
        do(v.tensor_tensor(sq[:, own, :], xc[:, own, :], xc[:, own, :], ALU.mult))
        do(v.tensor_reduce(var[:, own], sq[:, own, :], AX.X, ALU.add))
        v.wait_ge(self.s_var, 1)
        v.tensor_scalar(var[:], var[:], 1.0 / D, EPS, ALU.mult, ALU.add).then_inc(self.s_v, 1)
        v.wait_ge(self.s_sd, 1)
        v.reciprocal(r[:], var[:]).then_inc(self.s_r, 1)
        v.wait_ge(self.s_r, 1)
        for b in range(self.SCALED, NB):
            last = v.tensor_scalar(self.out[:, b, 0:D], xc[:, b, :], r[:, b:b + 1], 0.0, ALU.mult, ALU.max)
        last.then_inc(self.s_done[0], 1)

    def scalar(self, a):
        a.wait_ge(self.s_mean, 1)
        for b in range(self.SQUARES):
            last = a.activation(self.sq[:, b, :], self.x[:, b, :], ACT.Square, bias=self.m[:, b:b + 1],
                                accum_out=self.var[:, b:b + 1])
        last.then_inc(self.s_var, 1)
        a.wait_ge(self.s_v, 1)
        a.activation(self.var[:], self.var[:], ACT.Sqrt).then_inc(self.s_sd, 1)
        a.wait_ge(self.s_r, 1)
        for b in range(self.SCALED):
            last = a.activation(self.out[:, b, 0:D], self.xc[:, b, :], ACT.Relu, scale=self.r[:, b:b + 1])
        last.then_inc(self.s_done[1], 1)


def build_phase(nc, g, dr, io, w):
    with Phase(nc, "build") as ph:
        left = [ph.sb(f"left{s}", [128, 4, 128], BF16) for s in range(2)]
        right = [ph.sb(f"right{s}", [128, KEVEN], BF16) for s in range(2)]
        stage = [ph.sb(f"stage{j}", [B, WIN, NB]) for j in range(WPB)]
        adj = [ph.sb(f"adj{i}", [B, NB, B]) for i in range(2)]
        cnt = [ph.sb(f"cnt{i}", [B, NB, B], BF16) for i in range(2)]
        adj_t = ph.sb("adj_t", [B, N])
        rowsum = ph.sb("rowsum", [B, NB])
        ps = ph.ps()
        s_lane = [ph.sem(f"lane{s}") for s in range(2)]
        s_ready = [ph.sem(f"ready{s}") for s in range(2)]
        s_scaled = [ph.sem(f"scaled{s}") for s in range(2)]
        s_half = [ph.sem(f"half{s}") for s in range(2)]
        s_free = [ph.sem(f"free{s}") for s in range(2)]
        s_staged = ph.sem("staged")
        s_stagedv = ph.sem("stagedv")
        s_unstaged = ph.sem("unstaged")
        s_pool = ph.sem("pool")
        s_cnt = ph.sem("cnt")
        s_tr = ph.sem("tr")
        s_moved = [ph.sem(f"moved{i}") for i in range(2)]
        s_n1 = ph.sem("n1")
        s_n1c = ph.sem("n1c")
        s_sum = ph.sem("sum")
        s_sumadd = ph.sem("sumadd")
        s_adjout = ph.sem("adjout")
        s_cntout = ph.sem("cntout")
        s_weights = ph.sem("weights")
        s_tick = ph.sem("tick")
        block = ph.ctx.enter_context(nc.Block())
        NG = len(GROUPS)
        COUNT = 3
        FINISH = 2
        EVEN, ODD = (NG + 1) // 2, NG // 2
        TURN = {x: [6, x, x + 1, x + 2, 7, 6, x] for x in (0, 3)}
        PIECES = [[(0, 0, 500), (1, 0, KW - 500)], [(1, KW - 500, 500), (2, 0, 2 * KW - 1000)]]

        def windows(eng, step, between, d, ahead):
            for j in range(WPB):
                w = d * WPB + j
                lo, hi = ahead.range(j)
                step(lo, w, j, True)
                between(w, j)
                with eng.Fori(lo + 2, hi, 2) as t:
                    step(t, w, j, False)

        def staging(eng, w, j, parity, d, rounds_done):
            eng.wait_ge(s_free[1], rounds_done)
            if j == 0 and d is not None:
                eng.wait_ge(s_n1, d)
                eng.wait_ge(s_sumadd, d)
            return 3 * ((j + parity) % 2), lambda k0, k1: adj[parity][:, :, j * WIN + k0:j * WIN + k1]

        def by_block(sums):
            return sums.rearrange("p (k h) -> p h k", h=NB)

        def move_transposed(eng, copy, odd, d, x, after=lambda i: None):
            eng.wait_ge(s_adjout, d * 16 + 1)
            for i in range(odd, NG, 2):
                b0, n = GROUPS[i]
                eng.wait_ge(s_tr, d * NG + (i + 1))
                copy(adj_t[:, b0 * B:(b0 + n) * B], ps[0:B, TURN[x][i], 0:n * B]).then_inc(s_moved[odd], 1)
                after(i // 2)

        def before_window(w, j, d, parity, staged, done):
            if j > 0:
                staged(w - 1, j - 1, parity or 0, None if parity is None else d, done)
            elif parity is not None:
                staged(w - 1, WPB - 1, 1 - parity, d - 1, done)

        def windows_ahead(eng):
            ahead = Ranges(eng, g, WPB)
            for i in range(FINISH + 1):
                ahead.load(i, i)
            return ahead

        def load_ahead(ahead, d, windows=range(WPB)):
            for i in windows:
                ahead.load((FINISH + 1 + i) % WPB, d * WPB + (FINISH + 1 + i))

        @block.vector
        def _(v):
            rounds = Counter(v)
            ahead = windows_ahead(v)

            def factors(t, w, j, first):
                n = rounds.next()
                for s in range(2):
                    at = bass.ds(t + s, 1)
                    v.wait_ge(s_half[s], n)
                    v.tensor_scalar(left[s][:, COUNT, :], g.key_id[:, 0:128], g.lane[:, at], None,
                                    ALU.is_equal).then_inc(s_lane[s], 1)
                    v.tensor_scalar(left[s][:, 0, :], g.key_id[:, 0:128], g.lane[:, at], g.wpart[0][:, at],
                                    ALU.is_equal, ALU.mult)
                    v.wait_ge(s_free[s], n)
                    v.tensor_scalar(right[s][:], g.key_id[:], g.key[:, at], g.win_base[:, bass.ds(w, 1)],
                                    ALU.subtract, ALU.is_equal).then_inc(s_ready[s], 1)

            def row_sums(d, parity):
                v.wait_ge(s_staged, d * WPB + WPB)
                v.wait_ge(s_stagedv, d * WPB + WPB)
                v.wait_ge(s_sumadd, d + 1)
                v.tensor_reduce(rowsum[:], adj[parity][:], AX.X, ALU.add).then_inc(s_sum, 1)
                v.wait_ge(s_sum, d + 1)
                v.tensor_tensor(g.wsum_src[:], g.wsum_src[:], rowsum[:], ALU.add).then_inc(s_sumadd, 1)

            def staged(w, j, parity, d, rounds_done):
                bank, weights = staging(v, w, j, parity, d, rounds_done)
                v.tensor_copy(weights(0, 20), by_block(ps[0:B, bank, 0:500])).then_inc(s_stagedv, 1)

            def block_of(d, parity):
                def between(w, j):
                    before_window(w, j, d, parity, staged, v.snap(rounds.reg))
                    if j == FINISH:
                        if parity is not None:
                            move_transposed(v, v.tensor_copy, 0, d - 1, 3 * ((j + parity) % 2),
                                            lambda i: load_ahead(ahead, d, [i]))
                            load_ahead(ahead, d, [WPB - 1])
                            row_sums(d - 1, 1 - parity)
                        else:
                            load_ahead(ahead, d)

                windows(v, factors, between, d, ahead)

            v.memset(g.wsum_src[:], 0.0).then_inc(s_sumadd, 1)
            block_of(0, None)
            with v.Fori(0, NB // 2) as pair:
                d = pair * 2 + 1
                block_of(d, 1)
                block_of(d + 1, 0)
            staged(NW - 1, WPB - 1, 0, NB - 1, rounds.next())
            move_transposed(v, v.tensor_copy, 0, NB - 1, 3, lambda i: None)
            row_sums(NB - 1, 0)

        @block.tensor
        def _(pe):
            rounds = Counter(pe)
            ahead = windows_ahead(pe)
            pe.sem_inc(s_n1, 1)
            for s in range(2):
                pe.sem_inc(s_half[s], 1)
                pe.sem_inc(s_free[s], 1)

            def products(bank, start):
                n = rounds.next()
                for s in range(2):
                    pe.wait_ge(s_ready[s], n)
                    pe.wait_ge(s_scaled[s], n)
                    for k in (0, COUNT, 1, 2):
                        col = 0
                        for off, c0, c1 in PIECES[k == COUNT]:
                            opens = start and s == 0 and ((k == 0) or (off == 2))
                            last = pe.matmul(ps[0:B, bank + off, c0:c1], left[s][:, k, 0:B],
                                             right[s][:, col:col + c1 - c0], start=opens, stop=False,
                                             skip_group_check=True)
                            col += c1 - c0
                        if k == COUNT:
                            last.then_inc(s_half[s], 1)
                    last.then_inc(s_free[s], 1)

            def finish(d, x, parity, load_next):
                pe.wait_ge(s_staged, d * WPB + WPB)
                pe.wait_ge(s_stagedv, d * WPB + WPB)
                pe.wait_ge(s_n1c, d + 1)
                for i, (b0, n) in enumerate(GROUPS):
                    if i >= 5:
                        before = i - 5
                        pe.wait_ge(s_moved[before % 2], d * (EVEN, ODD)[before % 2] + (before // 2 + 1))
                    for k in range(n):
                        last = pe.transpose(ps[0:B, TURN[x][i], k * B:(k + 1) * B], adj[parity][:, b0 + k, :],
                                            g.ident[0:B, 0:B])
                    last.then_inc(s_tr, 1)
                pe.wait_ge(s_moved[0], d * EVEN + 3)
                for k in range(NB):
                    last = pe.matmul(ps[0:B, 7, 0:D + 1], adj[parity][:, k, :], g.h[:, k, :], start=k == 0, stop=k == NB - 1)
                    if k % 5 == 4:
                        load_next(k // 5)
                last.then_inc(s_n1, 1)
                pe.wait_ge(s_moved[0], d * EVEN + EVEN)
                pe.wait_ge(s_moved[1], d * ODD + ODD)

            def block_of(d, parity):
                def step(t, w, j, first):
                    bank = 3 * ((j + (parity or 0)) % 2)
                    if first and (parity is not None or j >= 2):
                        pe.wait_ge(s_staged, w - 1)
                        pe.wait_ge(s_stagedv, w - 1)
                    if first and j == FINISH and parity is not None:
                        finish(d - 1, bank, 1 - parity, lambda i: load_ahead(ahead, d, [i]))
                    products(bank, first)

                def between(w, j):
                    if j == FINISH and parity is None:
                        load_ahead(ahead, d)

                windows(pe, step, between, d, ahead)

            block_of(0, None)
            with pe.Fori(0, NB // 2) as pair:
                d = pair * 2 + 1
                block_of(d, 1)
                block_of(d + 1, 0)
            pe.wait_ge(s_staged, NW - 1)
            pe.wait_ge(s_stagedv, NW - 1)
            finish(NB - 1, 3, 0, lambda i: None)

        @block.scalar
        def _(a):
            rounds = Counter(a)
            ahead = windows_ahead(a)
            a.sem_inc(s_n1c, 1)

            def scaled(t, w, j, first):
                n = rounds.next()
                for s in range(2):
                    at = bass.ds(t + s, 1)
                    a.wait_ge(s_lane[s], n)
                    a.wait_ge(s_free[s], n)
                    a.activation(left[s][:, 1, :], left[s][:, COUNT, :], ACT.Copy, scale=g.wpart[1][:, at])
                    a.activation(left[s][:, 2, :], left[s][:, COUNT, :], ACT.Copy,
                                 scale=g.wpart[2][:, at]).then_inc(s_scaled[s], 1)

            def staged(w, j, parity, d, rounds_done):
                bank, weights = staging(a, w, j, parity, d, rounds_done)
                a.activation(weights(20, WIN), by_block(ps[0:B, bank + 1, 0:KW - 500]), ACT.Copy)
                if d is not None:
                    a.wait_ge(s_unstaged, w - (WPB - 2))
                flat = stage[j][:].rearrange("p k h -> p (k h)")
                col = 0
                for k, (off, c0, c1) in enumerate(PIECES[1]):
                    last = a.activation(flat[:, col:col + c1 - c0], ps[0:B, bank + off, c0:c1], ACT.Copy,
                                        accum_out=g.winsum[:, bass.ds(w * 2 + k, 1)])
                    col += c1 - c0
                last.then_inc(s_staged, 1)

            def finish(d, x, between):
                move_transposed(a, lambda out, in_: a.activation(out, in_, ACT.Copy), 1, d, x)
                between()
                a.wait_ge(s_n1, d + 2)
                a.activation(g.n1[:, bass.ds(d, 1), :].rearrange("p a k -> p (a k)"), ps[0:B, 7, 0:D + 1],
                             ACT.Copy).then_inc(s_n1c, 1)

            def block_of(d, parity):
                def between(w, j):
                    before_window(w, j, d, parity, staged, a.snap(rounds.reg))
                    if j == FINISH and parity is None:
                        load_ahead(ahead, d)
                    elif j == FINISH:
                        finish(d - 1, 3 * ((j + parity) % 2), lambda: load_ahead(ahead, d))

                windows(a, scaled, between, d, ahead)

            block_of(0, None)
            with a.Fori(0, NB // 2) as pair:
                d = pair * 2 + 1
                block_of(d, 1)
                block_of(d + 1, 0)
            staged(NW - 1, WPB - 1, 0, NB - 1, rounds.next())
            finish(NB - 1, 3, lambda: None)

        @block.gpsimd
        def _(pool):
            def unstage(w, j):
                pool.wait_ge(s_staged, w + 1)
                pool.sem_inc(s_tick, 1)
                cols = lambda t: t[:, :, j * WIN:(j + 1) * WIN].rearrange("p h k -> p k h")
                pool.tensor_copy(cols(cnt[0]), stage[j][:]).then_inc(s_pool, 1)
                pool.wait_ge(s_pool, w + 1)
                pool.tensor_tensor(cols(cnt[1]), stage[j][:], cols(cnt[0]), ALU.subtract).then_inc(s_unstaged, 1)

            def block_of(d, first):
                if not first:
                    pool.wait_ge(s_cntout, d * 32)
                for j in range(WPB):
                    unstage(d * WPB + j, j)
                pool.wait_ge(s_unstaged, d * WPB + (WPB + 1))
                pool.sem_inc(s_cnt, 1)

            pool.sem_inc(s_unstaged, 1)
            block_of(0, True)
            with pool.Fori(1, NB) as d:
                block_of(d, False)

        @block.sync
        def _(sp):
            load_gate_weights(sp, io, w, s_weights)
            sp.sem_inc(s_adjout, 1)
            with sp.Fori(0, NB) as d:
                built, moved = sp.snap(d + 1), [sp.snap(d * n + n) for n in (EVEN, ODD)]
                sp.wait_ge(s_cnt, built)
                sp.sem_inc(s_tick, 1)
                for i in range(2):
                    sp.dma_start(dr.cnt[i, bass.ds(d, 1), :, :].rearrange("a p n -> p (a n)"),
                                 cnt[i][:].rearrange("p h k -> p (h k)")).then_inc(s_cntout, 16)
                for sem, n in zip(s_moved, moved):
                    sp.wait_ge(sem, n)
                    sp.sem_inc(s_tick, 1)
                sp.dma_start(dr.adj_t[bass.ds(d, 1), :, :].rearrange("a p n -> p (a n)"), adj_t[:]).then_inc(s_adjout, 16)
            sp.wait_ge(s_cntout, NB * 32)
            sp.wait_ge(s_adjout, NB * 16 + 1)
            sp.wait_ge(s_weights, 7 * 16)


class Obj:
    pass


def program(nc, io, out):
    ctx = ExitStack()
    Phase.used.clear()
    with ctx:
        def sb(name, shape, dt=F32):
            return ctx.enter_context(nc.sbuf_tensor(name, shape, dt))

        g, dr, w = Obj(), Obj(), Obj()
        dr.cnt = nc.dram_tensor("cnt_panels", (2, NB, B, N), BF16, kind="Internal").ap()
        dr.adj_t = nc.dram_tensor("adj_rows", (NB, B, N), F32, kind="Internal").ap()
        dr.table = nc.dram_tensor("src_table", (N, D), F32, kind="Internal").ap()
        g.x = sb("x", [B, NB, D])
        g.h = sb("h", [B, NB, D + 1])
        g.ident = sb("ident", [128, 128])
        g.dst = sb("dst", [128, NT])
        g.src_idx = sb("src_idx", [128, NT], I32)
        g.ea = sb("ea", [128, NT])
        g.block_base = sb("block_base", [128, NB])
        g.bounds = sb("bounds", [1, 256], I32)
        g.n1 = sb("n1", [B, NB, D + 1])
        g.wsum_src = sb("wsum_src", [B, NB])
        g.winsum = sb("winsum", [B, 2 * NW])
        g.deg = sb("deg", [B, NB])
        g.bias_rows = sb("bias_rows", [3, BIAS_MESSAGE + D], BF16)
        with ExitStack() as gates:
            def sb_gates(name, shape, dt=F32):
                return gates.enter_context(nc.sbuf_tensor(name, shape, dt))

            w.sides = [sb_gates(f"w_side{i}", [D, D]) for i in range(2)]
            w.ih = sb_gates("w_ih", [128, 3, 2 * D])
            w.hh = sb_gates("w_hh", [128, 3, D])
            w.bih = sb_gates("w_bih", [3, 3 * D])
            w.bhh = sb_gates("w_bhh", [3, 3 * D])
            w.alpha = sb_gates("w_alpha", [B, 4])
            with ExitStack() as building:
                def sb_build(name, shape, dt=F32):
                    return building.enter_context(nc.sbuf_tensor(name, shape, dt))

                g.key_id = sb_build("key_id", [128, KEVEN], F16)
                g.key = sb_build("key", [128, NT])
                g.win_base = sb_build("win_base", [128, NW])
                g.lane = sb_build("lane", [128, NT])
                g.wpart = [sb_build(f"wpart{i}", [128, NT]) for i in range(3)]
                setup_phase(nc, g, io)
                build_phase(nc, g, dr, io, w)
            gate_and_propagation(nc, g, dr, io, w)
        attention_and_messages(nc, g, dr, io, out)


def bias_rows(nc, g, io, w, ph):
    n = g.bias_rows.shape[1]
    left, part, kept = (ph.sb(name, [3, n]) for name in ("bias_left", "bias_part", "bias_kept"))
    cut = ph.sb("bias_cut", [3, n], BF16)
    s_bin = ph.sem("bin")
    s_bias = ph.sem("bias")

    def run(pool):
        for at, name in ((BIAS_QK, "Wq_b"), (BIAS_QK + HEADS * D, "Wk_b"), (BIAS_MESSAGE, "mb1")):
            k = D if name == "mb1" else HEADS * D
            pool.dma_start(left[:, at:at + k],
                           io[name].rearrange("(a k) -> a k", a=1).to_broadcast([3, k])).then_inc(s_bin, 16)
        do = Chain(pool, s_bias)
        do(pool.tensor_copy(left[:, 0:3 * D], w.brow[:]))
        do(pool.tensor_copy(left[:, 3 * D:4 * D], w.bhh[:, 2 * D:3 * D]))
        pool.wait_ge(s_bin, 48)
        for i in range(3):
            do(pool.tensor_copy(cut[:], left[:]))
            do(pool.tensor_copy(part[:], cut[:]))
            if i < 2:
                do(pool.tensor_tensor(left[:], left[:], part[:], ALU.subtract))
            do(pool.tensor_scalar(part[:], part[:], g.ident[0:3, i:i + 1], None, ALU.mult))
            do(pool.tensor_copy(kept[:], part[:]) if i == 0 else
               pool.tensor_tensor(kept[:], kept[:], part[:], ALU.add))
        do(pool.tensor_copy(g.bias_rows[:], kept[:]))

    return run


def spmm_t_phase(nc, g, dr, name, y_in, y, hops, scale=None, alpha=None, aside=None,
                 normed=False):
    R = 5
    STEPS = NB // R
    with Phase(nc, name) as ph:
        rows = [ph.sb(f"rows{i}", [B, N]) for i in range(R)]
        y_one = [ph.sb(f"y_one{i}", [B, D]) for i in range(R)]
        y_t = ph.sb("y_t", [D, N])
        ps = ph.ps()
        s_row = [ph.sem(f"row{i}") for i in range(R)]
        s_used = [ph.sem(f"used{i}") for i in range(R)]
        s_one = [ph.sem(f"one{i}") for i in range(R)]
        s_tick = ph.sem("tick")
        s_sum = ph.sem("sum")
        s_tc = [ph.sem(f"tc{i}") for i in range(2)]
        s_tr = ph.sem("tr")
        s_y = [ph.sem(f"y{i}") for i in range(2)]
        s_x = ph.sem("x")
        NG = len(GROUPS)
        CHUNKS_OF = [(len(CHUNKS) + 1 - i) // 2 for i in range(2)]
        GROUPS_OF = [(NG + 1 - i) // 2 for i in range(2)]
        beside = aside(ph) if aside else None
        norm = Norm(ph, g.x, y_in) if normed else None
        block = ph.ctx.enter_context(nc.Block())

        if beside:
            @block.gpsimd
            def _(pool):
                beside(pool)

        def moved_back(eng, copy, hop, part):
            eng.wait_ge(s_sum, hop + 1)
            for k in range(part, len(CHUNKS), 2):
                c, n = CHUNKS[k]
                copy(y_t[:, c:c + n], ps[:, k, 0:n]).then_inc(s_tc[part], 1)
            for k in range(part, NG, 2):
                b0, n = GROUPS[k]
                eng.wait_ge(s_tr, hop * NG + (k + 1))
                if alpha is not None and k < 2:
                    eng.wait_ge(s_x, hop + 1)
                copy(y[:, b0:b0 + n, 0:D],
                     ps[0:B, k, 0:n * D].rearrange("p (a k) -> p a k", k=D)).then_inc(s_y[part], 1)

        @block.sync
        def _(sp):
            with sp.Fori(0, hops) as hop:
                with sp.Fori(0, STEPS) as o:
                    for i in range(R):
                        sp.wait_ge(s_used[i], sp.snap(hop * STEPS + o + 1))
                        sp.sem_inc(s_tick, 1)
                        sp.dma_start(rows[i][:], dr.adj_t[bass.ds(o * R + i, 1), :, :]
                                     .rearrange("a p n -> p (a n)")).then_inc(s_row[i], 16)

        @block.scalar
        def _(a):
            def ones(hop, o):
                for i in range(R):
                    a.wait_ge(s_used[i], a.snap(hop * STEPS + o + 1))
                    a.activation(y_one[i][:], y_in[:, bass.ds(o * R + i, 1), 0:D].rearrange("p a k -> p (a k)"),
                                 ACT.Copy).then_inc(s_one[i], 1)

            def hop_of(hop):
                with a.Fori(0, STEPS) as o:
                    ones(hop, o)
                moved_back(a, lambda out, in_: a.activation(out, in_, ACT.Copy), hop, 0)

            if norm:
                norm.scalar(a)
                norm.wait(a)
            hop_of(0)
            if hops > 1:
                with a.Fori(1, hops) as hop:
                    for part in range(2):
                        a.wait_ge(s_y[part], hop * GROUPS_OF[part])
                    hop_of(hop)

        @block.tensor
        def _(pe):
            for i in range(R):
                pe.sem_inc(s_used[i], 1)

            def products(hop, o, first):
                for i in range(R):
                    pe.wait_ge(s_row[i], (hop * STEPS + o + 1) * 16)
                    pe.wait_ge(s_one[i], hop * STEPS + o + 1)
                    for k, (c, n) in enumerate(CHUNKS):
                        last = pe.matmul(ps[:, k, 0:n], y_one[i][:], rows[i][:, c:c + n], start=first and i == 0,
                                         stop=False, skip_group_check=True)
                    last.then_inc(s_used[i], 1)

            with pe.Fori(0, hops) as hop:
                products(hop, 0, True)
                with pe.Fori(1, STEPS) as o:
                    products(hop, o, False)
                pe.drain().then_inc(s_sum, 1)
                for part in range(2):
                    pe.wait_ge(s_tc[part], (hop + 1) * CHUNKS_OF[part])
                for k, (b0, n) in enumerate(GROUPS):
                    for j in range(n):
                        last = pe.transpose(ps[0:B, k, j * D:(j + 1) * D], y_t[:, (b0 + j) * B:(b0 + j + 1) * B], g.ident[:])
                    last.then_inc(s_tr, 1)
                for part in range(2):
                    pe.wait_ge(s_y[part], (hop + 1) * GROUPS_OF[part])

        @block.vector
        def _(v):
            if norm:
                norm.vector(v)
                norm.wait(v)
            if alpha is not None:
                v.scalar_tensor_tensor(g.x[:], y_in[:, :, 0:D], alpha[:, 0:1], g.x[:], ALU.mult, ALU.add).then_inc(s_x, 1)
            with v.Fori(0, hops) as hop:
                moved_back(v, v.tensor_copy, hop, 1)
                for part in range(2):
                    v.wait_ge(s_y[part], (hop + 1) * GROUPS_OF[part])
                if scale is not None:
                    v.tensor_tensor(y[:, :, 0:D], y[:, :, 0:D], bc(scale, D), ALU.mult)
                if alpha is not None:
                    v.wait_ge(s_x, hop + 1)
                    v.scalar_tensor_tensor(g.x[:], y[:, :, 0:D], alpha[:, bass.ds(hop + 1, 1)], g.x[:], ALU.mult,
                                           ALU.add).then_inc(s_x, 1)


def transposed(pe, ps, bank, in_, ident, blocks, sem):
    for j, b in enumerate(blocks):
        last = pe.transpose(ps[:, bank, j * B:(j + 1) * B], in_(b), ident[0:B, 0:B])
    last.then_inc(sem, 1)


def load_gate_weights(sp, io, w, sem):
    for out, in_ in ((w.sides[0], io["W1"]), (w.sides[1], io["W2"]),
                     (w.ih, io["w_ih"].rearrange("(t p) k -> p t k", p=128)),
                     (w.hh, io["w_hh"].rearrange("(t p) k -> p t k", p=128)),
                     (w.bih, io["b_ih"].rearrange("(a k) -> a k", a=1).to_broadcast([3, 3 * D])),
                     (w.bhh, io["b_hh"].rearrange("(a k) -> a k", a=1).to_broadcast([3, 3 * D])),
                     (w.alpha, io["alpha"].rearrange("(a k) -> a k", a=1).to_broadcast([B, 4]))):
        sp.dma_start(out[:], in_).then_inc(sem, 16)


def weights_phase(nc, g, io, w):
    with Phase(nc, "gruw") as ph:
        wih_t = ph.sb("wih_t", [128, 2, 3 * D])
        ps = ph.ps()
        s_tr = ph.sem("tr")
        s_c = ph.sem("c")
        s_m = ph.sem("m")
        s_d = ph.sem("d")
        block = ph.ctx.enter_context(nc.Block())

        @block.tensor
        def _(pe):
            for i in range(2):
                for t in range(3):
                    last = pe.transpose(ps[:, i, t * D:(t + 1) * D], w.ih[:, t, i * D:(i + 1) * D], g.ident[:])
                last.then_inc(s_tr, 1)
            for t in range(3):
                last = pe.transpose(ps[:, 2, t * D:(t + 1) * D], w.hh[:, t, :], g.ident[:])
            last.then_inc(s_tr, 1)
            pe.wait_ge(s_c, 3)
            for i in range(2):
                last = pe.matmul(ps[:, 3 + i, 0:3 * D], w.sides[i][:], wih_t[:, i, :], start=True, stop=True)
            last.then_inc(s_m, 1)

        @block.vector
        def _(v):
            v.wait_ge(s_tr, 3)
            for i in range(2):
                v.tensor_copy(wih_t[:, i, :], ps[:, i, 0:3 * D]).then_inc(s_c, 1)
            v.tensor_copy(w.whh_t[:], ps[:, 2, 0:3 * D]).then_inc(s_c, 1)
            do = Chain(v, s_d)
            do(v.tensor_tensor(w.brow[:, 0:2 * D], w.bih[:, 0:2 * D], w.bhh[:, 0:2 * D], ALU.add))
            do(v.tensor_copy(w.brow[:, 2 * D:3 * D], w.bih[:, 2 * D:3 * D]))
            v.wait_ge(s_m, 1)
            for i in range(2):
                v.tensor_copy(w.m[:, i, :], ps[:, 3 + i, 0:3 * D])
            do(v.tensor_reduce(w.sums[:, 0:1], w.alpha[:], AX.X, ALU.max))
            v.tensor_scalar(w.alpha[:], w.alpha[:], w.sums[:, 0:1], None, ALU.subtract).then_inc(s_c, 1)
            v.wait_ge(s_c, 5)
            do(v.tensor_reduce(w.sums[:, 0:1], w.alpha[:], AX.X, ALU.add))
            do(v.reciprocal(w.sums[:, 1:2], w.sums[:, 0:1]))
            do(v.tensor_scalar(w.alpha[:], w.alpha[:], w.sums[:, 1:2], None, ALU.mult))
            for sums, out in ((g.wsum_src[:], w.r_src[:]), (g.n1[:, :, D], w.r_dst[:])):
                do(v.tensor_scalar(w.pos[:], sums, 0.0, None, ALU.is_gt))
                do(v.tensor_tensor(out, sums, w.pos[:], ALU.mult))
                do(v.tensor_scalar(w.neg[:], w.pos[:], -1.0, 1.0, ALU.mult, ALU.add))
                do(v.tensor_tensor(out, out, w.neg[:], ALU.add))
                do(v.reciprocal(out, out))
                do(v.tensor_tensor(out, out, w.pos[:], ALU.mult))
            do(v.tensor_tensor(g.n1[:, :, 0:D], g.n1[:, :, 0:D], bc(w.r_dst[:], D), ALU.mult))

        @block.scalar
        def _(a):
            a.wait_ge(s_c, 4)
            a.activation(w.alpha[:], w.alpha[:], ACT.Exp).then_inc(s_c, 1)


def gru_phase(nc, g, w, n2):
    with Phase(nc, "gru") as ph:
        tr = [ph.sb(f"tr{i}", [D, N]) for i in range(3)]
        rz = ph.sb("rz", [B, NB, 2 * D])
        t = ph.sb("t", [B, NB, D])
        ones = ph.sb("ones", [3, B], BF16)
        ps = ph.ps()
        s_one = ph.sem("one")
        s_tr = ph.sem("tr")
        s_c = [ph.sem(f"c{i}") for i in range(2)]
        s_g = ph.sem("g")
        s_sig = ph.sem("sig")
        s_t = ph.sem("t")
        s_nn = ph.sem("nn")
        s_d = ph.sem("d")
        block = ph.ctx.enter_context(nc.Block())
        jobs = [(i, b0, n) for i in range(3) for b0, n in GROUPS]
        srcs = [g.n1, n2, g.h]
        even, odd = (len(jobs) + 1) // 2, len(jobs) // 2

        @block.tensor
        def _(pe):
            for k, (i, b0, n) in enumerate(jobs):
                if k >= 8:
                    pe.wait_ge(s_c[k % 2], (k - 8) // 2 + 1)
                transposed(pe, ps, k % 8, lambda b: srcs[i][:, b, 0:D], g.ident, range(b0, b0 + n), s_tr)
            pe.wait_ge(s_c[0], even)
            pe.wait_ge(s_c[1], odd)
            pe.wait_ge(s_one, 1)
            for b in range(NB):
                at = slice(b * B, (b + 1) * B)
                p, q = 2 * (b % 3), 2 * (b % 3) + 1
                if b >= 3:
                    pe.wait_ge(s_t, b - 2)
                pe.matmul(ps[0:B, p, 0:3 * D], tr[0][:, at], w.m[:, 0, :], start=True, stop=False)
                pe.matmul(ps[0:B, p, 0:3 * D], tr[1][:, at], w.m[:, 1, :], start=False, stop=False)
                pe.matmul(ps[0:B, p, 0:2 * D], tr[2][:, at], w.whh_t[:, 0:2 * D], start=False, stop=False)
                pe.matmul(ps[0:B, p, 0:3 * D], ones[:], g.bias_rows[:, 0:3 * D], start=False, stop=True)
                pe.matmul(ps[0:B, q, 0:D], tr[2][:, at], w.whh_t[:, 2 * D:3 * D], start=True, stop=False)
                pe.matmul(ps[0:B, q, 0:D], ones[:], g.bias_rows[:, 3 * D:4 * D], start=False, stop=True).then_inc(s_g, 1)

        @block.scalar
        def _(a):
            for k, (i, b0, n) in enumerate(jobs):
                if k % 2 == 0:
                    a.wait_ge(s_tr, k + 1)
                    a.activation(tr[i][:, b0 * B:(b0 + n) * B], ps[:, k % 8, 0:n * B], ACT.Copy).then_inc(s_c[0], 1)
            for b in range(NB):
                a.wait_ge(s_g, b + 1)
                a.activation(rz[:, b, :], ps[0:B, 2 * (b % 3), 0:2 * D], ACT.Sigmoid).then_inc(s_sig, 1)
            a.wait_ge(s_t, NB)
            a.activation(t[:], t[:], ACT.Tanh).then_inc(s_nn, 1)

        @block.vector
        def _(v):
            v.memset(ones[:], 1.0).then_inc(s_one, 1)
            for k, (i, b0, n) in enumerate(jobs):
                if k % 2 == 1:
                    v.wait_ge(s_tr, k + 1)
                    v.tensor_copy(tr[i][:, b0 * B:(b0 + n) * B], ps[:, k % 8, 0:n * B]).then_inc(s_c[1], 1)
            do = Chain(v, s_d)
            for b in range(NB):
                v.wait_ge(s_sig, b + 1)
                do(v.tensor_tensor(t[:, b, :], rz[:, b, 0:D], ps[0:B, 2 * (b % 3) + 1, 0:D], ALU.mult))
                v.tensor_tensor(t[:, b, :], t[:, b, :], ps[0:B, 2 * (b % 3), 2 * D:3 * D], ALU.add).then_inc(s_t, 1)
            v.wait_ge(s_nn, 1)
            do(v.tensor_tensor(rz[:, :, 0:D], g.h[:, :, 0:D], t[:], ALU.subtract))
            do(v.tensor_tensor(rz[:, :, 0:D], rz[:, :, 0:D], rz[:, :, D:2 * D], ALU.mult))
            do(v.tensor_tensor(g.x[:], g.x[:], t[:], ALU.add))
            do(v.tensor_tensor(g.x[:], g.x[:], rz[:, :, 0:D], ALU.add))


def query_key_phase(nc, g, io, a2):
    with Phase(nc, "qk") as ph:
        h_t = ph.sb("h_t", [D, N])
        wqk = ph.sb("wqk", [D, 2, HEADS * D])
        q = ph.sb("q", [B, NB, HEADS * D])
        sq = ph.sb("sq", [B, 2, HEADS * D])
        nrm = ph.sb("nrm", [B, 2, NB, HEADS])
        inv = ph.sb("inv", [B, 2, NB, HEADS])
        ones = ph.sb("ones", [B, 1])
        onerow = ph.sb("onerow", [3, B], BF16)
        ksum = ph.sb("ksum", [D, HEADS])
        ps = ph.ps()
        s_in = ph.sem("in")
        s_one = ph.sem("one")
        s_wo = ph.sem("wo")
        s_tr = ph.sem("tr")
        s_c = [ph.sem(f"c{i}") for i in range(2)]
        s_q = ph.sem("q")
        s_qc = ph.sem("qc")
        s_sq = ph.sem("sq")
        s_n = ph.sem("n")
        s_unit = ph.sem("unit")
        s_qt = ph.sem("qt")
        s_qtc = [ph.sem(f"qtc{i}") for i in range(2)]
        s_ks = ph.sem("ks")
        s_ksc = ph.sem("ksc")
        s_den = ph.sem("den")
        s_d = ph.sem("d")
        norm = Norm(ph, g.x, g.h)
        block = ph.ctx.enter_context(nc.Block())
        jobs = [(h, b0, n) for b0, n in GROUPS for h in range(HEADS)]
        HALF = 12

        @block.sync
        def _(sp):
            for i, n in enumerate(("Wq", "Wk")):
                sp.dma_start(wqk[:, i, :], io[n + "_w"]).then_inc(s_in, 16)
            sp.dma_start(a2.wo[:], io["Wo_w"].rearrange("(t p) k -> p t k", p=D)).then_inc(s_wo, 16)
            sp.dma_start(a2.wob[:], io["Wo_b"].rearrange("(a k) -> a k", a=1).to_broadcast([B, D])).then_inc(s_wo, 16)
            sp.wait_ge(s_wo, 32)

        @block.tensor
        def _(pe):
            norm.wait(pe)
            for k, (b0, n) in enumerate(GROUPS):
                transposed(pe, ps, k, lambda b: g.h[:, b, 0:D], g.ident, range(b0, b0 + n), s_tr)
            pe.wait_ge(s_c[0], 4)
            pe.wait_ge(s_c[1], 3)
            pe.wait_ge(s_in, 32)
            pe.wait_ge(s_one, 2)
            for b in range(NB):
                if b >= 4:
                    pe.wait_ge(s_qc, b - 3)
                for i in range(2):
                    at = slice(i * HEADS * D, (i + 1) * HEADS * D)
                    pe.matmul(ps[0:B, b % 4, at], h_t[:, b * B:(b + 1) * B], wqk[:, i, :], start=True, stop=False)
                    last = pe.matmul(ps[0:B, b % 4, at], onerow[:],
                                     g.bias_rows[:, BIAS_QK + at.start:BIAS_QK + at.stop], start=False, stop=True)
                last.then_inc(s_q, 1)
            pe.wait_ge(s_unit, 1)
            pe.wait_ge(s_qc, NB)
            for h in range(HEADS):
                for b in range(NB):
                    last = pe.matmul(ps[:, 7, h:h + 1], a2.ks[:, b, h * D:(h + 1) * D], ones[:], start=b == 0,
                                     stop=b == NB - 1)
            last.then_inc(s_ks, 1)
            for k, (h, b0, n) in enumerate(jobs):
                pe.wait_ge(s_unit, 2 if b0 < HALF else 3)
                if k >= 4:
                    pe.wait_ge(s_qtc[k % 2], (k - 4) // 2 + 1)
                transposed(pe, ps, k % 4, lambda b: q[:, b, h * D:(h + 1) * D], g.ident, range(b0, b0 + n), s_qt)
            pe.wait_ge(s_qtc[0], 7)
            pe.wait_ge(s_qtc[1], 7)
            pe.wait_ge(s_ksc, 1)
            for b in range(NB):
                for h in range(HEADS):
                    last = pe.matmul(ps[0:B, 6, b * HEADS + h:b * HEADS + h + 1], a2.qs_t[:, h, b * B:(b + 1) * B],
                                     ksum[:, h:h + 1], start=True, stop=True)
            last.then_inc(s_den, 1)

        @block.scalar
        def _(a):
            norm.scalar(a)
            for k, (b0, n) in enumerate(GROUPS):
                if k % 2 == 0:
                    a.wait_ge(s_tr, k + 1)
                    a.activation(h_t[:, b0 * B:(b0 + n) * B], ps[:, k, 0:n * B], ACT.Copy).then_inc(s_c[0], 1)
            for b in range(NB):
                a.wait_ge(s_q, b + 1)
                if b:
                    a.wait_ge(s_sq, b)
                for i in range(2):
                    for h in range(HEADS):
                        at = (i * HEADS + h) * D
                        last = a.activation(sq[:, i, h * D:(h + 1) * D], ps[0:B, b % 4, at:at + D], ACT.Square,
                                            accum_out=nrm[:, i, b, h:h + 1])
                last.then_inc(s_sq, 1)
            a.wait_ge(s_sq, NB)
            a.activation(nrm[:], nrm[:], ACT.Sqrt).then_inc(s_n, 1)
            for k, (h, b0, n) in enumerate(jobs):
                if k % 2 == 0:
                    a.wait_ge(s_qt, k + 1)
                    a.activation(a2.qs_t[:, h, b0 * B:(b0 + n) * B], ps[:, k % 4, 0:n * B], ACT.Copy).then_inc(s_qtc[0], 1)

        @block.vector
        def _(v):
            do = Chain(v, s_d)
            v.memset(ones[:], 1.0).then_inc(s_one, 1)
            v.memset(onerow[:], 1.0).then_inc(s_one, 1)
            norm.vector(v)
            norm.wait(v)
            for k, (b0, n) in enumerate(GROUPS):
                if k % 2 == 1:
                    v.wait_ge(s_tr, k + 1)
                    v.tensor_copy(h_t[:, b0 * B:(b0 + n) * B], ps[:, k, 0:n * B]).then_inc(s_c[1], 1)
            for b in range(NB):
                v.wait_ge(s_sq, b + 1)
                v.tensor_copy(q[:, b, :], ps[0:B, b % 4, 0:HEADS * D])
                v.tensor_copy(a2.ks[:, b, :], ps[0:B, b % 4, HEADS * D:2 * HEADS * D]).then_inc(s_qc, 1)
            v.wait_ge(s_qc, NB)
            v.wait_ge(s_n, 1)
            do(v.reciprocal(inv[:], nrm[:]))
            for i, t, b0, b1 in ((1, a2.ks, 0, NB), (0, q, 0, HALF), (0, q, HALF, NB)):
                heads = t[:, b0:b1, :].rearrange("p b (h k) -> p (b h) k", h=HEADS)
                v.tensor_tensor(heads, heads, bc(inv[:, i, b0:b1, :].rearrange("p b h -> p (b h)"), D),
                                ALU.mult).then_inc(s_unit, 1)
            v.wait_ge(s_ks, 1)
            v.tensor_copy(ksum[:], ps[:, 7, 0:HEADS]).then_inc(s_ksc, 1)
            for k, (h, b0, n) in enumerate(jobs):
                if k % 2 == 1:
                    v.wait_ge(s_qt, k + 1)
                    v.tensor_copy(a2.qs_t[:, h, b0 * B:(b0 + n) * B], ps[:, k % 4, 0:n * B]).then_inc(s_qtc[1], 1)
            v.wait_ge(s_den, 1)
            do(v.tensor_scalar(a2.rden[:], ps[0:B, 6, 0:NB * HEADS], float(N), None, ALU.add))
            do(v.reciprocal(a2.rden[:], a2.rden[:]))
            for h in range(HEADS):
                v.tensor_copy(a2.t[:, :, h * D:(h + 1) * D], g.h[:, :, 0:D])
            do(v.tensor_reduce(a2.most[:], g.winsum[:], AX.X, ALU.max))


def term_phase(nc, g, dr, a2, k, last_term, panels):
    with Phase(nc, f"term{k}") as ph:
        R = 2
        PER = 5
        CUTS = 0 if last_term else NB // PER
        W = HEADS * D
        NG = len(GROUPS)
        t_t = ph.sb("t_t", [D, 4, 4 * B])
        rest = [ph.sb(f"rest{i}", [B, PER, W]) for i in range(R)]
        by_group = ph.sb("by_group", [D, HEADS, NG])
        vs = ph.sb("vs", [D, HEADS])
        vs_part = ph.sb("vs_part", [D, HEADS, 3])
        vs_bf = ph.sb("vs_bf", [D, HEADS], BF16)
        row = ph.sb("row", [1, B])
        most = ph.sb("most", [1, 1])
        ps = ph.ps()
        s_most = ph.sem("most")
        s_flag = ph.sem("flag")
        s_tr = ph.sem("tr")
        s_tc = ph.sem("tc")
        s_y = ph.sem("y")
        s_yc = ph.sem("yc")
        s_kv = ph.sem("kv")
        s_part = [ph.sem(f"part{p}") for p in range(3)]
        s_rest = [ph.sem(f"rest{p}") for p in range(2)]
        s_vs = ph.sem("vs")
        s_row = ph.sem("row")
        s_d = ph.sem("d")
        block = ph.ctx.enter_context(nc.Block())

        def cut(i):
            return slice(PER * i, PER * i + PER)

        if not last_term:
            @block.sync
            def _(sp):
                for i in range(EARLY):
                    sp.dma_start(panels.buf[i][:], dr.cnt[0, i, :, :]).then_inc(panels.s_in[i], 16)

        @block.tensor
        def _(pe):
            def project(i, b0, n):
                pe.wait_ge(s_tc, 2 * i + 2)
                if i >= 2:
                    pe.wait_ge(s_yc, i - 1)
                for j in range(n):
                    for h in range(HEADS):
                        last = pe.matmul(ps[0:B, 4 + i % 2, j * D:(j + 1) * D],
                                         t_t[:, 2 * (i % 2) + h, j * B:(j + 1) * B],
                                         a2.wo[:, h * (ORDER + 1) + k, :], start=h == 0, stop=h == HEADS - 1)
                last.then_inc(s_y, 1)

            if k == 0:
                pe.transpose(ps[0:1, 7, W:W + B], a2.most[:], g.ident[0:B, 0:B]).then_inc(s_most, 1)
            for i, (b0, n) in enumerate(GROUPS):
                for h in range(HEADS):
                    transposed(pe, ps, 2 * (i % 2) + h, lambda b: a2.t[:, b, h * D:(h + 1) * D], g.ident,
                               range(b0, b0 + n), s_tr)
                if i:
                    project(i - 1, *GROUPS[i - 1])
            project(NG - 1, *GROUPS[-1])
            if not last_term:
                for h in range(HEADS):
                    for b in range(NB):
                        last = pe.matmul(ps[:, 6, h * D:(h + 1) * D], a2.ks[:, b, h * D:(h + 1) * D],
                                         a2.t[:, b, h * D:(h + 1) * D], start=b == 0, stop=b == NB - 1)
                last.then_inc(s_kv, 1)
                pe.wait_ge(s_vs, 1)
                for h in range(HEADS):
                    last = pe.transpose(ps[0:3, 7, h * D:(h + 1) * D], vs_part[:, h, :], g.ident[:])
                last.then_inc(s_row, 1)

        @block.scalar
        def _(a):
            for i in range(NG):
                b0, n = GROUPS[i]
                for h in range(HEADS):
                    a.wait_ge(s_tr, 2 * i + h + 1)
                    if i >= 2:
                        a.wait_ge(s_y, i - 1)
                    a.activation(t_t[:, 2 * (i % 2) + h, 0:n * B], ps[:, 2 * (i % 2) + h, 0:n * B],
                                 ACT.Copy, accum_out=by_group[:, h, i:i + 1]).then_inc(s_tc, 1)
                if i < CUTS:
                    a.activation(a2.xp[:, cut(i), 0, 0:W], a2.t[:, cut(i), 0:W], ACT.Copy).then_inc(s_part[0], 1)
                for p in (1, 2):
                    if 0 <= i - p < CUTS:
                        a.wait_ge(s_rest[p - 1], i - p + 1)
                        a.activation(a2.xp[:, cut(i - p), p, 0:W], rest[(i - p) % R][:], ACT.Copy).then_inc(s_part[p], 1)

        @block.gpsimd
        def _(pool):
            if k == 0:
                pool.memset(a2.xp[:, :, 0, W:W + 1], 1.0)

        @block.vector
        def _(v):
            do = Chain(v, s_d)

            def add_projection(i):
                b0, n = GROUPS[i]
                v.wait_ge(s_y, i + 1)
                blocks = ps[0:B, 4 + i % 2, 0:n * D].rearrange("p (a k) -> p a k", k=D)
                if k == 0:
                    v.tensor_copy(a2.y[:, b0:b0 + n, :], blocks).then_inc(s_yc, 1)
                else:
                    v.tensor_tensor(a2.y[:, b0:b0 + n, :], a2.y[:, b0:b0 + n, :], blocks, ALU.add).then_inc(s_yc, 1)

            for i in range(NG + 1):
                if i < CUTS:
                    v.wait_ge(s_part[0], i + 1)
                    if i >= R:
                        v.wait_ge(s_part[2], i - R + 1)
                    v.tensor_tensor(rest[i % R][:], a2.t[:, cut(i), 0:W], a2.xp[:, cut(i), 0, 0:W],
                                    ALU.subtract).then_inc(s_rest[0], 1)
                if 0 <= i - 1 < CUTS:
                    v.wait_ge(s_part[1], i)
                    v.tensor_tensor(rest[(i - 1) % R][:], rest[(i - 1) % R][:], a2.xp[:, cut(i - 1), 1, 0:W],
                                    ALU.subtract).then_inc(s_rest[1], 1)
                if i:
                    add_projection(i - 1)
            if k == 0:
                v.wait_ge(s_most, 1)
                do(v.tensor_copy(row[:], ps[0:1, 7, W:W + B]))
                do(v.tensor_reduce(most[:], row[:], AX.X, ALU.max))
                do(v.tensor_scalar(most[:], most[:], 256.0, 1.0, ALU.is_gt, ALU.add))
                v.tensor_copy(a2.nparts[:], most[:]).then_inc(s_flag, 1)
                v.wait_ge(s_flag, 1)
            if not last_term:
                v.wait_ge(s_tc, HEADS * NG)
                do(v.tensor_reduce(vs[:], by_group[:], AX.X, ALU.add))
                for p in range(3):
                    do(v.tensor_copy(vs_bf[:], vs[:]))
                    do(v.tensor_copy(vs_part[:, :, p], vs_bf[:]))
                    if p < 2:
                        do(v.tensor_tensor(vs[:], vs[:], vs_part[:, :, p], ALU.subtract))
                v.sem_inc(s_vs, 1)
                v.wait_ge(s_kv, 1)
                v.tensor_copy(a2.kv[:], ps[:, 6, 0:W])
                v.wait_ge(s_row, 1)
                do(v.tensor_copy(a2.vsum[:], ps[0:3, 7, 0:W]))
            else:
                v.wait_ge(s_yc, NG)
                do(v.tensor_tensor(a2.y[:], a2.y[:], a2.wob[:].unsqueeze(1).to_broadcast([B, NB, D]), ALU.add))
                do(v.scalar_tensor_tensor(g.x[:], a2.y[:], 1.0 / HEADS, g.x[:], ALU.mult, ALU.add))


def count_phase(nc, g, dr, a2, k, panels):
    R = PANELS
    STEPS = NB // R
    W = HEADS * D
    lo = D if k == 0 else 0
    with Phase(nc, f"count{k}") as ph:
        panel = panels.buf + [ph.sb(f"panel{i}", [B, N], BF16) for i in range(EARLY, R)]
        s_in = panels.s_in
        ps = ph.ps()
        s_zero = ph.sem("zero")
        s_used = [ph.sem(f"used{i}") for i in range(R)]
        s_added = [ph.sem(f"added{i}") for i in range(R)]
        s_tick = ph.sem("tick")
        block = ph.ctx.enter_context(nc.Block())

        @block.gpsimd
        def _(pool):
            pool.memset(a2.t[:], 0.0).then_inc(s_zero, 1)

        @block.sync
        def _(sp):
            nparts = sp.value_load(a2.nparts[0:1, 0:1], min_val=1, max_val=2)
            for i in range(EARLY, R):
                sp.dma_start(panel[i][:], dr.cnt[0, i, :, :]).then_inc(s_in[i], 16)
            rows = dr.cnt.rearrange("q a p n -> (q a) p n")
            with sp.Fori(1, nparts * STEPS) as step:
                for i in range(R):
                    sp.wait_ge(s_used[i], step)
                    sp.sem_inc(s_tick, 1)
                    sp.dma_start(panel[i][:], rows[bass.ds(step * R + i, 1), :, :]
                                 .rearrange("a p n -> p (a n)")).then_inc(s_in[i], 16)

        @block.tensor
        def _(pe):
            nparts = pe.value_load(a2.nparts[0:1, 0:1], min_val=1, max_val=2)
            rounds = Counter(pe)
            for i in range(R):
                pe.sem_inc(s_added[i], 1)
            with pe.Fori(0, nparts):
                with pe.Fori(0, STEPS):
                    n = rounds.next()
                    landed = pe.snap(n * 16)
                    for i in range(R):
                        pe.wait_ge(s_in[i], landed)
                        pe.wait_ge(s_added[i], n)
                        for b in range(NB):
                            for p in range(3):
                                hi = W + 1 if p == 0 else W
                                last = pe.matmul(ps[0:B, i, lo:hi], panel[i][:, b * B:(b + 1) * B],
                                                 a2.xp[:, b, p, lo:hi], start=b == 0 and p == 0,
                                                 stop=b == NB - 1 and p == 2, skip_group_check=True)
                        last.then_inc(s_used[i], 1)

        @block.vector
        def _(v):
            nparts = v.value_load(a2.nparts[0:1, 0:1], min_val=1, max_val=2)
            rounds = Counter(v)
            v.wait_ge(s_zero, 1)
            with v.Fori(0, nparts):
                with v.Fori(0, STEPS) as o:
                    n = rounds.next()
                    used = n
                    for i in range(R):
                        at = a2.t[:, bass.ds(o * R + i, 1), lo:W + 1].rearrange("p a k -> p (a k)")
                        v.wait_ge(s_used[i], used)
                        v.tensor_tensor(at, at, ps[0:B, i, lo:W + 1], ALU.add).then_inc(s_added[i], 1)


def combine_phase(nc, g, a2, k):
    W = HEADS * D
    with Phase(nc, f"comb{k}") as ph:
        pos = ph.sb("pos", [B, NB])
        neg = ph.sb("neg", [B, NB])
        onerow = ph.sb("onerow", [3, B], BF16)
        ps = ph.ps()
        s_one = ph.sem("one")
        s_at = ph.sem("at")
        s_free = ph.sem("free")
        s_d = ph.sem("d")
        block = ph.ctx.enter_context(nc.Block())
        K = 8

        @block.tensor
        def _(pe):
            pe.wait_ge(s_one, 1)
            for b in range(NB):
                if b >= K:
                    pe.wait_ge(s_free, b - K + 1)
                pe.matmul(ps[0:B, b % K, 0:W], onerow[:], a2.vsum[:], start=True, stop=False, skip_group_check=True)
                for h in range(HEADS):
                    at = slice(h * D, (h + 1) * D)
                    last = pe.matmul(ps[0:B, b % K, at], a2.qs_t[:, h, b * B:(b + 1) * B], a2.kv[:, at], start=False,
                                     stop=True, skip_group_check=True)
                last.then_inc(s_at, 1)

        @block.vector
        def _(v):
            do = Chain(v, s_d)
            v.memset(onerow[:], 1.0).then_inc(s_one, 1)
            if k == 0:
                do(v.tensor_copy(g.deg[:], a2.t[:, :, W]))
                do(v.tensor_scalar(pos[:], g.deg[:], 0.0, None, ALU.is_gt))
                do(v.tensor_scalar(neg[:], pos[:], -1.0, 1.0, ALU.mult, ALU.add))
                do(v.tensor_tensor(neg[:], neg[:], g.deg[:], ALU.add))
                do(v.reciprocal(neg[:], neg[:]))
                do(v.scalar_tensor_tensor(a2.half_inv[:], neg[:], 0.5, pos[:], ALU.mult, ALU.mult))
            both = slice(D if k == 0 else 0, W)
            do(v.tensor_tensor(a2.t[:, :, both], a2.t[:, :, both], bc(a2.half_inv[:], W - both.start), ALU.mult))
            for b in range(NB):
                v.wait_ge(s_at, b + 1)
                for h in range(HEADS):
                    at = slice(h * D, (h + 1) * D)
                    last = v.scalar_tensor_tensor(a2.t[:, b, at], ps[0:B, b % K, at],
                                                  a2.rden[:, b * HEADS + h:b * HEADS + h + 1],
                                                  a2.t[:, b, D:W] if k == 0 else a2.t[:, b, at],
                                                  ALU.mult, ALU.add)
                last.then_inc(s_free, 1)


def message_table_phase(nc, g, dr, io, a3):
    with Phase(nc, "table") as ph:
        w1 = ph.sb("w1", [D, 2, D])
        onerow = ph.sb("onerow", [3, B], BF16)
        src = ph.sb("src", [B, NB, D])
        ps = ph.ps()
        s_in = ph.sem("in")
        s_one = ph.sem("one")
        s_tr = ph.sem("tr")
        s_c = [ph.sem(f"c{i}") for i in range(2)]
        s_p = ph.sem("p")
        s_pc = [ph.sem(f"pc{i}") for i in range(2)]
        s_out = ph.sem("out")
        norm = Norm(ph, g.x, g.h)
        block = ph.ctx.enter_context(nc.Block())

        @block.sync
        def _(sp):
            sp.dma_start(w1[:], io["mw1"][0:2 * D, :].rearrange("(a p) k -> p a k", p=D)).then_inc(s_in, 16)
            sp.dma_start(a3.q_all[B:B + 1, :, :],
                         io["mw1"][2 * D:2 * D + 1, :].unsqueeze(1).to_broadcast([1, NB, D])).then_inc(s_in, 16)
            sp.wait_ge(s_pc[0], NB)
            sp.dma_start(dr.table.rearrange("(b p) d -> p b d", p=B), src[:]).then_inc(s_out, 16)
            sp.wait_ge(s_out, 16)
            sp.wait_ge(s_in, 32)

        @block.tensor
        def _(pe):
            norm.wait(pe)
            for k, (b0, n) in enumerate(GROUPS):
                transposed(pe, ps, k, lambda b: g.h[:, b, 0:D], g.ident, range(b0, b0 + n), s_tr)
            pe.wait_ge(s_c[0], 4)
            pe.wait_ge(s_c[1], 3)
            pe.wait_ge(s_in, 32)
            pe.wait_ge(s_one, 1)
            for b in range(NB):
                if b >= 8:
                    pe.wait_ge(s_pc[0], b - 7)
                    pe.wait_ge(s_pc[1], b - 7)
                pe.matmul(ps[0:B, b % 8, 0:2 * D], a3.h_t[:, b * B:(b + 1) * B], w1[:].rearrange("p a k -> p (a k)"),
                          start=True, stop=False, skip_group_check=True)
                pe.matmul(ps[0:B, b % 8, D:2 * D], onerow[:], g.bias_rows[:, BIAS_MESSAGE:BIAS_MESSAGE + D],
                          start=False, stop=True,
                          skip_group_check=True).then_inc(s_p, 1)

        @block.scalar
        def _(a):
            norm.scalar(a)
            for k, (b0, n) in enumerate(GROUPS):
                if k % 2 == 0:
                    a.wait_ge(s_tr, k + 1)
                    a.activation(a3.h_t[:, b0 * B:(b0 + n) * B], ps[:, k, 0:n * B], ACT.Copy).then_inc(s_c[0], 1)
            for b in range(NB):
                a.wait_ge(s_p, b + 1)
                a.activation(src[:, b, :], ps[0:B, b % 8, 0:D], ACT.Copy).then_inc(s_pc[0], 1)

        @block.vector
        def _(v):
            v.memset(onerow[:], 1.0).then_inc(s_one, 1)
            norm.vector(v)
            for k, (b0, n) in enumerate(GROUPS):
                if k % 2 == 1:
                    v.wait_ge(s_tr, k + 1)
                    v.tensor_copy(a3.h_t[:, b0 * B:(b0 + n) * B], ps[:, k, 0:n * B]).then_inc(s_c[1], 1)
            for b in range(NB):
                v.wait_ge(s_pc[0], b + 1)
                v.tensor_copy(a3.q_all[0:B, b, :], ps[0:B, b % 8, D:2 * D]).then_inc(s_pc[1], 1)


def edge_phase(nc, g, dr, a3):
    S = 5
    with Phase(nc, "edge") as ph:
        idx = [ph.sb(f"idx{s}", [128, 1], I32) for s in range(S)]
        rows = [ph.sb(f"rows{s}", [128, D]) for s in range(S)]
        hot = [ph.sb(f"hot{s}", [128, B + 1]) for s in range(S)]
        hot_t = [ph.sb(f"hot_t{s}", [B + 1, 128]) for s in range(S)]
        act = [ph.sb(f"act{s}", [128, D]) for s in range(S)]
        lane_id = ph.sb("lane_id", [128, B])
        ps = ph.ps()
        s_lane = ph.sem("lane")
        s_idx = [ph.sem(f"idx{s}") for s in range(S)]
        s_rows = [ph.sem(f"rows{s}") for s in range(S)]
        s_hot = [ph.sem(f"hot{s}") for s in range(S)]
        s_tr = [ph.sem(f"tr{s}") for s in range(S)]
        s_hot_t = [ph.sem(f"hot_t{s}") for s in range(S)]
        s_pre = [ph.sem(f"pre{s}") for s in range(S)]
        s_act = [ph.sem(f"act{s}") for s in range(S)]
        s_sum = [ph.sem(f"sum{s}") for s in range(S)]
        s_out = ph.sem("out")
        s_tick = ph.sem("tick")
        block = ph.ctx.enter_context(nc.Block())
        SUMS = S

        def tiles(eng, ranges, d, body):
            lo, hi = ranges.range(0)
            body(lo, True)
            ranges.load(0, d + (128 + 1))
            with eng.Fori(lo + S, hi, S) as t:
                body(t, False)

        @block.gpsimd
        def _(pool):
            pool.iota(lane_id[:], [[1, B]], base=0, channel_multiplier=0,
                      allow_small_or_imprecise_dtypes=True).then_inc(s_lane, 1)
            rounds = Counter(pool)
            ranges = Ranges(pool, g, 1)
            ranges.load(0, 128)

            def gather(t, first):
                n = rounds.next()

                for s in range(S):
                    pool.wait_ge(s_idx[s], n)
                    pool.sem_inc(s_tick, 1)
                    pool.indirect_dma_start(rows[s][:], None, dr.table,
                                            bass.IndirectOffsetOnAxis(ap=idx[s][:], axis=0)).then_inc(s_rows[s], 16)

            with pool.Fori(0, NB) as d:
                tiles(pool, ranges, d, gather)

        @block.vector
        def _(v):
            rounds = Counter(v)
            ranges = Ranges(v, g, 1)
            ranges.load(0, 128)
            v.wait_ge(s_lane, 1)

            with v.Fori(0, NB) as d:
                def one_hot(t, first):
                    n = rounds.next()

                    def index(s):
                        v.wait_ge(s_pre[s], n)
                        v.tensor_copy(idx[s][:], g.src_idx[:, bass.ds(t + s, 1)]).then_inc(s_idx[s], 1)

                    index(0)
                    index(1)
                    for s in range(S):
                        at = bass.ds(t + s, 1)
                        v.wait_ge(s_sum[s], n)
                        v.tensor_scalar(hot[s][:, 0:B], lane_id[:], g.dst[:, at], g.block_base[:, bass.ds(d, 1)],
                                        ALU.subtract, ALU.is_equal)
                        v.tensor_copy(hot[s][:, B:B + 1], g.ea[:, at]).then_inc(s_hot[s], 1)
                        if s + 2 < S:
                            index(s + 2)

                tiles(v, ranges, d, one_hot)

        @block.tensor
        def _(pe):
            rounds = Counter(pe)
            ranges = Ranges(pe, g, 1)
            ranges.load(0, 128)
            so_far = pe.alloc_register()
            for s in range(S):
                pe.sem_inc(s_sum[s], 1)
                pe.sem_inc(s_pre[s], 1)

            with pe.Fori(0, NB) as d:
                def turned(s, n):
                    pe.wait_ge(s_hot[s], n)
                    pe.transpose(ps[0:B + 1, s, 0:128], hot[s][:], g.ident[:]).then_inc(s_tr[s], 1)

                def before_relu(s, n, landed):
                    pe.wait_ge(s_hot_t[s], n)
                    pe.wait_ge(s_rows[s], landed)
                    pe.matmul(ps[:, s, 128:256], hot_t[s][:], a3.q_all[:, bass.ds(d, 1), :].rearrange("p a k -> p (a k)"),
                              start=True, stop=False)
                    pe.matmul(ps[:, s, 128:256], g.ident[:], rows[s][:], start=False, stop=True).then_inc(s_pre[s], 1)

                def summed(s, n, start=False, stop=False):
                    pe.wait_ge(s_act[s], n)
                    pe.matmul(ps[:, SUMS, 0:B], act[s][:], hot[s][:, 0:B], start=start, stop=stop,
                              skip_group_check=True).then_inc(s_sum[s], 1)

                def messages(t, first):
                    if not first:
                        pe.reg_mov(so_far, rounds.reg)
                    n = rounds.next()
                    landed = pe.snap(n * 16)
                    turned(0, n)
                    turned(1, n)
                    if not first:
                        summed(S - 1, pe.snap(so_far))
                    for s in range(S):
                        before_relu(s, n, landed)
                        if s + 2 < S:
                            turned(s + 2, n)
                        if s == 1 and first:
                            pe.wait_ge(s_out, d + 1)
                        if s >= 1:
                            summed(s - 1, n, start=first and s == 1)

                tiles(pe, ranges, d, messages)
                summed(S - 1, pe.snap(rounds.reg), stop=True)

        @block.scalar
        def _(a):
            rounds = Counter(a)
            ranges = Ranges(a, g, 1)
            ranges.load(0, 128)
            a.sem_inc(s_out, 1)

            def sums_of(d, n):
                a.wait_ge(s_sum[S - 1], n)
                a.activation(a3.agg_t[:, bass.ds(d * B, B)], ps[:, SUMS, 0:B], ACT.Copy).then_inc(s_out, 1)

            def block_of(d, before):
                def steps(t, first):
                    n = rounds.next()

                    def turned(s):
                        a.wait_ge(s_tr[s], n)
                        a.activation(hot_t[s][:], ps[0:B + 1, s, 0:128], ACT.Copy).then_inc(s_hot_t[s], 1)

                    turned(0)
                    turned(1)
                    if first and before:
                        sums_of(d - 1, n)
                    for s in range(S):
                        a.wait_ge(s_pre[s], n + 1)
                        a.activation(act[s][:], ps[:, s, 128:256], ACT.Relu).then_inc(s_act[s], 1)
                        if s + 2 < S:
                            turned(s + 2)

                tiles(a, ranges, d, steps)

            block_of(0, False)
            with a.Fori(1, NB) as d:
                block_of(d, True)
            sums_of(NB - 1, rounds.next())
            a.wait_ge(s_out, NB + 1)


def update_phase(nc, g, io, a3, out):
    with Phase(nc, "upd") as ph:
        mw2 = ph.sb("mw2", [D, D])
        mw2_t = ph.sb("mw2_t", [D, D])
        mb2 = ph.sb("mb2", [D, 1])
        uw1 = ph.sb("uw1", [D, 2, D])
        ub1 = ph.sb("ub1", [D, 1])
        uw2 = ph.sb("uw2", [D, D])
        ub2 = ph.sb("ub2", [B, D])
        joined = ph.sb("joined", [D, D])
        bias = ph.sb("bias", [B, D])
        diag = [ph.sb(f"diag{i}", [B, 4, B]) for i in range(2)]
        u = [ph.sb(f"u{i}", [D, 4 * B]) for i in range(2)]
        ps = ph.ps()
        s_in = ph.sem("in")
        s_t = ph.sem("t")
        s_tc = ph.sem("tc")
        s_j = ph.sem("j")
        s_jc = ph.sem("jc")
        s_diag = ph.sem("diag")
        s_u = ph.sem("u")
        s_uc = ph.sem("uc")
        s_o = ph.sem("o")
        s_oc = ph.sem("oc")
        s_x = ph.sem("x")
        s_out = ph.sem("out")
        block = ph.ctx.enter_context(nc.Block())

        @block.sync
        def _(sp):
            sp.dma_start(mw2[:], io["mw2"]).then_inc(s_in, 16)
            sp.dma_start(mb2[:], io["mb2"].rearrange("(k a) -> k a", a=1)).then_inc(s_in, 16)
            sp.dma_start(uw1[:], io["uw1"].rearrange("(a p) k -> p a k", p=D)).then_inc(s_in, 16)
            sp.dma_start(ub1[:], io["ub1"].rearrange("(k a) -> k a", a=1)).then_inc(s_in, 16)
            sp.dma_start(uw2[:], io["uw2"]).then_inc(s_in, 16)
            sp.dma_start(ub2[:], io["ub2"].rearrange("(a k) -> a k", a=1).to_broadcast([B, D])).then_inc(s_in, 16)
            sp.wait_ge(s_x, 1)
            sp.dma_start(out.rearrange("(b p) d -> p b d", p=B), g.x[:]).then_inc(s_out, 16)
            sp.wait_ge(s_out, 16)

        @block.tensor
        def _(pe):
            pe.wait_ge(s_in, 96)
            pe.transpose(ps[:, 6, 0:D], mw2[:], g.ident[:]).then_inc(s_t, 1)
            pe.wait_ge(s_tc, 1)
            pe.matmul(ps[:, 6, 0:D], mw2_t[:], uw1[:, 1, :], start=True, stop=True)
            pe.matmul(ps[0:B, 7, 0:D], mb2[:].to_broadcast([D, B]), uw1[:, 1, :], start=True, stop=True).then_inc(s_j, 1)
            pe.wait_ge(s_jc, 1)
            for k, (b0, n) in enumerate(GROUPS):
                at = slice(b0 * B, (b0 + n) * B)
                p = k % 2
                if k >= 2:
                    pe.wait_ge(s_uc, k - 1)
                pe.matmul(ps[:, p, 0:n * B], uw1[:, 0, :], a3.h_t[:, at], start=True, stop=False)
                pe.matmul(ps[:, p, 0:n * B], joined[:], a3.agg_t[:, at], start=False, stop=False)
                pe.wait_ge(s_diag, k + 1)
                pe.matmul(ps[:, p, 0:n * B], bias[:], diag[p][:, 0:n, :].rearrange("p a k -> p (a k)"), start=False,
                          stop=True).then_inc(s_u, 1)
                pe.wait_ge(s_uc, k + 1)
                if k >= 2:
                    pe.wait_ge(s_oc, k - 1)
                for j in range(n):
                    last = pe.matmul(ps[0:B, 2 + p, j * D:(j + 1) * D], u[p][:, j * B:(j + 1) * B], uw2[:],
                                     start=True, stop=True)
                last.then_inc(s_o, 1)

        @block.scalar
        def _(a):
            a.wait_ge(s_in, 96)
            for k, (b0, n) in enumerate(GROUPS):
                a.wait_ge(s_u, k + 1)
                if k >= 2:
                    a.wait_ge(s_o, k - 1)
                a.activation(u[k % 2][:, 0:n * B], ps[:, k % 2, 0:n * B], ACT.Relu, bias=ub1[:]).then_inc(s_uc, 1)

        @block.vector
        def _(v):
            v.wait_ge(s_t, 1)
            v.tensor_copy(mw2_t[:], ps[:, 6, 0:D]).then_inc(s_tc, 1)
            v.wait_ge(s_j, 1)
            v.tensor_copy(joined[:], ps[:, 6, 0:D])
            v.tensor_copy(bias[:], ps[0:B, 7, 0:D]).then_inc(s_jc, 1)
            v.wait_ge(s_in, 96)
            v.tensor_tensor(g.x[:], g.x[:], g.h[:, :, 0:D], ALU.add).then_inc(s_tc, 1)
            v.wait_ge(s_tc, 2)
            v.tensor_tensor(g.x[:], g.x[:], ub2[:].unsqueeze(1).to_broadcast([B, NB, D]), ALU.add).then_inc(s_tc, 1)
            v.wait_ge(s_tc, 3)

            def diagonals(k):
                b0, n = GROUPS[k]
                if k >= 2:
                    v.wait_ge(s_u, k - 1)
                for j in range(n):
                    last = v.tensor_scalar(diag[k % 2][:, j, :], g.ident[0:B, 0:B], g.deg[:, b0 + j:b0 + j + 1], None,
                                           ALU.mult)
                last.then_inc(s_diag, 1)

            diagonals(0)
            for k, (b0, n) in enumerate(GROUPS):
                if k + 1 < len(GROUPS):
                    diagonals(k + 1)
                v.wait_ge(s_o, k + 1)
                v.tensor_tensor(g.x[:, b0:b0 + n, :], g.x[:, b0:b0 + n, :],
                                ps[0:B, 2 + k % 2, 0:n * D].rearrange("p (a k) -> p a k", k=D),
                                ALU.add).then_inc(s_oc, 1)
            v.wait_ge(s_oc, len(GROUPS))
            v.sem_inc(s_x, 1)


def gate_and_propagation(nc, g, dr, io, w):
    with ExitStack() as ctx:
        def sb(name, shape, dt=F32):
            return ctx.enter_context(nc.sbuf_tensor(name, shape, dt))

        w.m = sb("w_m", [D, 2, 3 * D])
        w.whh_t = sb("w_whh_t", [D, 3 * D])
        w.brow = sb("w_brow", [3, 3 * D])
        w.sums = sb("w_sums", [B, 2])
        w.r_src = sb("w_r_src", [B, NB])
        w.r_dst = sb("w_r_dst", [B, NB])
        w.pos = sb("w_pos", [B, NB])
        w.neg = sb("w_neg", [B, NB])
        y = sb("y", [B, NB, D])
        weights_phase(nc, g, io, w)
        spmm_t_phase(nc, g, dr, "back", g.h, y, 1, scale=w.r_src[:], aside=lambda ph: bias_rows(nc, g, io, w, ph))
        gru_phase(nc, g, w, y)
        spmm_t_phase(nc, g, dr, "hops", y, y, HOPS, alpha=w.alpha, normed=True)


def attention_and_messages(nc, g, dr, io, out):
    with ExitStack() as ctx:
        def sb(name, shape, dt=F32):
            return ctx.enter_context(nc.sbuf_tensor(name, shape, dt))

        a2 = Obj()
        a2.ks = sb("a_ks", [B, NB, HEADS * D])
        a2.qs_t = sb("a_qs_t", [D, HEADS, N])
        a2.rden = sb("a_rden", [B, NB * HEADS])
        a2.t = sb("a_t", [B, NB, HEADS * D + 1])
        a2.kv = sb("a_kv", [D, HEADS * D])
        a2.vsum = sb("a_vsum", [3, HEADS * D], BF16)
        a2.half_inv = sb("a_half_inv", [B, NB])
        a2.most = sb("a_most", [B, 1])
        a2.nparts = sb("a_nparts", [1, 1], I32)
        a2.wo = sb("a_wo", [D, HEADS * (ORDER + 1), D])
        a2.wob = sb("a_wob", [B, D])
        query_key_phase(nc, g, io, a2)
        a2.xp = sb("a_xp", [B, NB, 3, HEADS * D + 1], BF16)
        a2.y = g.n1[:, :, 0:D]
        for k in range(ORDER):
            with Phase(nc, f"panels{k}") as ph:
                panels = Panels(ph)
                term_phase(nc, g, dr, a2, k, False, panels)
                count_phase(nc, g, dr, a2, k, panels)
            combine_phase(nc, g, a2, k)
        term_phase(nc, g, dr, a2, ORDER, True, None)
    with ExitStack() as ctx:
        def sb(name, shape, dt=F32):
            return ctx.enter_context(nc.sbuf_tensor(name, shape, dt))

        a3 = Obj()
        a3.h_t = sb("m_h_t", [D, N])
        a3.agg_t = sb("m_agg_t", [D, N])
        a3.q_all = sb("m_q_all", [B + 1, NB, D])
        message_table_phase(nc, g, dr, io, a3)
        edge_phase(nc, g, dr, a3)
        update_phase(nc, g, io, a3, out)


_INS = {'x': 'x', 'src': 'src', 'dst': 'dst', 'edge_weight': 'w', 'edge_weight1': 'ea', 'L0_gnn_W1': 'W1',
        'L0_gnn_W2': 'W2', 'L0_gnn_w_ih': 'w_ih', 'L0_gnn_w_hh': 'w_hh', 'L0_gnn_b_ih': 'b_ih',
        'L0_gnn_b_hh': 'b_hh', 'L1_gnn_alpha_logits': 'alpha', 'L2_gnn_Wq_w': 'Wq_w', 'L2_gnn_Wq_b': 'Wq_b',
        'L2_gnn_Wk_w': 'Wk_w', 'L2_gnn_Wk_b': 'Wk_b', 'L2_gnn_Wo_w': 'Wo_w', 'L2_gnn_Wo_b': 'Wo_b',
        'L3_gnn_msg_w1': 'mw1', 'L3_gnn_msg_b1': 'mb1', 'L3_gnn_msg_w2': 'mw2', 'L3_gnn_msg_b2': 'mb2',
        'L3_gnn_upd_w1': 'uw1', 'L3_gnn_upd_b1': 'ub1', 'L3_gnn_upd_w2': 'uw2', 'L3_gnn_upd_b2': 'ub2'}


def kernel(**inputs):
    import numpy as np
    import concourse.bacc as bacc
    from concourse.bass_utils import run_bass_kernel_spmd
    nc = bacc.Bacc("TRN2", target_bir_lowering=False, num_devices=1)
    arrays, io = {}, {}
    for name, short in _INS.items():
        a = np.ascontiguousarray(inputs[name])
        if name == 'edge_weight1':
            a = a.reshape(-1)
        arrays[name + "_dram"] = a
        io[short] = nc.dram_tensor(name + "_dram", a.shape, mybir.dt.from_np(a.dtype), kind="ExternalInput").ap()
    out = nc.dram_tensor("out_dram", (N, D), F32, kind="ExternalOutput").ap()
    program(nc, io, out)
    r = run_bass_kernel_spmd(nc, [arrays], core_ids=[0])
    return r.results[0]["out_dram"]
```
